# Optimizing a Trainium2 kernel written in Bass

```python
import numpy as np
import jax
import jax.numpy as jnp

def _softmax(x, axis=-1):
    return jax.nn.softmax(x, axis=axis)
def _gelu(x):
    return jax.nn.gelu(x, approximate=True)
def _silu(x):
    return jax.nn.silu(x)
def _sigmoid(x):
    return jax.nn.sigmoid(x)
def _layernorm(x, axis=-1, eps=1e-5):
    m = jnp.mean(x, axis=axis, keepdims=True)
    v = jnp.var(x, axis=axis, keepdims=True)
    return (x - m) / jnp.sqrt(v + eps)
def _scatter_add(tgt, idx, src, axis=0):
    return tgt.at[idx].add(src)
def _segment_sum(src, seg, n):
    return jax.ops.segment_sum(src, seg, n)

kernel_name = 'mk_dlrm_tower_d1_rec_0dbbd4'

def setup_inputs(seed: int = 0):
    np.random.seed(seed)
    _w = jnp.asarray
    def _rec_inputs():
        import jax
        import jax.numpy as jnp
        _tk = jax.random.key(seed)
        ids = jnp.stack([jax.random.randint(jax.random.fold_in(_tk, 200 + f), (1024,), 0, v, jnp.int32) for f, v in enumerate([10000, 1000, 1000000, 1000])], axis=1)
        tbl_0 = 0.05 * jax.random.normal(jax.random.fold_in(_tk, 500 + 0), (10000, 4), jnp.float32)
        tbl_1 = 0.05 * jax.random.normal(jax.random.fold_in(_tk, 500 + 1), (1000, 4), jnp.float32)
        tbl_2 = 0.05 * jax.random.normal(jax.random.fold_in(_tk, 500 + 2), (1000000, 4), jnp.float32)
        tbl_3 = 0.05 * jax.random.normal(jax.random.fold_in(_tk, 500 + 3), (1000, 4), jnp.float32)
        _rk = jax.random.fold_in(_tk, 7)
        r_x = 7.22013e-05 + 1.00017 * jax.random.normal(jax.random.fold_in(_rk, 101), (1024, 2048), jnp.float32)
        W_top1 = 0.0197642 * jax.random.normal(jax.random.fold_in(_tk, 801), (2560, 512), jnp.float32)
        W_top2 = 0.0441942 * jax.random.normal(jax.random.fold_in(_tk, 802), (512, 256), jnp.float32)
        W_top3 = 0.0625 * jax.random.normal(jax.random.fold_in(_tk, 803), (256, 1), jnp.float32)
        b_top1 = jnp.zeros((512,), jnp.float32)
        b_top2 = jnp.zeros((256,), jnp.float32)
        return r_x, ids, tbl_0, tbl_1, tbl_2, tbl_3, W_top1, b_top1, W_top2, b_top2, W_top3
    r_x, ids, tbl_0, tbl_1, tbl_2, tbl_3, W_top1, b_top1, W_top2, b_top2, W_top3 = _rec_inputs()
    def _L0_rec_setup():
        import jax, jax.numpy as jnp
        import numpy as np
        B, IN, HID, D, N, OUT = (4096, 2048, 2048, 512, 4, 512)
        H = 8
        HD = D // H

        def _ln(x, g, b):
            m = x.mean(-1, keepdims=True)
            v = ((x - m) ** 2).mean(-1, keepdims=True)
            return (x - m) / jnp.sqrt(v + 1e-05) * g + b
        key = jax.random.key(seed)
        ks = jax.random.split(key, 32)

        def nrm(k, shape, scale=0.02):
            return jax.random.normal(k, shape, jnp.float32) * scale
        inp = {}
        inp['x'] = jax.random.normal(ks[0], (B, IN), jnp.float32)
        inp['strength'] = jax.random.uniform(ks[1], (B, N, N), jnp.float32)
        for t, i in (('er', 2), ('ei', 4)):
            inp[t + '_W1'] = nrm(ks[i], (HID, IN))
            inp[t + '_b1'] = jnp.zeros((HID,), jnp.float32)
            inp[t + '_g1'] = jnp.ones((HID,), jnp.float32)
            inp[t + '_be1'] = jnp.zeros((HID,), jnp.float32)
            inp[t + '_W2'] = nrm(ks[i + 1], (N * D, HID))
            inp[t + '_b2'] = jnp.zeros((N * D,), jnp.float32)
        names = ['Wq_r', 'Wq_i', 'Wk_r', 'Wk_i', 'Wv_r', 'Wv_i', 'Wo_r', 'Wo_i']
        for j, nm in enumerate(names):
            inp[nm] = nrm(ks[6 + j], (D, D))
            inp['b' + nm[1:]] = jnp.zeros((D,), jnp.float32)
        inp['int_Wr'] = jnp.tile(jnp.eye(D, dtype=jnp.float32)[None], (N, 1, 1))
        inp['int_Wi'] = jnp.zeros((N, D, D), jnp.float32)
        inp['meas_Mr'] = nrm(ks[20], (OUT, D), 1.0 / np.sqrt(D))
        inp['meas_Mi'] = nrm(ks[21], (OUT, D), 1.0 / np.sqrt(D))
        inp['post_W'] = nrm(ks[22], (OUT, OUT))
        inp['post_b'] = jnp.zeros((OUT,), jnp.float32)
        inp['post_g'] = jnp.ones((OUT,), jnp.float32)
        inp['post_be'] = jnp.zeros((OUT,), jnp.float32)
        return inp
    _L0_rec_all = _L0_rec_setup()
    _L0_rec_in = {k: v for k, v in _L0_rec_all.items() if k in ('er_W1', 'er_b1', 'er_g1', 'er_be1', 'er_W2', 'er_b2', 'ei_W1', 'ei_b1', 'ei_g1', 'ei_be1', 'ei_W2', 'ei_b2', 'Wq_r', 'bq_r', 'Wq_i', 'bq_i', 'Wk_r', 'bk_r', 'Wk_i', 'bk_i', 'Wv_r', 'bv_r', 'Wv_i', 'bv_i', 'Wo_r', 'bo_r', 'Wo_i', 'bo_i', 'int_Wr', 'int_Wi', 'meas_Mr', 'meas_Mi', 'post_W', 'post_b', 'post_g', 'post_be', )}
    del _L0_rec_all

    return {
        "r_x": r_x,
        "ids": ids,
        "tbl_0": tbl_0,
        "tbl_1": tbl_1,
        "tbl_2": tbl_2,
        "tbl_3": tbl_3,
        "W_top1": W_top1,
        "b_top1": b_top1,
        "W_top2": W_top2,
        "b_top2": b_top2,
        "W_top3": W_top3,
        "L0_rec_er_W1": _L0_rec_in["er_W1"],
        "L0_rec_er_b1": _L0_rec_in["er_b1"],
        "L0_rec_er_g1": _L0_rec_in["er_g1"],
        "L0_rec_er_be1": _L0_rec_in["er_be1"],
        "L0_rec_er_W2": _L0_rec_in["er_W2"],
        "L0_rec_er_b2": _L0_rec_in["er_b2"],
        "L0_rec_ei_W1": _L0_rec_in["ei_W1"],
        "L0_rec_ei_b1": _L0_rec_in["ei_b1"],
        "L0_rec_ei_g1": _L0_rec_in["ei_g1"],
        "L0_rec_ei_be1": _L0_rec_in["ei_be1"],
        "L0_rec_ei_W2": _L0_rec_in["ei_W2"],
        "L0_rec_ei_b2": _L0_rec_in["ei_b2"],
        "L0_rec_Wq_r": _L0_rec_in["Wq_r"],
        "L0_rec_bq_r": _L0_rec_in["bq_r"],
        "L0_rec_Wq_i": _L0_rec_in["Wq_i"],
        "L0_rec_bq_i": _L0_rec_in["bq_i"],
        "L0_rec_Wk_r": _L0_rec_in["Wk_r"],
        "L0_rec_bk_r": _L0_rec_in["bk_r"],
        "L0_rec_Wk_i": _L0_rec_in["Wk_i"],
        "L0_rec_bk_i": _L0_rec_in["bk_i"],
        "L0_rec_Wv_r": _L0_rec_in["Wv_r"],
        "L0_rec_bv_r": _L0_rec_in["bv_r"],
        "L0_rec_Wv_i": _L0_rec_in["Wv_i"],
        "L0_rec_bv_i": _L0_rec_in["bv_i"],
        "L0_rec_Wo_r": _L0_rec_in["Wo_r"],
        "L0_rec_bo_r": _L0_rec_in["bo_r"],
        "L0_rec_Wo_i": _L0_rec_in["Wo_i"],
        "L0_rec_bo_i": _L0_rec_in["bo_i"],
        "L0_rec_int_Wr": _L0_rec_in["int_Wr"],
        "L0_rec_int_Wi": _L0_rec_in["int_Wi"],
        "L0_rec_meas_Mr": _L0_rec_in["meas_Mr"],
        "L0_rec_meas_Mi": _L0_rec_in["meas_Mi"],
        "L0_rec_post_W": _L0_rec_in["post_W"],
        "L0_rec_post_b": _L0_rec_in["post_b"],
        "L0_rec_post_g": _L0_rec_in["post_g"],
        "L0_rec_post_be": _L0_rec_in["post_be"],
    }

def reference(r_x, ids, tbl_0, tbl_1, tbl_2, tbl_3, W_top1, b_top1, W_top2, b_top2, W_top3, L0_rec_er_W1, L0_rec_er_b1, L0_rec_er_g1, L0_rec_er_be1, L0_rec_er_W2, L0_rec_er_b2, L0_rec_ei_W1, L0_rec_ei_b1, L0_rec_ei_g1, L0_rec_ei_be1, L0_rec_ei_W2, L0_rec_ei_b2, L0_rec_Wq_r, L0_rec_bq_r, L0_rec_Wq_i, L0_rec_bq_i, L0_rec_Wk_r, L0_rec_bk_r, L0_rec_Wk_i, L0_rec_bk_i, L0_rec_Wv_r, L0_rec_bv_r, L0_rec_Wv_i, L0_rec_bv_i, L0_rec_Wo_r, L0_rec_bo_r, L0_rec_Wo_i, L0_rec_bo_i, L0_rec_int_Wr, L0_rec_int_Wi, L0_rec_meas_Mr, L0_rec_meas_Mi, L0_rec_post_W, L0_rec_post_b, L0_rec_post_g, L0_rec_post_be):
    import jax
    import jax.numpy as jnp
    def _L0_rec_ref(x, strength, er_W1, er_b1, er_g1, er_be1, er_W2, er_b2, ei_W1, ei_b1, ei_g1, ei_be1, ei_W2, ei_b2, Wq_r, bq_r, Wq_i, bq_i, Wk_r, bk_r, Wk_i, bk_i, Wv_r, bv_r, Wv_i, bv_i, Wo_r, bo_r, Wo_i, bo_i, int_Wr, int_Wi, meas_Mr, meas_Mi, post_W, post_b, post_g, post_be):
        import jax, jax.numpy as jnp
        import numpy as np
        B, IN, HID, D, N, OUT = (4096, 2048, 2048, 512, 4, 512)
        H = 8
        HD = D // H

        def _ln(x, g, b):
            m = x.mean(-1, keepdims=True)
            v = ((x - m) ** 2).mean(-1, keepdims=True)
            return (x - m) / jnp.sqrt(v + 1e-05) * g + b
        Bsz = x.shape[0]

        def enc(W1, b1, g, be, W2, b2):
            h = jax.nn.gelu(_ln(x @ W1.T + b1, g, be), approximate=False)
            return (h @ W2.T + b2).reshape(Bsz, N, D)
        sr = enc(er_W1, er_b1, er_g1, er_be1, er_W2, er_b2)
        si = enc(ei_W1, ei_b1, ei_g1, ei_be1, ei_W2, ei_b2)

        def heads(t):
            return t.reshape(Bsz, N, H, HD).transpose(0, 2, 1, 3)
        qr = heads(sr @ Wq_r.T + bq_r)
        qi = heads(si @ Wq_i.T + bq_i)
        kr = heads(sr @ Wk_r.T + bk_r)
        ki = heads(si @ Wk_i.T + bk_i)
        vr = heads(sr @ Wv_r.T + bv_r)
        vi = heads(si @ Wv_i.T + bv_i)
        ar = jnp.einsum('bhnd,bhmd->bhnm', qr, kr) + jnp.einsum('bhnd,bhmd->bhnm', qi, ki)
        ai = jnp.einsum('bhnd,bhmd->bhnm', qi, kr) - jnp.einsum('bhnd,bhmd->bhnm', qr, ki)
        mag = jnp.sqrt(ar ** 2 + ai ** 2 + 1e-08) * HD ** (-0.5)
        w = jax.nn.softmax(mag, axis=-1)
        out_r = jnp.einsum('bhnm,bhmd->bhnd', w, vr).transpose(0, 2, 1, 3).reshape(Bsz, N, D)
        out_i = jnp.einsum('bhnm,bhmd->bhnd', w, vi).transpose(0, 2, 1, 3).reshape(Bsz, N, D)
        attn_r = out_r @ Wo_r.T + bo_r
        attn_i = out_i @ Wo_i.T + bo_i
        R = jnp.einsum('bnd,ned->bne', attn_r, int_Wr) - jnp.einsum('bnd,ned->bne', attn_i, int_Wi)
        I = jnp.einsum('bnd,ned->bne', attn_r, int_Wi) + jnp.einsum('bnd,ned->bne', attn_i, int_Wr)
        Ri, Ii = (R[:, :, None, :], I[:, :, None, :])
        Rj, Ij = (R[:, None, :, :], I[:, None, :, :])
        phase = jnp.arctan2(Ii * Rj - Ri * Ij, Ri * Rj + Ii * Ij)
        f = jnp.cos(phase) * strength[..., None]
        sup_r = jnp.einsum('bijd,bjd->bd', f, R)
        sup_i = jnp.einsum('bijd,bjd->bd', f, I)
        norm = jnp.sqrt(jnp.sum(sup_r ** 2 + sup_i ** 2, axis=-1, keepdims=True) + 1e-08)
        sup_r = sup_r / norm
        sup_i = sup_i / norm
        mr = sup_r @ meas_Mr.T - sup_i @ meas_Mi.T
        mi = sup_r @ meas_Mi.T + sup_i @ meas_Mr.T
        amp = jnp.sqrt(mr ** 2 + mi ** 2)
        out = jax.nn.gelu(_ln(amp @ post_W.T + post_b, post_g, post_be), approximate=False)
        return out

    e = jnp.stack([tbl_0[ids[:, 0]], tbl_1[ids[:, 1]], tbl_2[ids[:, 2]], tbl_3[ids[:, 3]]], axis=1)
    z = _L0_rec_ref(r_x, e, L0_rec_er_W1, L0_rec_er_b1, L0_rec_er_g1, L0_rec_er_be1, L0_rec_er_W2, L0_rec_er_b2, L0_rec_ei_W1, L0_rec_ei_b1, L0_rec_ei_g1, L0_rec_ei_be1, L0_rec_ei_W2, L0_rec_ei_b2, L0_rec_Wq_r, L0_rec_bq_r, L0_rec_Wq_i, L0_rec_bq_i, L0_rec_Wk_r, L0_rec_bk_r, L0_rec_Wk_i, L0_rec_bk_i, L0_rec_Wv_r, L0_rec_bv_r, L0_rec_Wv_i, L0_rec_bv_i, L0_rec_Wo_r, L0_rec_bo_r, L0_rec_Wo_i, L0_rec_bo_i, L0_rec_int_Wr, L0_rec_int_Wi, L0_rec_meas_Mr, L0_rec_meas_Mi, L0_rec_post_W, L0_rec_post_b, L0_rec_post_g, L0_rec_post_be)
    z = z.reshape(z.shape[0], -1)
    h = jnp.concatenate([z, r_x], axis=1)
    h = jnp.maximum(h @ W_top1 + b_top1, 0.0)
    h = jnp.maximum(h @ W_top2 + b_top2, 0.0)
    y = h @ W_top3
    return y


_drawn_inputs = setup_inputs


def setup_inputs(seed=0):
    import zlib

    import numpy as np

    out = dict(_drawn_inputs(seed))
    spreads = {'b_top1': (0.0, 0.1),
     'b_top2': (0.0, 0.1),
     'L0_rec_er_b1': (0.0, 0.8),
     'L0_rec_er_g1': (1.0, 0.6),
     'L0_rec_er_be1': (0.0, 0.8),
     'L0_rec_er_b2': (0.0, 0.8),
     'L0_rec_ei_b1': (0.0, 0.8),
     'L0_rec_ei_g1': (1.0, 0.6),
     'L0_rec_ei_be1': (0.0, 0.8),
     'L0_rec_ei_b2': (0.0, 0.8),
     'L0_rec_bq_r': (0.0, 0.8),
     'L0_rec_bq_i': (0.0, 0.8),
     'L0_rec_bk_r': (0.0, 0.8),
     'L0_rec_bk_i': (0.0, 0.8),
     'L0_rec_bv_r': (0.0, 0.1),
     'L0_rec_bv_i': (0.0, 0.1),
     'L0_rec_bo_r': (0.0, 0.1),
     'L0_rec_bo_i': (0.0, 0.1),
     'L0_rec_int_Wi': (0.0, 0.1),
     'L0_rec_post_b': (0.0, 0.1),
     'L0_rec_post_g': (1.0, 0.2),
     'L0_rec_post_be': (0.0, 0.1)}
    factors = {'L0_rec_Wq_r': 8.0, 'L0_rec_Wq_i': 8.0, 'L0_rec_Wk_r': 8.0, 'L0_rec_Wk_i': 8.0}
    for name, (base, spread) in spreads.items():
        noise = np.random.default_rng([zlib.crc32(name.encode()), seed]).standard_normal(out[name].shape)
        drawn = base * np.exp(spread * noise) if base else spread * noise
        out[name] = jnp.asarray(drawn.astype(out[name].dtype))
    for name, factor in factors.items():
        out[name] = (out[name] * factor).astype(out[name].dtype)
    return out
```

```python
from contextlib import ExitStack

import numpy as np

import concourse.bass as bass
from concourse import mybir

F32 = mybir.dt.float32
R32 = mybir.dt.float32r
I32 = mybir.dt.int32
ACT = mybir.ActivationFunctionType
ALU = mybir.AluOpType
AX = mybir.AxisListType

P = 128
TOK = 1024
IN = 2048
N = 4
D = 512
H = 8
HD = D // H
HALF = 512
HALVES = TOK // HALF
KT = IN // P
DT = D // P
CH = TOK // P
EPS = 1e-5
RING = 4


class Mem:

    def __init__(self, nc, ctx, phase):
        self.nc, self.ctx, self.phase = nc, ctx, phase

    def sb(self, name, shape, dt=F32):
        return self.ctx.enter_context(self.nc.sbuf_tensor(f"{self.phase}_{name}", shape, dt))

    def bank(self, name):
        return self.ctx.enter_context(self.nc.psum_tensor(f"{self.phase}_{name}", [P, 512], F32))

    def sem(self, name):
        return self.ctx.enter_context(self.nc.semaphore(f"{self.phase}_{name}"))


def product(nc, out, a, b, first, last):
    (ah, al), (bh, bl) = a, b
    nc.tensor.matmul(out, ah, bh, start=first, stop=False)
    nc.tensor.matmul(out, ah, bl, start=False, stop=False)
    return nc.tensor.matmul(out, al, bh, start=False, stop=last)


def encoders(nc, xT, w_enc, b1, g1T, be1T, b2T, s_out):
    with ExitStack() as ctx:
        m = Mem(nc, ctx, "enc")
        x_hi = m.sb("x_hi", [P, KT, HALF], R32)
        x_lo = m.sb("x_lo", [P, KT, HALF], R32)
        hid = m.sb("hid", [P, 4, IN])
        act_hi = m.sb("act_hi", [P, KT, HALF], R32)
        act_lo = m.sb("act_lo", [P, KT, HALF], R32)
        act_f = m.sb("act_f", [P, 2, HALF])
        w_raw = m.sb("w_raw", [P, 2, 2, 512])
        w_hi = m.sb("w_hi", [P, RING, 512], R32)
        w_lo = m.sb("w_lo", [P, RING, 512], R32)
        b1_row = m.sb("b1_row", [P, 2, 512])
        s_stage = m.sb("s_stage", [P, 2, HALF])
        ident = m.sb("ident", [P, P])
        stats = m.sb("stats", [P, 4, 4 * 6])
        mean_var = m.sb("mean_var", [P, 4, 2])
        std = m.sb("std", [P, 4])
        rstd = m.sb("rstd", [P, 4])
        gain = m.sb("gain", [P, KT])
        shift = m.sb("shift", [P, KT])
        b2 = m.sb("b2", [P, KT])
        banks = [[m.bank(f"acc{s}{t}") for t in range(4)] for s in range(2)]

        x_landed = [m.sem(f"x_landed{i}") for i in range(4)]
        w_landed = [m.sem(f"w_landed{i}") for i in range(2)]
        b1_landed = [m.sem(f"b1_landed{i}") for i in range(2)]
        c_landed = m.sem("c_landed")
        x_hi_done, x_lo_done = m.sem("x_hi_done"), m.sem("x_lo_done")
        w_hi_done, w_lo_done, w_used = m.sem("w_hi_done"), m.sem("w_lo_done"), m.sem("w_used")
        hid_done, s_done, s_stored = m.sem("hid_done"), m.sem("s_done"), [m.sem(f"s_stored{i}") for i in range(2)]
        ident_ready, var_done, std_done, rstd_done = m.sem("ident_ready"), m.sem("var_done"), m.sem("std_done"), m.sem("rstd_done")
        stat_done, z_done, zt_done, gelu_done = m.sem("stat_done"), m.sem("z_done"), m.sem("zt_done"), m.sem("gelu_done")
        act_hi_done, act_lo_done = m.sem("act_hi_done"), m.sem("act_lo_done")
        block = ctx.enter_context(nc.Block())

        ITEMS = 2 * 4 * KT
        LO0, HID0, S0 = 4, 8, 16

        @block.sync
        def _(sp):
            def load_x(half):
                for r in range(4):
                    sp.dma_start(hid[:, r, :].rearrange("p (k t) -> p k t", k=4),
                                 xT[bass.ds(half * KT + 4 * r, 4)].rearrange("k p t -> p k t")).then_inc(x_landed[r], 16)

            load_x(0)
            with sp.Fori(0, HALVES) as half:
                with sp.Fori(0, 2) as e:
                    it = half * 2 + e
                    with sp.Fori(0, 2) as c2:
                        for cc in range(2):
                            sp.wait_ge(hid_done, it * 16 + c2 * 8 + (4 * cc + 4))
                            sp.dma_start(b1_row[:, cc, :], b1[bass.ds(e * 4 + c2 * 2 + cc, 1)].rearrange("a j -> (a j)").partition_broadcast(P)).then_inc(b1_landed[cc], 16)
                            for q in range(8):
                                sp.wait_ge(w_lo_done, it * ITEMS + c2 * 32 + (16 * cc + 2 * q + 2))
                                sp.dma_start(w_raw[:, q % 2, :, :], w_enc[bass.ds(e * 64 + c2 * 16 + (8 * cc + q), 1)].rearrange("a p k j -> p (a k) j")).then_inc(w_landed[q % 2], 16)
                    for first, pairs in ((0, 5), (5, 11)):
                        with sp.Fori(first, first + pairs) as q2:
                            for qq in range(2):
                                sp.wait_ge(w_lo_done, it * ITEMS + q2 * 4 + (64 + 2 * qq + 2))
                                sp.dma_start(w_raw[:, qq, :, :], w_enc[bass.ds(e * 64 + q2 * 2 + (32 + qq), 1)].rearrange("a p k j -> p (a k) j")).then_inc(w_landed[qq], 16)
                        if not first:
                            sp.wait_ge(zt_done, it * KT + KT)
                            load_x((half + e) % 2)
            for r in range(4):
                sp.wait_ge(x_landed[r], 5 * 16)

        @block.gpsimd
        def _(pool):
            nc.gpsimd.memset(ident[:], 0.0).then_inc(ident_ready, 1)
            pool.wait_ge(ident_ready, 1)
            nc.gpsimd.affine_select(out=ident[:], in_=ident[:], compare_op=ALU.not_equal, fill=1.0, base=0,
                                    pattern=[[-1, P]], channel_multiplier=1).then_inc(ident_ready, 1)
            def high_x(rounds):
                for k in range(KT):
                    if k % 4 == 0:
                        pool.wait_ge(x_landed[k // 4], rounds * 16 + 16)
                        pool.nop(nofuse=True)
                    nc.gpsimd.tensor_copy(x_hi[:, k, :], hid[:, k // 4, 512 * (k % 4):512 * (k % 4) + 512]).then_inc(x_hi_done, 1)

            high_x(0)
            with pool.Fori(0, HALVES) as half:
                with pool.Fori(0, 2) as e:
                    it = half * 2 + e
                    for k in range(KT):
                        pool.wait_ge(gelu_done, it * KT + (k + 1))
                        pool.nop(nofuse=True)
                        nc.gpsimd.tensor_copy(act_hi[:, k, :], act_f[:, k % 2, :]).then_inc(act_hi_done, 1)
                    high_x(it + 1)

        @block.scalar
        def _(act):
            def high(base, i):
                act.wait_ge(w_used, base + (i + 1))
                if i % 2 == 0:
                    act.wait_ge(w_landed[i // 2 % 2], base * 4 + (i // 4 + 1) * 16)
                nc.scalar.activation(w_hi[:, i % RING, :], w_raw[:, i // 2 % 2, i % 2, :], ACT.Copy).then_inc(w_hi_done, 1)

            act.sem_inc(s_done, S0)
            for i in range(2):
                act.sem_inc(s_stored[i], 16)
            act.dma_start(gain[:], g1T[0]).then_inc(c_landed, 16)
            act.dma_start(shift[:], be1T[0]).then_inc(c_landed, 16)
            act.dma_start(b2[:], b2T[0]).then_inc(c_landed, 16)
            with act.Fori(0, HALVES) as half:
                with act.Fori(0, 2) as e:
                    it = half * 2 + e
                    base = act.snap(it * ITEMS)
                    for i in range(RING):
                        high(base, i)
                    with act.Fori(0, 4) as c:
                        gbase = act.snap(base + c * 16)
                        for j in range(RING, 16 + RING):
                            high(gbase, j)
                    act.wait_ge(var_done, it + 1)
                    nc.scalar.activation(std[:], mean_var[:, :, 1], ACT.Sqrt).then_inc(std_done, 1)
                    act.wait_ge(c_landed, it * 48 + 48)
                    for k in range(KT + 2):
                        if k < KT:
                            act.wait_ge(zt_done, it * KT + (k + 1))
                            if k >= 2:
                                act.wait_ge(act_lo_done, it * KT + (k - 1))
                            nc.scalar.activation(act_f[:, k % 2, :], banks[1][k % 4][:], ACT.Gelu,
                                                 bias=shift[:, k:k + 1], scale=gain[:, k:k + 1]).then_inc(gelu_done, 1)
                        if k >= 2:
                            high(base, 64 + RING + k - 2)
                    for n in range(4):
                        if n:
                            for j in range(RING, 16 + RING):
                                if 16 * n + j < 64:
                                    high(base, 64 + 16 * n + j)
                        for f in range(4):
                            r = 4 * n + f
                            act.wait_ge(w_used, base + (64 + 16 * n + 16 + RING))
                            act.wait_ge(s_stored[f % 2], it * (8 * 16) + (r // 2 + 1) * 16)
                            nc.scalar.activation(s_stage[:, f % 2, :], banks[n % 2][f][:], ACT.Identity,
                                                 bias=b2[:, r:r + 1]).then_inc(s_done, 1)
                            act.wait_ge(s_done, it * 16 + (r + 1 + S0))
                            act.dma_start(s_out[bass.ds(half * 4, 4), bass.ds(e, 1), :, f, n, :].rearrange("c e p t -> p (c e) t"),
                                          s_stage[:, f % 2, :].rearrange("p (c t) -> p c t", c=4)).then_inc(s_stored[f % 2], 16)
                    act.wait_ge(s_done, it * 16 + (16 + S0))
                    act.dma_start(gain[:], g1T[bass.ds(1 - e, 1)].rearrange("a p k -> p (a k)")).then_inc(c_landed, 16)
                    act.dma_start(shift[:], be1T[bass.ds(1 - e, 1)].rearrange("a p k -> p (a k)")).then_inc(c_landed, 16)
                    act.dma_start(b2[:], b2T[bass.ds(1 - e, 1)].rearrange("a p k -> p (a k)")).then_inc(c_landed, 16)
            act.wait_ge(c_landed, 5 * 48)
            for i in range(2):
                act.wait_ge(s_stored[i], 4 * 8 * 16 + 16)

        @block.vector
        def _(dve):
            def low(base, i):
                dve.wait_ge(w_hi_done, base + (i + 1))
                nc.vector.tensor_tensor(w_lo[:, i % RING, :], w_raw[:, i // 2 % 2, i % 2, :],
                                        w_hi[:, i % RING, :].bitcast(F32), ALU.subtract).then_inc(w_lo_done, 1)

            dve.sem_inc(w_lo_done, LO0)
            dve.sem_inc(hid_done, HID0)
            def low_x(rounds, k):
                dve.wait_ge(x_hi_done, rounds * KT + (k + 1))
                nc.vector.tensor_tensor(x_lo[:, k, :], hid[:, k // 4, 512 * (k % 4):512 * (k % 4) + 512],
                                        x_hi[:, k, :].bitcast(F32), ALU.subtract).then_inc(x_lo_done, 1)

            for k in range(KT):
                low_x(0, k)
            with dve.Fori(0, HALVES) as half:
                with dve.Fori(0, 2) as e:
                    it = half * 2 + e
                    base = dve.snap(it * ITEMS)
                    for i in range(RING):
                        low(base, i)
                    with dve.Fori(0, 2) as c2:
                        for cc in range(2):
                            gbase = dve.snap(base + c2 * 32 + 16 * cc)
                            for j in range(RING, 16 + RING):
                                low(gbase, j)
                            dve.wait_ge(b1_landed[cc], it * 32 + c2 * 16 + 16)
                            dve.wait_ge(w_used, gbase + (16 + RING))
                            for t in range(4):
                                nc.vector.tensor_tensor(hid[:, t, bass.ds(c2 * 1024 + 512 * cc, 512)], banks[cc][t][:],
                                                        b1_row[:, cc, :], ALU.add).then_inc(hid_done, 1)
                            for t in range(4):
                                dve.wait_ge(hid_done, it * 16 + c2 * 8 + (4 * cc + t + 1 + HID0))
                                nc.vector.bn_stats(stats[:, t, bass.ds(c2 * 12 + 6 * cc, 6)],
                                                   hid[:, t, bass.ds(c2 * 1024 + 512 * cc, 512)]).then_inc(stat_done, 1)
                    dve.wait_ge(stat_done, it * 20 + 16)
                    dve.nop(nofuse=True)
                    for t in range(4):
                        nc.vector.bn_aggr(mean_var[:, t, :], stats[:, t, :]).then_inc(stat_done, 1)
                    dve.wait_ge(stat_done, it * 20 + 20)
                    nc.vector.tensor_scalar(mean_var[:, :, 1], mean_var[:, :, 1], EPS, None, ALU.add).then_inc(var_done, 1)
                    dve.wait_ge(std_done, it + 1)
                    nc.vector.reciprocal(rstd[:], std[:]).then_inc(rstd_done, 1)
                    dve.wait_ge(rstd_done, it + 1)

                    def normalise(c):
                        for t in range(4):
                            nc.vector.tensor_scalar(hid[:, t, 512 * c:512 * c + 512], hid[:, t, 512 * c:512 * c + 512],
                                                    mean_var[:, t, 0:1], rstd[:, t:t + 1], ALU.subtract,
                                                    ALU.mult).then_inc(z_done, 1)
                    normalise(0)
                    normalise(1)
                    for k in range(KT + 2):
                        if k < KT:
                            dve.wait_ge(act_hi_done, it * KT + (k + 1))
                            nc.vector.tensor_tensor(act_lo[:, k, :], act_f[:, k % 2, :], act_hi[:, k, :].bitcast(F32),
                                                    ALU.subtract).then_inc(act_lo_done, 1)
                        if k in (1, 5):
                            normalise(2 + k // 4)
                        if k >= 2:
                            low(base, 64 + RING + k - 2)
                    for n in range(1, 4):
                        for j in range(RING, 16 + RING):
                            if 16 * n + j < 64:
                                low(base, 64 + 16 * n + j)
                            if n == 2:
                                low_x(it + 1, j - RING)

        @block.tensor
        def _(pe):
            pe.sem_inc(w_used, RING)
            pe.wait_ge(ident_ready, 2)
            with pe.Fori(0, HALVES) as half:
                with pe.Fori(0, 2) as e:
                    it = half * 2 + e
                    base = pe.snap(it * ITEMS)
                    with pe.Fori(0, 2) as c2:
                        for cc in range(2):
                            pe.wait_ge(hid_done, it * 16 + c2 * 8 + (4 * cc + 4))
                            pe.wait_ge(s_done, it * 16 + (12 + 4 * cc))
                            for k in range(KT):
                                pe.wait_ge(x_lo_done, it * KT + (k + 1))
                                pe.wait_ge(w_lo_done, base + c2 * 32 + (16 * cc + k + 1 + LO0))
                                w = (w_hi[:, k % RING, :], w_lo[:, k % RING, :])
                                for t in range(4):
                                    s = slice(P * t, P * t + P)
                                    mm = product(nc, banks[cc][t][:], (x_hi[:, k, s], x_lo[:, k, s]), w, k == 0, k == KT - 1)
                                mm.then_inc(w_used, 1)

                    def turn(k):
                        pe.wait_ge(z_done, it * 16 + (k // 4 * 4 + 4))
                        if k >= 4:
                            pe.wait_ge(gelu_done, it * KT + (k - 3))
                        for t in range(4):
                            mm = nc.tensor.transpose(banks[1][k % 4][:, P * t:P * t + P], hid[:, t, P * k:P * k + P], ident[:])
                        mm.then_inc(zt_done, 1)

                    for n in range(4):
                        if n == 0:
                            for k in range(3):
                                turn(k)
                            pe.wait_ge(hid_done, it * 16 + (12 + HID0))
                        elif n == 1:
                            pe.wait_ge(gelu_done, it * KT + KT)
                        else:
                            pe.wait_ge(s_done, it * 16 + (4 * n - 4 + S0))
                        for k in range(KT):
                            pe.wait_ge(w_lo_done, base + (64 + 16 * n + k + 1 + LO0))
                            if n == 0:
                                pe.wait_ge(act_lo_done, it * KT + (k + 1))
                            a = (act_hi[:, k, :], act_lo[:, k, :])
                            for f in range(4):
                                s = slice(P * f, P * f + P)
                                mm = product(nc, banks[n % 2][f][:], (w_hi[:, k % RING, s], w_lo[:, k % RING, s]), a,
                                             k == 0, k == KT - 1)
                            mm.then_inc(w_used, 1)
                            if n == 0 and k + 3 < KT:
                                turn(k + 3)


def projections(nc, s_in, w_qkv, b_qkvT, b_v, qkv_out):
    with ExitStack() as ctx:
        m = Mem(nc, ctx, "proj")
        MATS = 6
        w_hi = m.sb("w_hi", [P, MATS, DT, 512], R32)
        w_lo = m.sb("w_lo", [P, MATS, DT, 512], R32)
        s_raw = m.sb("s_raw", [P, 2, DT, 512])
        s_hi = m.sb("s_hi", [P, 2, 2, DT, 512], R32)
        s_lo = m.sb("s_lo", [P, 2, 2, DT, 512], R32)
        stage_a = m.sb("stage_a", [P, DT, 512])
        stage_d = m.sb("stage_d", [P, DT, 512])
        b_col = m.sb("b_col", [P, 4, DT])
        bv_row = m.sb("bv_row", [P, 2, 512])
        banks = [[m.bank(f"acc{s}{t}") for t in range(4)] for s in range(2)]

        b_landed = m.sem("b_landed")
        w_landed = [m.sem(f"w_landed{i}") for i in range(2)]
        s_landed = [m.sem(f"s_landed{i}") for i in range(2)]
        w_hi_done, w_lo_done = m.sem("w_hi_done"), m.sem("w_lo_done")
        s_hi_done, s_lo_done = m.sem("s_hi_done"), m.sem("s_lo_done")
        mm_done, act_out, dve_out, neg_out = m.sem("mm_done"), m.sem("act_out"), m.sem("dve_out"), m.sem("neg_out")
        act_stored, dve_stored = m.sem("act_stored"), m.sem("dve_stored")
        block = ctx.enter_context(nc.Block())

        def by_group(x):
            return x.rearrange("p (n g t) -> p g n t", n=N, g=4)

        def grouped(x, buf, comp, k):
            return x[:, buf, comp, k, :].rearrange("p (g n t) -> p g n t", n=N, g=4)

        AO, DO, SL, ST, MM = 8, 16, 2, 16, 6

        @block.sync
        def _(sp):
            sp.dma_start(b_col[:], b_qkvT).then_inc(b_landed, 16)
            sp.dma_start(bv_row[:], b_v.partition_broadcast(P)).then_inc(b_landed, 16)

            def load_s(c):
                for comp in range(2):
                    sp.wait_ge(s_lo_done, c * 2 + (comp + 1))
                    sp.dma_start(s_raw[:, comp, :, :].rearrange("p k (n t) -> p k n t", n=N),
                                 s_in[bass.ds(c % CH, 1), comp].rearrange("a p k n t -> p (a k) n t")).then_inc(s_landed[comp], 16)

            for mat in range(MATS):
                if mat >= 2:
                    sp.wait_ge(w_lo_done, mat - 1)
                sp.dma_start((stage_a, stage_d)[mat % 2][:], w_qkv[mat]).then_inc(w_landed[mat % 2], 16)
                if mat == 0:
                    load_s(0)
            with sp.Fori(0, CH) as c:
                load_s(c + 1)
                for g in range(4):
                    sp.wait_ge(dve_out, c * 16 + (4 * g + 4 + DO))
                    sp.dma_start(qkv_out[bass.ds(c, 1), 2 + g].rearrange("a p k j -> p (a k) j"), stage_d[:]).then_inc(dve_stored, 16)
            sp.wait_ge(dve_stored, CH * 4 * 16 + ST)
            for comp in range(2):
                sp.wait_ge(s_landed[comp], (CH + 1) * 16)

        @block.scalar
        def _(act):
            act.sem_inc(act_out, AO)
            act.sem_inc(act_stored, ST)

            def high_s(c, buf):
                for comp in range(2):
                    act.wait_ge(s_landed[comp], c * 16 + 16)
                    for k in range(DT):
                        ins = nc.scalar.activation(grouped(s_hi, buf, comp, k), by_group(s_raw[:, comp, k, :]), ACT.Copy)
                    ins.then_inc(s_hi_done, 1)

            def high_w(mat):
                act.wait_ge(w_landed[mat % 2], 16 * (mat // 2 + 1))
                nc.scalar.activation(w_hi[:, mat, :, :], (stage_a, stage_d)[mat % 2][:], ACT.Copy).then_inc(w_hi_done, 1)

            high_w(0)
            high_s(0, 0)
            for mat in range(1, MATS):
                high_w(mat)
            act.wait_ge(b_landed, 32)
            act.wait_ge(w_lo_done, MATS)
            with act.Fori(0, CH // 2) as c2:
                for u in range(2):
                    c = act.snap(c2 * 2 + u)
                    act.wait_ge(mm_done, c * 6 + MM)
                    high_s(c + 1, 1 - u)
                    for g in range(2):
                        act.wait_ge(mm_done, c * 6 + (g + 1 + MM))
                        act.wait_ge(act_stored, c * 48 + (16 * g + ST))
                        for f in range(4):
                            nc.scalar.activation(stage_a[:, f, :], banks[g][f][:], ACT.Identity,
                                                 bias=b_col[:, g, f:f + 1]).then_inc(act_out, 1)
                        act.wait_ge(act_out, c * 8 + (4 * g + 4 + AO))
                        act.dma_start(qkv_out[bass.ds(c, 1), g].rearrange("a p k j -> p (a k) j"), stage_a[:]).then_inc(act_stored, 16)
                    act.wait_ge(dve_out, c * 16 + (8 + DO))
                    act.wait_ge(act_stored, c * 48 + (32 + ST))
                    nc.scalar.activation(stage_a[:], stage_d[:], ACT.Copy, scale=-1.0).then_inc(neg_out, 1)
                    act.wait_ge(neg_out, c + 1)
                    act.dma_start(qkv_out[bass.ds(c, 1), 6].rearrange("a p k j -> p (a k) j"), stage_a[:]).then_inc(act_stored, 16)
            act.wait_ge(act_stored, CH * 48 + ST)

        @block.vector
        def _(dve):
            dve.sem_inc(s_lo_done, SL)
            dve.sem_inc(dve_out, DO)
            dve.sem_inc(dve_stored, ST)

            def low_s(c, buf):
                for comp in range(2):
                    dve.wait_ge(s_hi_done, c * 2 + (comp + 1))
                    for k in range(DT):
                        ins = nc.vector.tensor_tensor(grouped(s_lo, buf, comp, k), by_group(s_raw[:, comp, k, :]),
                                                      grouped(s_hi, buf, comp, k).bitcast(F32), ALU.subtract)
                    ins.then_inc(s_lo_done, 1)

            def low_w(mat):
                dve.wait_ge(w_hi_done, mat + 1)
                nc.vector.tensor_tensor(w_lo[:, mat, :, :], (stage_a, stage_d)[mat % 2][:],
                                        w_hi[:, mat, :, :].bitcast(F32), ALU.subtract).then_inc(w_lo_done, 1)

            low_w(0)
            low_s(0, 0)
            for mat in range(1, MATS):
                low_w(mat)
            dve.wait_ge(b_landed, 32)
            with dve.Fori(0, CH // 2) as c2:
                for u in range(2):
                    c = dve.snap(c2 * 2 + u)
                    for g in range(4):
                        dve.wait_ge(mm_done, c * 6 + (g + 3 + MM))
                        dve.wait_ge(dve_stored, c * 64 + (16 * g + ST))
                        if g == 2:
                            dve.wait_ge(neg_out, c + 1)
                        for f in range(4):
                            if g < 2:
                                nc.vector.tensor_scalar(stage_d[:, f, :], banks[g % 2][f][:], b_col[:, 2 + g, f:f + 1], None,
                                                        ALU.add).then_inc(dve_out, 1)
                            else:
                                nc.vector.tensor_tensor(stage_d[:, f, :], banks[g % 2][f][:], bv_row[:, g - 2, :],
                                                        ALU.add).then_inc(dve_out, 1)
                        if g == 1:
                            low_s(c + 1, 1 - u)

        @block.tensor
        def _(pe):
            pe.sem_inc(mm_done, MM)
            with pe.Fori(0, CH // 2) as c2:
                for u in range(2):
                    c = pe.snap(c2 * 2 + u)
                    for g in range(6):
                        if g in (2, 3):
                            pe.wait_ge(act_out, c * 8 + (4 * g - 4 + AO))
                        else:
                            pe.wait_ge(dve_out, c * 16 + {0: 12, 1: 16, 4: 4 + DO, 5: 8 + DO}[g])
                        if u == 0:
                            pe.wait_ge(w_lo_done, g + 1)
                        comp = g % 2
                        pe.wait_ge(s_lo_done, c * 2 + (comp + 1 + SL))
                        for k in range(DT):
                            for t in range(4):
                                s = slice(P * t, P * t + P)
                                if g < 4:
                                    a = (w_hi[:, g, k, s], w_lo[:, g, k, s])
                                    b = (s_hi[:, u, comp, k, :], s_lo[:, u, comp, k, :])
                                else:
                                    a = (s_hi[:, u, comp, k, s], s_lo[:, u, comp, k, s])
                                    b = (w_hi[:, g, k, :], w_lo[:, g, k, :])
                                mm = product(nc, banks[g % 2][t][:], a, b, k == 0, k == DT - 1)
                        mm.then_inc(mm_done, 1)


def attention(nc, qkv_in, w_o, b_oT, attn_out):
    with ExitStack() as ctx:
        m = Mem(nc, ctx, "attn")
        G = P // 32
        SCALE = float(HD) ** -0.5
        w_hi = m.sb("w_hi", [P, 2, DT, 512], R32)
        w_lo = m.sb("w_lo", [P, 2, DT, 512], R32)
        q = m.sb("q", [P, H, 512])
        kk = m.sb("kk", [P, H, 2, 512])
        v = m.sb("v", [P, G, H, 2, HD])
        o_hi = m.sb("o_hi", [P, 2, DT, 512], R32)
        o_lo = m.sb("o_lo", [P, 2, DT, 512], R32)
        stage = m.sb("stage", [P, 2, DT, 512])
        masked = m.sb("masked", [P, 2, 512])
        mask = m.sb("mask", [P, 32])
        score = m.sb("score", [P, H * G * 8])
        square = m.sb("square", [P, H * G * 8])
        mag = m.sb("mag", [P, H * G, N])
        top = m.sb("top", [P, H * G])
        total = m.sb("total", [P, H * G])
        weight = m.sb("weight", [P, H * G, N])
        turned = m.sb("turned", [P, H * G, N])
        spread = m.sb("spread", [P, 8, 512])
        b_col = m.sb("b_col", [P, 2, DT])
        banks = [m.bank(f"bank{i}") for i in range(8)]

        b_landed, w_landed = m.sem("b_landed"), m.sem("w_landed")
        q_landed, v_landed = m.sem("q_landed"), m.sem("v_landed")
        w_hi_done, w_lo_done, mask_done = m.sem("w_hi_done"), m.sem("w_lo_done"), m.sem("mask_done")
        pair_done, masked_done, score_done = m.sem("pair_done"), m.sem("masked_done"), m.sem("score_done")
        step, mag_done, exp_done, turned_done = m.sem("step"), m.sem("mag_done"), m.sem("exp_done"), m.sem("turned_done")
        sum_done = m.sem("sum_done")
        spread_done, av_done, o_hi_done, o_lo_done = m.sem("spread_done"), m.sem("av_done"), m.sem("o_hi_done"), m.sem("o_lo_done")
        wo_done, out_done = m.sem("wo_done"), m.sem("out_done")
        stored = [m.sem(f"stored{i}") for i in range(2)]
        block = ctx.enter_context(nc.Block())

        STEPS = 6
        OD, ST = 8, 16

        @block.sync
        def _(sp):
            sp.dma_start(b_col[:], b_oT).then_inc(b_landed, 16)
            for mat in range(2):
                sp.dma_start(stage[:, mat, :, :], w_o[mat]).then_inc(w_landed, 16)

            def rows(c, kind, half):
                return qkv_in[bass.ds(c, 1), kind, 64 * half:64 * half + 64].rearrange("a p f j -> p (a f) j")

            def load(c, waits):
                if waits:
                    sp.wait_ge(pair_done, c * 16)
                for half in range(2):
                    for comp in range(2):
                        part = slice(64 * comp, 64 * comp + 64)
                        sp.dma_start(q[part, half::2, :], rows(c, comp, half)).then_inc(q_landed, 16)
                        sp.dma_start(kk[part, half::2, 0, :], rows(c, 2 + comp, half)).then_inc(q_landed, 16)
                        sp.dma_start(kk[part, half::2, 1, :], rows(c, (6, 2)[comp], half)).then_inc(q_landed, 16)
                if waits:
                    sp.wait_ge(av_done, c * 8)
                for comp in range(2):
                    sp.dma_start(v[:, :, :, comp, :].rearrange("p g h d -> p (g h) d"),
                                 qkv_in[bass.ds(c, 1), 4 + comp].rearrange("a p g (h d) -> p (a g h) d", h=H)).then_inc(v_landed, 16)

            load(0, False)
            with sp.Fori(1, CH) as c:
                load(c, True)

        def chunks(eng, first, rest, tail=None):
            first(0)
            with eng.Fori(1, CH) as c:
                rest(c)
            if tail:
                tail()

        @block.gpsimd
        def _(pool):
            nc.gpsimd.memset(mask[:], 0.0).then_inc(mask_done, 1)
            pool.wait_ge(mask_done, 1)
            for n in range(N):
                if n:
                    pool.wait_ge(mask_done, n + 1)
                nc.gpsimd.affine_select(out=mask[:], in_=mask[:], compare_op=ALU.not_equal, fill=1.0, base=-32 * n,
                                        pattern=[[-1, 32]], channel_multiplier=1).then_inc(mask_done, 1)
            pool.wait_ge(mask_done, 5)

            def spread_out(c):
                for i in range(8):
                    hh, g = i // 4, i % 4
                    pool.wait_ge(turned_done, (c + 1) * 16)
                    w = turned[:].rearrange("p (h g) n -> p h g n", g=G)[:, 4 * hh:4 * hh + 4, g, :]
                    for j in range(4):
                        ins = nc.gpsimd.tensor_tensor(
                            spread[:, i, P * j:P * j + P].rearrange("p (n t) -> p n t", n=N),
                            w[:, j, :].unsqueeze(2).to_broadcast([P, N, 32]),
                            mask[:].unsqueeze(1).to_broadcast([P, N, 32]), ALU.mult)
                    ins.then_inc(spread_done, 1)

            chunks(pool, spread_out, spread_out)

        @block.scalar
        def _(act):
            act.sem_inc(out_done, OD)
            for comp in range(2):
                act.sem_inc(stored[comp], ST)
            for mat in range(2):
                act.wait_ge(w_landed, 32)
                nc.scalar.activation(w_hi[:, mat, :, :], stage[:, mat, :, :], ACT.Copy).then_inc(w_hi_done, 1)
            act.wait_ge(b_landed, 16)
            act.wait_ge(w_lo_done, 2)

            def magnitudes(c):
                act.wait_ge(step, c * STEPS + 2)
                nc.scalar.activation(mag[:], mag[:], ACT.Sqrt).then_inc(mag_done, 1)
                act.wait_ge(step, c * STEPS + 4)
                nc.scalar.activation(weight[:], mag[:], ACT.Exp, scale=SCALE).then_inc(exp_done, 1)

            def values(c):
                for h in range(H):
                    act.wait_ge(av_done, c * 8 + (h + 1))
                    for comp in range(2):
                        part, to = slice(64 * comp, 64 * comp + 64), slice(64 * (h % 2), 64 * (h % 2) + 64)
                        nc.scalar.activation(o_hi[to, comp, h // 2, :], banks[4 + h % 4][part, :], ACT.Copy).then_inc(o_hi_done, 1)

            def outputs(c):
                for comp in range(2):
                    act.wait_ge(wo_done, c * 2 + (comp + 1))
                    act.wait_ge(stored[comp], c * 16 + ST)
                    for f in range(4):
                        nc.scalar.activation(stage[:, comp, f, :].rearrange("p (n g t) -> p n g t", n=N, g=G),
                                             banks[4 - 4 * comp + f][:].rearrange("p (g n t) -> p n g t", n=N, g=G), ACT.Identity,
                                             bias=b_col[:, comp, f:f + 1]).then_inc(out_done, 1)
                    act.wait_ge(out_done, c * 8 + (4 * comp + 4 + OD))
                    act.dma_start(attn_out[bass.ds(c, 1), comp].rearrange("a p f j -> p (a f) j"),
                                  stage[:, comp, :, :]).then_inc(stored[comp], 16)

            def first(c):
                magnitudes(c)
                values(c)

            def rest(c):
                magnitudes(c)
                outputs(c - 1)
                values(c)

            chunks(act, first, rest, lambda: outputs(CH - 1))
            for comp in range(2):
                act.wait_ge(stored[comp], CH * 16 + ST)

        @block.vector
        def _(dve):
            for mat in range(2):
                dve.wait_ge(w_hi_done, mat + 1)
                nc.vector.tensor_tensor(w_lo[:, mat, :, :], stage[:, mat, :, :], w_hi[:, mat, :, :].bitcast(F32),
                                        ALU.subtract).then_inc(w_lo_done, 1)
            dve.wait_ge(mask_done, 5)

            def scores(c):
                for i in range(16):
                    dve.wait_ge(pair_done, c * 16 + (i + 1))
                    nc.vector.tensor_tensor(masked[:, i % 2, :].rearrange("p (a t) -> p a t", t=32),
                                            banks[i % 4][:].rearrange("p (a t) -> p a t", t=32),
                                            mask[:].unsqueeze(1).to_broadcast([P, 16, 32]), ALU.mult).then_inc(masked_done, 1)
                    dve.wait_ge(masked_done, c * 16 + (i + 1))
                    nc.vector.tensor_reduce(score[:, 16 * i:16 * i + 16], masked[:, i % 2, :].rearrange("p (a t) -> p a t", t=32),
                                            AX.X, ALU.add).then_inc(score_done, 1)

            def softmax(c):
                b = c * STEPS
                dve.wait_ge(score_done, c * 16 + 16)
                nc.vector.tensor_tensor(square[:], score[:], score[:], ALU.mult).then_inc(step, 1)
                dve.wait_ge(step, b + 1)
                parts = square[:].rearrange("p (a w n) -> p a w n", w=2, n=N)
                nc.vector.scalar_tensor_tensor(out=mag[:], in0=parts[:, :, 0, :], scalar=1e-8, in1=parts[:, :, 1, :],
                                               op0=ALU.add, op1=ALU.add).then_inc(step, 1)
                dve.wait_ge(mag_done, c + 1)
                nc.vector.tensor_reduce(top[:], mag[:], AX.X, ALU.max).then_inc(step, 1)
                dve.wait_ge(step, b + 3)
                nc.vector.tensor_tensor(mag[:], mag[:], top[:].unsqueeze(2).to_broadcast([P, H * G, N]),
                                        ALU.subtract).then_inc(step, 1)
                dve.wait_ge(exp_done, c + 1)
                nc.vector.tensor_reduce(total[:], weight[:], AX.X, ALU.add).then_inc(sum_done, 1)
                dve.wait_ge(sum_done, c + 1)
                nc.vector.reciprocal(total[:], total[:]).then_inc(step, 1)
                dve.wait_ge(step, b + 5)
                nc.vector.tensor_tensor(weight[:], weight[:], total[:].unsqueeze(2).to_broadcast([P, H * G, N]),
                                        ALU.mult).then_inc(step, 1)
                dve.wait_ge(step, b + 6)
                for n in range(N):
                    for k in range(N):
                        nc.vector.tensor_copy(turned[32 * k:32 * k + 32, :, n], weight[32 * n:32 * n + 32, :, k]).then_inc(turned_done, 1)

            def values(c):
                for h in range(H):
                    for comp in range(2):
                        dve.wait_ge(o_hi_done, c * 16 + (2 * h + comp + 1))
                        part, to = slice(64 * comp, 64 * comp + 64), slice(64 * (h % 2), 64 * (h % 2) + 64)
                        nc.vector.tensor_tensor(o_lo[to, comp, h // 2, :], banks[4 + h % 4][part, :],
                                                o_hi[to, comp, h // 2, :].bitcast(F32), ALU.subtract).then_inc(o_lo_done, 1)

            def whole(c):
                scores(c)
                softmax(c)
                values(c)

            chunks(dve, whole, whole)

        @block.tensor
        def _(pe):
            def scores(c):
                pe.wait_ge(q_landed, (c + 1) * (12 * 16))
                for i in range(16):
                    h, pair = i // 2, i % 2
                    if i >= 4 or type(c) is not int:
                        pe.wait_ge(masked_done, c * 16 + (i - 3))
                    if i == 0:
                        pe.wait_ge(out_done, c * 8)
                    for gi in range(2):
                        s = slice(P * (2 * pair + gi), P * (2 * pair + gi) + P)
                        mm = nc.tensor.matmul(banks[i % 4][:, 256 * gi:256 * gi + 256].rearrange("p (w r) -> p w r", w=2),
                                              q[:, h, s], kk[:, h, :, s], start=True, stop=True)
                    mm.then_inc(pair_done, 1)

            def values(c):
                pe.wait_ge(v_landed, (c + 1) * 32)
                if type(c) is not int:
                    pe.wait_ge(out_done, c * 8 + 4)
                for hh in range(2):
                    for g in range(G):
                        pe.wait_ge(spread_done, c * 8 + (4 * hh + g + 1))
                        for j in range(4):
                            h = 4 * hh + j
                            if hh and not g:
                                pe.wait_ge(o_lo_done, c * 16 + (2 * j + 2))
                            mm = nc.tensor.matmul(banks[4 + j][:, P * g:P * g + P], v[:, g, h, :, :].rearrange("p w d -> p (w d)"),
                                                  spread[:, 4 * hh + g, P * j:P * j + P], start=True, stop=True)
                            if g == G - 1:
                                mm.then_inc(av_done, 1)

            def outputs(c):
                pe.wait_ge(w_lo_done, 2)
                pe.wait_ge(o_lo_done, (c + 1) * 16)
                for comp in range(2):
                    if comp:
                        pe.wait_ge(masked_done, CH * 16 if type(c) is int else (c + 2) * 16)
                    for k in range(DT):
                        for f in range(4):
                            s = slice(P * f, P * f + P)
                            mm = product(nc, banks[4 - 4 * comp + f][:], (w_hi[:, comp, k, s], w_lo[:, comp, k, s]),
                                         (o_hi[:, comp, k, :], o_lo[:, comp, k, :]), k == 0, k == DT - 1)
                    mm.then_inc(wo_done, 1)

            def first(c):
                scores(c)
                values(c)

            def rest(c):
                scores(c)
                outputs(c - 1)
                values(c)

            chunks(pe, first, rest, lambda: outputs(CH - 1))


def superposition(nc, attn_in, w_int, ids, tables, sup_out):
    with ExitStack() as ctx:
        m = Mem(nc, ctx, "sup")
        HD2 = D // 2
        w_hi = m.sb("w_hi", [P, 2 * N, DT, 512], R32)
        w_lo = m.sb("w_lo", [P, 2 * N, DT, 512], R32)
        a_raw = m.sb("a_raw", [P, 2, 2, DT, P])
        a_hi = m.sb("a_hi", [P, 2, 2, DT, P], R32)
        a_lo = m.sb("a_lo", [P, 2, 2, DT, P], R32)
        u = m.sb("u", [P, 2, N, 2, 512])
        part = m.sb("part", [P, 512])
        mag = m.sb("mag", [P, N, HD2])
        g = m.sb("g", [P, N, HD2])
        cos = m.sb("cos", [P, 6, HD2])
        cos_i = m.sb("cos_i", [P, 3, HD2])
        index = m.sb("index", [P, CH, N], I32)
        strengths = m.sb("strengths", [P, CH, N, N])
        strength = m.sb("strength", [P, N, N])
        norm = m.sb("norm", [P, 2])
        banks = [m.bank(f"bank{i}") for i in range(8)]

        index_landed, strengths_landed = m.sem("index_landed"), m.sem("strengths_landed")
        w_landed = [m.sem(f"w_landed{i}") for i in range(4)]
        a_landed = [m.sem(f"a_landed{i}") for i in range(2)]
        w_hi_done, w_lo_done, a_hi_done, a_lo_done = m.sem("w_hi_done"), m.sem("w_lo_done"), m.sem("a_hi_done"), m.sem("a_lo_done")
        mm_done, part_done, ui_out, ur_out = m.sem("mm_done"), m.sem("part_done"), m.sem("ui_out"), m.sem("ur_out")
        sq_done, m2_done, mag_done, inv_done = m.sem("sq_done"), m.sem("m2_done"), m.sem("mag_done"), m.sem("inv_done")
        unit_r, unit_i, cos_r_done, cos_i_done = m.sem("unit_r"), m.sem("unit_i"), m.sem("cos_r_done"), m.sem("cos_i_done")
        cos_sum, cos_done, clean_done, g_step, g_done = m.sem("cos_sum"), m.sem("cos_done"), m.sem("clean_done"), m.sem("g_step"), m.sem("g_done")
        r_step, i_step = m.sem("r_step"), m.sem("i_step")
        strength_done, norm_sum, norm_eps, norm_root, norm_done, sup_done = (m.sem(x) for x in (
            "strength_done", "norm_sum", "norm_eps", "norm_root", "norm_done", "sup_done"))
        stored = m.sem("stored")
        block = ctx.enter_context(nc.Block())
        MM, OUT, STEP, NORM, ST = 3, 2, 3, 1, 32

        def chunks(eng, body, tail):
            body(0, 0, False)
            with eng.Fori(0, CH // 2 - 1) as c2:
                for par in (1, 0):
                    body(eng.snap(c2 * 2 + (2 - par)), par, True)
            body(CH - 1, 1, True)
            for quarter in range(4):
                tail(CH - 1, 1, quarter)

        def slot(mat):
            return u[:, mat // 2 % 2, 2 * (mat % 2):2 * (mat % 2) + 2].rearrange("p n w j -> p (n w j)")

        @block.sync
        def _(sp):
            sp.dma_start(index[:], ids).then_inc(index_landed, 16)

            def load_a(c, n):
                for comp in range(2):
                    sp.dma_start(a_raw[:, n % 2, comp], attn_in[bass.ds(c, 1), comp, :, :, P * n:P * n + P].rearrange("a p f t -> p (a f) t")
                                 ).then_inc(a_landed[n % 2], 16)

            def load_w(mat):
                sp.dma_start(slot(mat), w_int[mat]).then_inc(w_landed[mat % 4], 16)

            for mat in range(4):
                load_w(mat)
            load_a(0, 0)
            load_a(0, 1)
            for mat in range(4, 8):
                sp.wait_ge(w_lo_done, mat - 3)
                load_w(mat)
            with sp.Fori(0, CH) as c:
                for n in range(N):
                    sp.wait_ge(a_lo_done, c * N + (n + 1))
                    load_a(c if n < 2 else (c + 1) % CH, (n + 2) % N)
            for s in range(2):
                sp.wait_ge(a_landed[s], (CH * 2 + 1) * 32)

        @block.gpsimd
        def _(pool):
            pool.wait_ge(index_landed, 16)
            for c in range(CH):
                for f in range(N):
                    nc.gpsimd.indirect_dma_start(out=strengths[:, c, f, :], out_offset=None, in_=tables[f],
                                                 in_offset=bass.IndirectOffsetOnAxis(ap=index[:, c, f:f + 1], axis=0)
                                                 ).then_inc(strengths_landed, 16)

            def slices(c, par, quarter):
                d, late = quarter // 2, quarter % 2
                h = c * 2 + (d + 1)
                ui = u[:, par, :, 1, HD2 * d:HD2 * d + HD2]
                if not late:
                    pool.wait_ge(sq_done, h)
                    nc.gpsimd.tensor_tensor(mag[:], mag[:], g[:], ALU.add).then_inc(m2_done, 1)
                    pool.wait_ge(inv_done, h)
                    nc.gpsimd.tensor_tensor(ui, ui, g[:], ALU.mult).then_inc(unit_i, 1)
                    pool.wait_ge(unit_i, h)
                    nc.gpsimd.tensor_tensor(cos_i[:], ui[:, 0:3], ui[:, 1:4], ALU.mult)
                    pool.wait_ge(unit_r, h)
                    nc.gpsimd.tensor_tensor(g[:, 0:2], ui[:, 0:2], ui[:, 2:4], ALU.mult)
                    nc.gpsimd.tensor_tensor(g[:, 2:3], ui[:, 0:1], ui[:, 3:4], ALU.mult).then_inc(cos_i_done, 1)
                else:
                    pool.wait_ge(clean_done, h)
                    pool.wait_ge(g_done, h)
                    nc.gpsimd.tensor_tensor(ui, ui, g[:], ALU.mult).then_inc(i_step, 1)
                    pool.wait_ge(i_step, h * 3 + (STEP - 2))
                    nc.gpsimd.tensor_tensor(ui[:, 0:2], ui[:, 0:2], ui[:, 2:4], ALU.add).then_inc(i_step, 1)
                    pool.wait_ge(i_step, h * 3 + (STEP - 1))
                    nc.gpsimd.tensor_tensor(ui[:, 0:1], ui[:, 0:1], ui[:, 1:2], ALU.add).then_inc(i_step, 1)

            def body(c, par, due):
                if due:
                    for quarter in range(4):
                        slices(c - 1, 1 - par, quarter)

            pool.sem_inc(i_step, STEP)
            chunks(pool, body, slices)

        @block.scalar
        def _(act):
            act.sem_inc(ui_out, OUT)
            act.sem_inc(norm_sum, NORM)
            act.sem_inc(stored, ST)

            def high_a(c, n):
                act.wait_ge(a_landed[n % 2], c * 64 + 32 * (n // 2 + 1))
                act.wait_ge(mm_done, c * 12 + (3 * n - 3 + MM))
                nc.scalar.activation(a_hi[:, n % 2], a_raw[:, n % 2], ACT.Copy).then_inc(a_hi_done, 1)

            def high_w(mat):
                act.wait_ge(w_landed[mat % 4], 16 * (mat // 4 + 1))
                nc.scalar.activation(w_hi[:, mat, :, :].rearrange("p k j -> p (k j)"), slot(mat), ACT.Copy).then_inc(w_hi_done, 1)

            def slices(c, par, quarter):
                d, late = quarter // 2, quarter % 2
                h = c * 2 + (d + 1)
                cols = slice(HD2 * d, HD2 * d + HD2)
                if not late:
                    act.wait_ge(ur_out, c * 4 + (4 + OUT))
                    act.wait_ge(ui_out, c * 4 + (4 + OUT))
                    act.wait_ge(r_step, h * 3)
                    act.wait_ge(i_step, h * 3)
                    nc.scalar.activation(mag[:], u[:, par, :, 0, cols], ACT.Square)
                    nc.scalar.activation(g[:], u[:, par, :, 1, cols], ACT.Square).then_inc(sq_done, 1)
                    act.wait_ge(m2_done, h)
                    nc.scalar.activation(mag[:], mag[:], ACT.Sqrt).then_inc(mag_done, 1)
                elif d == 1:
                    sup = u[:, par, 0, :, :].rearrange("p w j -> p (w j)")
                    act.wait_ge(r_step, h * 3 + STEP)
                    act.wait_ge(i_step, h * 3 + STEP)
                    nc.scalar.activation(cos[:].rearrange("p a j -> p (a j)")[:, 0:2 * D], sup, ACT.Square,
                                         accum_out=norm[:, 0:1]).then_inc(norm_sum, 1)
                    act.wait_ge(norm_eps, c + 1)
                    nc.scalar.activation(norm[:, 0:1], norm[:, 0:1], ACT.Sqrt).then_inc(norm_root, 1)
                    act.wait_ge(sup_done, c + 1)
                    act.dma_start(sup_out[bass.ds(c, 1)].rearrange("a p j -> p (a j)"), sup).then_inc(stored, 16)

            high_w(0)
            high_w(1)
            act.wait_ge(a_landed[0], 32)
            nc.scalar.activation(a_hi[:, 0], a_raw[:, 0], ACT.Copy).then_inc(a_hi_done, 1)
            for mat in range(2, 8):
                high_w(mat)
            act.wait_ge(w_lo_done, 8)

            def body(c, par, due):
                for n in range(N):
                    w = c * N + n
                    high_a(c + (n + 1) // N, (n + 1) % N)
                    if n == 0:
                        act.wait_ge(stored, c * 16 + 16)
                    act.wait_ge(mm_done, c * 12 + (3 * n + 1 + MM))
                    act.wait_ge(ur_out, c * 4 + (n + OUT))
                    nc.scalar.activation(part[:], banks[n % 2 * 3][:], ACT.Copy).then_inc(part_done, 1)
                    act.wait_ge(mm_done, c * 12 + (3 * n + 3 + MM))
                    nc.scalar.activation(u[:, par, n, 1, :], banks[n % 2 * 3 + 2][:], ACT.Copy).then_inc(ui_out, 1)
                    if due:
                        slices(c - 1, 1 - par, n)

            chunks(act, body, slices)
            act.wait_ge(stored, CH * 16 + ST)

        @block.vector
        def _(dve):
            dve.sem_inc(ur_out, OUT)
            dve.sem_inc(r_step, STEP)

            def low_a(c, n):
                dve.wait_ge(a_hi_done, c * N + (n + 1))
                nc.vector.tensor_tensor(a_lo[:, n % 2], a_raw[:, n % 2], a_hi[:, n % 2].bitcast(F32),
                                        ALU.subtract).then_inc(a_lo_done, 1)

            def low_w(mat):
                dve.wait_ge(w_hi_done, mat + 1)
                nc.vector.tensor_tensor(w_lo[:, mat, :, :].rearrange("p k j -> p (k j)"), slot(mat),
                                        w_hi[:, mat, :, :].rearrange("p k j -> p (k j)").bitcast(F32),
                                        ALU.subtract).then_inc(w_lo_done, 1)

            def s(i, j):
                return strength[:, i, j:j + 1]

            PAIR = {(0, 1): 0, (1, 2): 1, (2, 3): 2, (0, 2): 3, (1, 3): 4, (0, 3): 5}

            def slices(c, par, quarter):
                d, late = quarter // 2, quarter % 2
                h = c * 2 + (d + 1)
                cols = slice(HD2 * d, HD2 * d + HD2)
                ur = u[:, par, :, 0, cols]
                if not late:
                    if d == 0:
                        dve.wait_ge(strengths_landed, CH * N * 16)
                        nc.vector.tensor_copy(strength[:], strengths[:, bass.ds(c, 1)].rearrange("p a i j -> p (a i) j")).then_inc(strength_done, 1)
                        dve.wait_ge(norm_sum, c + NORM)
                    dve.wait_ge(mag_done, h)
                    nc.vector.reciprocal(g[:], mag[:]).then_inc(inv_done, 1)
                    dve.wait_ge(inv_done, h)
                    nc.vector.tensor_tensor(ur, ur, g[:], ALU.mult).then_inc(unit_r, 1)
                    dve.wait_ge(unit_r, h)
                    nc.vector.tensor_tensor(cos[:, 0:3], ur[:, 0:3], ur[:, 1:4], ALU.mult)
                    nc.vector.tensor_tensor(cos[:, 3:5], ur[:, 0:2], ur[:, 2:4], ALU.mult)
                    nc.vector.tensor_tensor(cos[:, 5:6], ur[:, 0:1], ur[:, 3:4], ALU.mult).then_inc(cos_r_done, 1)
                    dve.wait_ge(cos_r_done, h)
                    dve.wait_ge(cos_i_done, h)
                    nc.vector.tensor_tensor(cos[:, 0:3], cos[:, 0:3], cos_i[:], ALU.add)
                    nc.vector.tensor_tensor(cos[:, 3:6], cos[:, 3:6], g[:, 0:3], ALU.add).then_inc(cos_sum, 1)
                    return
                dve.wait_ge(cos_sum, h)
                nc.vector.tensor_scalar(cos[:], cos[:], 1.0, None, ALU.min).then_inc(cos_done, 1)
                nc.vector.tensor_scalar(u[:, par, :, :, cols], u[:, par, :, :, cols], 1.0, -1.0, ALU.min, ALU.max).then_inc(clean_done, 1)
                dve.wait_ge(cos_done, h)
                if d == 0:
                    dve.wait_ge(strength_done, c + 1)
                for r in range(3):
                    for j in range(N):
                        i = [x for x in range(N) if x != j][r]
                        pair = cos[:, PAIR[min(i, j), max(i, j)], :]
                        if r == 0:
                            nc.vector.tensor_scalar(g[:, j, :], pair, s(i, j), s(j, j), ALU.mult, ALU.add).then_inc(g_step, 1)
                        else:
                            dve.wait_ge(g_step, h * 12 + (4 * r + j - 15))
                            nc.vector.scalar_tensor_tensor(out=g[:, j, :], in0=pair, scalar=s(i, j), in1=g[:, j, :],
                                                           op0=ALU.mult, op1=ALU.add).then_inc(g_step, 1)
                dve.wait_ge(g_step, h * 12)
                nc.vector.tensor_tensor(g[:], g[:], mag[:], ALU.mult).then_inc(g_done, 1)
                dve.wait_ge(g_done, h)
                dve.wait_ge(clean_done, h)
                nc.vector.tensor_tensor(ur, ur, g[:], ALU.mult).then_inc(r_step, 1)
                dve.wait_ge(r_step, h * 3 + (STEP - 2))
                nc.vector.tensor_tensor(ur[:, 0:2], ur[:, 0:2], ur[:, 2:4], ALU.add).then_inc(r_step, 1)
                dve.wait_ge(r_step, h * 3 + (STEP - 1))
                nc.vector.tensor_tensor(ur[:, 0:1], ur[:, 0:1], ur[:, 1:2], ALU.add).then_inc(r_step, 1)
                if d == 1:
                    sup = u[:, par, 0, :, :].rearrange("p w j -> p (w j)")
                    dve.wait_ge(norm_sum, c + (1 + NORM))
                    nc.vector.tensor_scalar(norm[:, 0:1], norm[:, 0:1], 1e-8, None, ALU.add).then_inc(norm_eps, 1)
                    dve.wait_ge(norm_root, c + 1)
                    nc.vector.reciprocal(norm[:, 1:2], norm[:, 0:1]).then_inc(norm_done, 1)
                    dve.wait_ge(norm_done, c + 1)
                    nc.vector.tensor_scalar(sup, sup, norm[:, 1:2], None, ALU.mult).then_inc(sup_done, 1)

            low_w(0)
            low_w(1)
            low_a(0, 0)
            for mat in range(2, 8):
                low_w(mat)

            def body(c, par, due):
                for n in range(N):
                    low_a(c + (n + 1) // N, (n + 1) % N)
                    dve.wait_ge(mm_done, c * 12 + (3 * n + 2 + MM))
                    dve.wait_ge(part_done, c * 4 + (n + 1))
                    nc.vector.tensor_tensor(u[:, par, n, 0, :], banks[n % 2 * 3 + 1][:], part[:], ALU.subtract).then_inc(ur_out, 1)
                    if due:
                        slices(c - 1, 1 - par, n)

            chunks(dve, body, slices)

        @block.tensor
        def _(pe):
            pe.sem_inc(mm_done, MM)

            def body(c, par, due):
                for n in range(N):
                    if not due:
                        pe.wait_ge(w_lo_done, 2 * n + 2)
                    pe.wait_ge(a_lo_done, c * N + (n + 1))
                    pe.wait_ge(ur_out, c * 4 + (n - 1 + OUT))
                    pe.wait_ge(ui_out, c * 4 + (n - 1 + OUT))
                    for x, terms in enumerate((((1, 1),), ((0, 0),), ((0, 1), (1, 0)))):
                        for i, (comp, w) in enumerate(terms):
                            for k in range(DT):
                                mm = product(nc, banks[n % 2 * 3 + x][:], (a_hi[:, n % 2, comp, k, :], a_lo[:, n % 2, comp, k, :]),
                                             (w_hi[:, 2 * n + w, k, :], w_lo[:, 2 * n + w, k, :]),
                                             i == 0 and k == 0, i == len(terms) - 1 and k == DT - 1)
                        mm.then_inc(mm_done, 1)

            chunks(pe, body, lambda c, par, quarter: None)


def tower(nc, sup_in, xT, w_tail, b_post, g_postT, be_postT, b1T, b2T, w3, y_out):
    with ExitStack() as ctx:
        m = Mem(nc, ctx, "tower")
        RAW, RING = 3, 6
        sup = m.sb("sup", [P, 4, 2 * D])
        sup_hi = m.sb("sup_hi", [P, 2 * DT, HALF], R32)
        sup_lo = m.sb("sup_lo", [P, 2 * DT, HALF], R32)
        w_raw = m.sb("w_raw", [P, RAW, 2, 512])
        w_hi = m.sb("w_hi", [P, RING, 512], R32)
        w_lo = m.sb("w_lo", [P, RING, 512], R32)
        x_raw = m.sb("x_raw", [P, 4, HALF])
        x_hi = m.sb("x_hi", [P, 4, HALF], R32)
        x_lo = m.sb("x_lo", [P, 4, HALF], R32)
        square = m.sb("square", [P, 2, HALF])
        f32 = m.sb("f32", [P, DT, HALF])
        y_hi = [m.sb(f"y_hi{i}", [P, DT, HALF], R32) for i in range(3)]
        y_lo = [m.sb(f"y_lo{i}", [P, DT, HALF], R32) for i in range(3)]
        post = m.sb("post", [P, 4, D])
        h2 = m.sb("h2", [P, 2, HALF])
        y = m.sb("y", [1, HALF])
        ident = m.sb("ident", [P, P])
        post_row = m.sb("post_row", [P, D])
        stats = m.sb("stats", [P, 4, 6])
        mean_var = m.sb("mean_var", [P, 4, 2])
        std = m.sb("std", [P, 4])
        rstd = m.sb("rstd", [P, 4])
        gain = m.sb("gain", [P, DT])
        shift = m.sb("shift", [P, DT])
        b1 = m.sb("b1", [P, DT])
        b2 = m.sb("b2", [P, 2])
        w3_col = m.sb("w3_col", [P, 2])
        banks = [m.bank(f"bank{i}") for i in range(8)]

        TILES = ([("mr", k, 1) for k in range(4)] + [("mr", 4 + k, -1) for k in range(4)]
                 + [("mi", 4 + k, 1) for k in range(4)] + [("mi", k, 1) for k in range(4)]
                 + [("x", k, 1) for k in range(8)] + [("post", k, 1) for k in range(4)]
                 + [("x", 8 + k, 1) for k in range(8)] + [("z", k, 1) for k in range(4)]
                 + [("top2", k, 1) for k in range(2)])
        PAIRS = [0, 1, 2, 3, 0, 1, 2, 3, 6, 7, 8, 9, 4, 5, 10, 11, 12, 13, 14, 15, 16]
        NT = len(TILES)
        FIRST = {layer: [t[0] for t in TILES].index(layer) for layer in ("mr", "mi", "x", "post", "z", "top2")}
        X_AT = [i for i, t in enumerate(TILES) if t[0] == "x"]

        c_landed, ident_ready = m.sem("c_landed"), m.sem("ident_ready")
        sup_landed = m.sem("sup_landed")
        w_landed = [m.sem(f"w_landed{i}") for i in range(RAW)]
        x_landed = [m.sem(f"x_landed{i}") for i in range(4)]
        w_hi_done, w_lo_done, w_used = m.sem("w_hi_done"), m.sem("w_lo_done"), m.sem("w_used")
        x_hi_done, x_lo_done = m.sem("x_hi_done"), m.sem("x_lo_done")
        turned, sup_hi_done, sup_lo_done = m.sem("turned"), m.sem("sup_hi_done"), m.sem("sup_lo_done")
        sq_done, power, amp_done = m.sem("sq_done"), m.sem("power"), m.sem("amp_done")
        f32_done, y_hi_done, y_lo_done = m.sem("f32_done"), m.sem("y_hi_done"), m.sem("y_lo_done")
        post_done, stat_done, var_done, std_done, rstd_done, z_done, zt_done = (m.sem(x) for x in (
            "post_done", "stat_done", "var_done", "std_done", "rstd_done", "z_done", "zt_done"))
        h2_done, top_done, y_done, y_stored = m.sem("h2_done"), m.sem("top_done"), m.sem("y_done"), m.sem("y_stored")
        block = ctx.enter_context(nc.Block())

        LO, XL, SL, ST = 2 * RAW, 4, 8, 16

        @block.sync
        def _(sp):
            for to, of in ((post_row[:], b_post.partition_broadcast(P)), (gain[:], g_postT), (shift[:], be_postT),
                           (b1[:], b1T), (b2[:], b2T), (w3_col[:], w3)):
                sp.dma_start(to, of).then_inc(c_landed, 16)
            with sp.Fori(0, HALVES) as hf:
                sp.wait_ge(sup_lo_done, hf * 8 + SL)
                sp.dma_start(sup[:], sup_in[bass.ds(hf * 4, 4)].rearrange("t p j -> p t j")).then_inc(sup_landed, 16)
                for pair in range(NT // 2):
                    sp.wait_ge(w_lo_done, hf * NT + (2 * pair + 2 - 2 * RAW + LO))
                    sp.dma_start(w_raw[:, pair % RAW], w_tail[PAIRS[pair]]).then_inc(w_landed[pair % RAW], 16)
                    for i in (2 * pair, 2 * pair + 1):
                        if i in X_AT:
                            k = X_AT.index(i)
                            sp.wait_ge(x_lo_done, hf * KT + (k - 3 + XL))
                            sp.dma_start(x_raw[:, k % 4, :], xT[bass.ds(hf * KT + k, 1)].rearrange("a p t -> p (a t)")).then_inc(x_landed[k % 4], 16)

        @block.gpsimd
        def _(pool):
            nc.gpsimd.memset(ident[:], 0.0).then_inc(ident_ready, 1)
            pool.wait_ge(ident_ready, 1)
            nc.gpsimd.affine_select(out=ident[:], in_=ident[:], compare_op=ALU.not_equal, fill=1.0, base=0,
                                    pattern=[[-1, P]], channel_multiplier=1).then_inc(ident_ready, 1)

        @block.scalar
        def _(act):
            def high(hf, i):
                act.wait_ge(w_landed[i // 2 % RAW], hf * (NT // 2 // RAW * 16) + (i // 2 // RAW + 1) * 16)
                act.wait_ge(w_used, hf * NT + (i + 1))
                nc.scalar.activation(w_hi[:, i % RING, :], w_raw[:, i // 2 % RAW, i % 2, :], ACT.Copy,
                                     scale=float(TILES[i][2])).then_inc(w_hi_done, 1)
                if i in X_AT:
                    k = X_AT.index(i)
                    if k >= 4:
                        act.wait_ge(w_used, hf * NT + (X_AT[k - 4] + 1 + RING))
                    act.wait_ge(x_landed[k % 4], hf * 64 + (k // 4 + 1) * 16)
                    nc.scalar.activation(x_hi[:, k % 4, :], x_raw[:, k % 4, :], ACT.Copy).then_inc(x_hi_done, 1)

            def split_high(hf, layer, k):
                act.wait_ge(f32_done, hf * 12 + (4 * layer + k + 1))
                nc.scalar.activation(y_hi[layer][:, k, :], f32[:, k, :], ACT.Copy).then_inc(y_hi_done, 1)

            act.sem_inc(y_stored, ST)
            act.wait_ge(c_landed, 6 * 16)
            with act.Fori(0, HALVES) as hf:
                for k in range(8):
                    act.wait_ge(turned, hf * 8 + (k + 1))
                    nc.scalar.activation(sup_hi[:, k, :], banks[4 + k % 4][:], ACT.Copy).then_inc(sup_hi_done, 1)
                    if k < RING:
                        high(hf, k)
                for i in range(RING, FIRST["x"]):
                    high(hf, i)
                act.wait_ge(w_used, hf * NT + (FIRST["x"] + RING))
                for f in range(4):
                    if f:
                        act.wait_ge(power, hf * 4 + f)
                    nc.scalar.activation(square[:, 0, :], banks[f][:], ACT.Square)
                    nc.scalar.activation(square[:, 1, :], banks[4 + f][:], ACT.Square).then_inc(sq_done, 1)
                    high(hf, FIRST["x"] + f)
                    act.wait_ge(power, hf * 4 + (f + 1))
                    nc.scalar.activation(f32[:, f, :], f32[:, f, :], ACT.Sqrt).then_inc(f32_done, 1)
                    split_high(hf, 0, f)
                for i in range(FIRST["x"] + 4, FIRST["post"] + 4 + 7):
                    high(hf, i)
                act.wait_ge(var_done, hf + 1)
                nc.scalar.activation(std[:], mean_var[:, :, 1], ACT.Sqrt).then_inc(std_done, 1)
                high(hf, FIRST["post"] + 11)
                for k in range(4):
                    act.wait_ge(zt_done, hf * 4 + (k + 1))
                    nc.scalar.activation(f32[:, k, :], banks[k][:], ACT.Gelu, bias=shift[:, k:k + 1],
                                         scale=gain[:, k:k + 1]).then_inc(f32_done, 1)
                    split_high(hf, 1, k)
                    high(hf, FIRST["z"] + k)
                for k in range(2):
                    high(hf, FIRST["top2"] + k)
                act.wait_ge(w_used, hf * NT + (FIRST["top2"] + RING))
                for f in range(4):
                    nc.scalar.activation(f32[:, f, :], banks[4 + f][:], ACT.Relu, bias=b1[:, f:f + 1]).then_inc(f32_done, 1)
                    split_high(hf, 2, f)
                act.wait_ge(w_used, hf * NT + (NT + RING))
                for f in range(2):
                    nc.scalar.activation(h2[:, f, :], banks[f][:], ACT.Relu, bias=b2[:, f:f + 1]).then_inc(h2_done, 1)
                act.wait_ge(top_done, hf + 1)
                act.wait_ge(y_stored, hf * 16 + ST)
                nc.scalar.activation(y[:], banks[2][0:1, :], ACT.Copy).then_inc(y_done, 1)
                act.wait_ge(y_done, hf + 1)
                act.dma_start(y_out[bass.ds(hf * HALF, HALF), :].rearrange("t a -> a t"), y[:]).then_inc(y_stored, 16)
            act.wait_ge(y_stored, HALVES * 16 + ST)

        @block.vector
        def _(dve):
            def low(hf, i):
                raw, hi, lo = w_raw[:, i // 2 % RAW, i % 2, :], w_hi[:, i % RING, :].bitcast(F32), w_lo[:, i % RING, :]
                dve.wait_ge(w_hi_done, hf * NT + (i + 1))
                if TILES[i][2] < 0:
                    nc.vector.scalar_tensor_tensor(out=lo, in0=raw, scalar=-1.0, in1=hi, op0=ALU.mult,
                                                   op1=ALU.subtract).then_inc(w_lo_done, 1)
                else:
                    nc.vector.tensor_tensor(lo, raw, hi, ALU.subtract).then_inc(w_lo_done, 1)
                if i in X_AT:
                    k = X_AT.index(i)
                    dve.wait_ge(x_hi_done, hf * KT + (k + 1))
                    nc.vector.tensor_tensor(x_lo[:, k % 4, :], x_raw[:, k % 4, :], x_hi[:, k % 4, :].bitcast(F32),
                                            ALU.subtract).then_inc(x_lo_done, 1)

            def split_low(hf, layer, k):
                dve.wait_ge(y_hi_done, hf * 12 + (4 * layer + k + 1))
                nc.vector.tensor_tensor(y_lo[layer][:, k, :], f32[:, k, :], y_hi[layer][:, k, :].bitcast(F32),
                                        ALU.subtract).then_inc(y_lo_done, 1)

            dve.sem_inc(w_lo_done, LO)
            dve.sem_inc(x_lo_done, XL)
            dve.sem_inc(sup_lo_done, SL)
            dve.wait_ge(c_landed, 6 * 16)
            with dve.Fori(0, HALVES) as hf:
                for k in range(8):
                    dve.wait_ge(sup_hi_done, hf * 8 + (k + 1))
                    nc.vector.tensor_tensor(sup_lo[:, k, :], banks[4 + k % 4][:], sup_hi[:, k, :].bitcast(F32),
                                            ALU.subtract).then_inc(sup_lo_done, 1)
                    if k < RING:
                        low(hf, k)
                for i in range(RING, FIRST["x"]):
                    low(hf, i)
                for f in range(4):
                    dve.wait_ge(sq_done, hf * 4 + (f + 1))
                    nc.vector.tensor_tensor(f32[:, f, :], square[:, 0, :], square[:, 1, :], ALU.add).then_inc(power, 1)
                    low(hf, FIRST["x"] + f)
                    split_low(hf, 0, f)
                for i in range(FIRST["x"] + 4, FIRST["post"] + 4 + 7):
                    low(hf, i)
                dve.wait_ge(w_used, hf * NT + (FIRST["post"] + 4 + RING))
                for t in range(4):
                    nc.vector.tensor_tensor(post[:, t, :], banks[t][:], post_row[:], ALU.add).then_inc(post_done, 1)
                for t in range(4):
                    dve.wait_ge(post_done, hf * 4 + (t + 1))
                    nc.vector.bn_stats(stats[:, t, :], post[:, t, :]).then_inc(stat_done, 1)
                dve.wait_ge(stat_done, hf * 8 + 4)
                dve.nop(nofuse=True)
                for t in range(4):
                    nc.vector.bn_aggr(mean_var[:, t, :], stats[:, t, :]).then_inc(stat_done, 1)
                dve.wait_ge(stat_done, hf * 8 + 8)
                nc.vector.tensor_scalar(mean_var[:, :, 1], mean_var[:, :, 1], EPS, None, ALU.add).then_inc(var_done, 1)
                dve.wait_ge(std_done, hf + 1)
                nc.vector.reciprocal(rstd[:], std[:]).then_inc(rstd_done, 1)
                dve.wait_ge(rstd_done, hf + 1)
                for t in range(4):
                    nc.vector.tensor_scalar(post[:, t, :], post[:, t, :], mean_var[:, t, 0:1], rstd[:, t:t + 1], ALU.subtract,
                                            ALU.mult).then_inc(z_done, 1)
                low(hf, FIRST["post"] + 11)
                for k in range(4):
                    split_low(hf, 1, k)
                    low(hf, FIRST["z"] + k)
                for k in range(2):
                    low(hf, FIRST["top2"] + k)
                for f in range(4):
                    split_low(hf, 2, f)

        @block.tensor
        def _(pe):
            pe.sem_inc(w_used, RING)
            pe.wait_ge(ident_ready, 2)
            pe.wait_ge(c_landed, 6 * 16)
            with pe.Fori(0, HALVES) as hf:
                def w(i, cols=slice(0, 512)):
                    return (w_hi[:, i % RING, cols], w_lo[:, i % RING, cols])

                pe.wait_ge(sup_landed, hf * 16 + 16)
                for k in range(8):
                    if k < 4:
                        pe.wait_ge(sup_lo_done, hf * 8 + SL)
                    else:
                        pe.wait_ge(sup_lo_done, hf * 8 + (k - 3 + SL))
                    for t in range(4):
                        mm = nc.tensor.transpose(banks[4 + k % 4][:, P * t:P * t + P], sup[:, t, P * k:P * k + P], ident[:])
                    mm.then_inc(turned, 1)
                for i, (layer, k, _) in enumerate(TILES):
                    if i == FIRST["z"]:
                        for j in range(4):
                            pe.wait_ge(z_done, hf * 4 + 4)
                            for t in range(4):
                                mm = nc.tensor.transpose(banks[j][:, P * t:P * t + P], post[:, t, P * j:P * j + P], ident[:])
                            mm.then_inc(zt_done, 1)
                    pe.wait_ge(w_lo_done, hf * NT + (i + 1 + LO))
                    if i == FIRST["mi"]:
                        pe.wait_ge(sup_lo_done, hf * 8 + (8 + SL))
                    if layer == "mr":
                        pe.wait_ge(sup_lo_done, hf * 8 + (k + 1 + SL))
                    if layer == "x":
                        if k == 0:
                            pe.wait_ge(sq_done, hf * 4 + 4)
                        pe.wait_ge(x_lo_done, hf * KT + (k + 1 + XL))
                    if layer == "post":
                        pe.wait_ge(y_lo_done, hf * 12 + (k + 1))
                    if layer == "z":
                        pe.wait_ge(y_lo_done, hf * 12 + (4 + k + 1))
                    if layer == "top2":
                        pe.wait_ge(y_lo_done, hf * 12 + (8 + 2 * k + 2))
                        for kk in range(2):
                            for f in range(2):
                                c = 256 * kk + P * f
                                kt = 2 * k + kk
                                mm = product(nc, banks[f][:], w(i, slice(c, c + P)), (y_hi[2][:, kt, :], y_lo[2][:, kt, :]),
                                             kt == 0, kt == 3)
                        mm.then_inc(w_used, 1)
                        continue
                    for f in range(4):
                        s = slice(P * f, P * f + P)
                        if layer == "mr":
                            mm = product(nc, banks[f][:], w(i, s), (sup_hi[:, k, :], sup_lo[:, k, :]), k == 0, k == 7)
                        elif layer == "mi":
                            mm = product(nc, banks[4 + f][:], w(i, s), (sup_hi[:, k, :], sup_lo[:, k, :]), k == 4, k == 3)
                        elif layer == "post":
                            mm = product(nc, banks[f][:], (y_hi[0][:, k, s], y_lo[0][:, k, s]), w(i), k == 0, k == 3)
                        elif layer == "x":
                            mm = product(nc, banks[4 + f][:], w(i, s), (x_hi[:, k % 4, :], x_lo[:, k % 4, :]), k == 0, False)
                        else:
                            mm = product(nc, banks[4 + f][:], w(i, s), (y_hi[1][:, k, :], y_lo[1][:, k, :]), False, k == 3)
                    mm.then_inc(w_used, 1)
                for f in range(2):
                    pe.wait_ge(h2_done, hf * 2 + (f + 1))
                    mm = nc.tensor.matmul(banks[2][0:1, :], w3_col[:, f:f + 1], h2[:, f, :], start=(f == 0), stop=(f == 1))
                mm.then_inc(top_done, 1)


def kernel(**inputs):
    import concourse.bacc as bacc
    from concourse.bass_utils import run_bass_kernel_spmd

    p = {k.removeprefix("L0_rec_"): np.asarray(v) for k, v in inputs.items()}

    def tiles(w):
        return w.reshape(w.shape[0], -1, P).transpose(2, 1, 0)

    def pairs(w):
        return w.reshape(-1, 2, P, w.shape[1]).transpose(0, 2, 1, 3)

    def columns(*vectors):
        return np.stack(vectors).reshape(len(vectors), -1, P).transpose(2, 0, 1)

    enc = ("er", "ei")
    top1 = p["W_top1"]
    host = {
        "xT": p["r_x"].reshape(HALVES, HALF, KT, P).transpose(0, 2, 3, 1).reshape(HALVES * KT, P, HALF),
        "w_enc": np.stack([p[f"{e}_{w}"].reshape(4, 512, KT // 2, 2, P).transpose(0, 2, 4, 3, 1)
                           for e in enc for w in ("W1", "W2")]).reshape(-1, P, 2, 512),
        "b1": np.stack([p[f"{e}_b1"] for e in enc]).reshape(-1, 512),
        "g1T": columns(*[p[f"{e}_g1"] for e in enc]).transpose(1, 0, 2),
        "be1T": columns(*[p[f"{e}_be1"] for e in enc]).transpose(1, 0, 2),
        "b2T": columns(*[p[f"{e}_b2"] for e in enc]).transpose(1, 0, 2),
        "w_qkv": np.stack([tiles(p[n]) for n in ("Wq_r", "Wq_i", "Wk_r", "Wk_i", "Wv_r", "Wv_i")]),
        "b_qkT": columns(p["bq_r"], p["bq_i"], p["bk_r"], p["bk_i"]),
        "b_v": np.stack([p["bv_r"], p["bv_i"]]),
        "w_o": np.stack([tiles(p["Wo_r"]), tiles(p["Wo_i"])]),
        "b_oT": columns(p["bo_r"], p["bo_i"]),
        "w_int": np.stack([tiles(p[w][n]).reshape(P, DT * 512) for n in range(N) for w in ("int_Wr", "int_Wi")]),
        "ids": p["ids"].reshape(CH, P, N).transpose(1, 0, 2),
        "w_tail": np.concatenate([pairs(p["meas_Mr"].T), pairs(p["meas_Mi"].T), pairs(p["post_W"].T), pairs(top1[D:]),
                                  pairs(top1[:D]),
                                  p["W_top2"].reshape(1, 2, 2, P, 256).transpose(0, 3, 1, 2, 4).reshape(1, P, 2, 512)]),
        "b_post": p["post_b"],
        "g_postT": columns(p["post_g"])[:, 0],
        "be_postT": columns(p["post_be"])[:, 0],
        "b_top1T": columns(p["b_top1"])[:, 0],
        "b_top2T": columns(p["b_top2"])[:, 0],
        "w3": p["W_top3"].reshape(2, P).T,
    }
    for f in range(N):
        host[f"tbl_{f}"] = p[f"tbl_{f}"]
    nc = bacc.Bacc("TRN2", target_bir_lowering=False, num_devices=1)
    arrays, d = {}, {}
    for name, a in host.items():
        arrays[f"in_{name}"] = np.ascontiguousarray(a)
        d[name] = nc.dram_tensor(f"in_{name}", a.shape, mybir.dt.from_np(a.dtype), kind="ExternalInput").ap()

    def scratch(name, shape):
        return nc.dram_tensor(name, shape, F32, kind="Internal").ap()

    s = scratch("s", (CH, 2, P, DT, N, P))
    qkv = scratch("qkv", (CH, 7, P, DT, 512))
    attn = scratch("attn", (CH, 2, P, DT, 512))
    sup = scratch("sup", (CH, P, 2 * D))
    y = nc.dram_tensor("out_y", (TOK, 1), F32, kind="ExternalOutput").ap()
    encoders(nc, d["xT"], d["w_enc"], d["b1"], d["g1T"], d["be1T"], d["b2T"], s)
    projections(nc, s, d["w_qkv"], d["b_qkT"], d["b_v"], qkv)
    attention(nc, qkv, d["w_o"], d["b_oT"], attn)
    superposition(nc, attn, d["w_int"], d["ids"], [d[f"tbl_{f}"] for f in range(N)], sup)
    tower(nc, sup, d["xT"], d["w_tail"], d["b_post"], d["g_postT"], d["be_postT"], d["b_top1T"], d["b_top2T"], d["w3"], y)
    return run_bass_kernel_spmd(nc, [arrays], core_ids=[0]).results[0]["out_y"]
```

```python
from contextlib import ExitStack

import numpy as np

import concourse.bass as bass
from concourse import mybir

F32 = mybir.dt.float32
R32 = mybir.dt.float32r
I32 = mybir.dt.int32
ACT = mybir.ActivationFunctionType
ALU = mybir.AluOpType
AX = mybir.AxisListType

P = 128
TOK = 1024
IN = 2048
N = 4
D = 512
H = 8
HD = D // H
HALF = 512
HALVES = TOK // HALF
KT = IN // P
DT = D // P
CH = TOK // P
EPS = 1e-5
RING = 4


class Mem:

    def __init__(self, nc, ctx, phase):
        self.nc, self.ctx, self.phase = nc, ctx, phase

    def sb(self, name, shape, dt=F32):
        return self.ctx.enter_context(self.nc.sbuf_tensor(f"{self.phase}_{name}", shape, dt))

    def bank(self, name):
        return self.ctx.enter_context(self.nc.psum_tensor(f"{self.phase}_{name}", [P, 512], F32))

    def sem(self, name):
        return self.ctx.enter_context(self.nc.semaphore(f"{self.phase}_{name}"))


def product(nc, out, a, b, first, last):
    (ah, al), (bh, bl) = a, b
    nc.tensor.matmul(out, ah, bh, start=first, stop=False)
    nc.tensor.matmul(out, ah, bl, start=False, stop=False)
    return nc.tensor.matmul(out, al, bh, start=False, stop=last)


def encoders(nc, xT, w_enc, b1, g1T, be1T, b2T, s_out):
    with ExitStack() as ctx:
        m = Mem(nc, ctx, "enc")
        x_hi = m.sb("x_hi", [P, KT, HALF], R32)
        x_lo = m.sb("x_lo", [P, KT, HALF], R32)
        hid = m.sb("hid", [P, 4, IN])
        act_hi = m.sb("act_hi", [P, KT, HALF], R32)
        act_lo = m.sb("act_lo", [P, KT, HALF], R32)
        act_f = m.sb("act_f", [P, 2, HALF])
        w_raw = m.sb("w_raw", [P, 2, 2, 512])
        w_hi = m.sb("w_hi", [P, RING, 512], R32)
        w_lo = m.sb("w_lo", [P, RING, 512], R32)
        b1_row = m.sb("b1_row", [P, 2, 512])
        s_stage = m.sb("s_stage", [P, 2, HALF])
        ident = m.sb("ident", [P, P])
        stats = m.sb("stats", [P, 4, 4 * 6])
        mean_var = m.sb("mean_var", [P, 4, 2])
        std = m.sb("std", [P, 4])
        rstd = m.sb("rstd", [P, 4])
        gain = m.sb("gain", [P, KT])
        shift = m.sb("shift", [P, KT])
        b2 = m.sb("b2", [P, KT])
        banks = [[m.bank(f"acc{s}{t}") for t in range(4)] for s in range(2)]

        x_landed = [m.sem(f"x_landed{i}") for i in range(4)]
        w_landed = [m.sem(f"w_landed{i}") for i in range(2)]
        b1_landed = [m.sem(f"b1_landed{i}") for i in range(2)]
        c_landed = m.sem("c_landed")
        x_hi_done, x_lo_done = m.sem("x_hi_done"), m.sem("x_lo_done")
        w_hi_done, w_lo_done, w_used = m.sem("w_hi_done"), m.sem("w_lo_done"), m.sem("w_used")
        hid_done, s_done, s_stored = m.sem("hid_done"), m.sem("s_done"), [m.sem(f"s_stored{i}") for i in range(2)]
        ident_ready, var_done, std_done, rstd_done = m.sem("ident_ready"), m.sem("var_done"), m.sem("std_done"), m.sem("rstd_done")
        row_done = m.sem("row_done")
        stat_done, z_done, zt_done, gelu_done = m.sem("stat_done"), m.sem("z_done"), m.sem("zt_done"), m.sem("gelu_done")
        act_hi_done, act_lo_done = m.sem("act_hi_done"), m.sem("act_lo_done")
        block = ctx.enter_context(nc.Block())

        ITEMS = 2 * 4 * KT
        LO0, HID0, S0 = 4, 8, 16

        @block.sync
        def _(sp):
            def load_x(half, rows=range(4)):
                for r in rows:
                    sp.dma_start(hid[:, r, :].rearrange("p (k t) -> p k t", k=4),
                                 xT[bass.ds(half * KT + 4 * r, 4)].rearrange("k p t -> p k t")).then_inc(x_landed[r], 16)

            load_x(0, [0])
            with sp.Fori(0, HALVES) as half:
                with sp.Fori(0, 2) as e:
                    it = half * 2 + e
                    with sp.Fori(0, 2) as c2:
                        for cc in range(2):
                            sp.wait_ge(hid_done, it * 16 + c2 * 8 + (4 * cc + 4))
                            sp.dma_start(b1_row[:, cc, :], b1[bass.ds(e * 4 + c2 * 2 + cc, 1)].rearrange("a j -> (a j)").partition_broadcast(P)).then_inc(b1_landed[cc], 16)
                            for q in range(8):
                                sp.wait_ge(w_lo_done, it * ITEMS + c2 * 32 + (16 * cc + 2 * q + 2))
                                sp.dma_start(w_raw[:, q % 2, :, :], w_enc[bass.ds(e * 64 + c2 * 16 + (8 * cc + q), 1)].rearrange("a p k j -> p (a k) j")).then_inc(w_landed[q % 2], 16)
                    for first, pairs in ((0, 5), (5, 11)):
                        with sp.Fori(first, first + pairs) as q2:
                            for qq in range(2):
                                sp.wait_ge(w_lo_done, it * ITEMS + q2 * 4 + (64 + 2 * qq + 2))
                                sp.dma_start(w_raw[:, qq, :, :], w_enc[bass.ds(e * 64 + q2 * 2 + (32 + qq), 1)].rearrange("a p k j -> p (a k) j")).then_inc(w_landed[qq], 16)
                        if not first:
                            sp.wait_ge(zt_done, it * KT + KT)
                            load_x((half + e) % 2)
            for q in range(2):
                sp.wait_ge(w_lo_done, 4 * ITEMS + 2 * q + 2)
                sp.dma_start(w_raw[:, q, :, :], w_enc[q]).then_inc(w_landed[q], 16)
            for r in range(4):
                sp.wait_ge(x_landed[r], 5 * 16)

        @block.gpsimd
        def _(pool):
            nc.gpsimd.memset(ident[:], 0.0).then_inc(ident_ready, 1)
            pool.wait_ge(ident_ready, 1)
            nc.gpsimd.affine_select(out=ident[:], in_=ident[:], compare_op=ALU.not_equal, fill=1.0, base=0,
                                    pattern=[[-1, P]], channel_multiplier=1).then_inc(ident_ready, 1)
            def high_x(rounds):
                for k in range(KT):
                    if k % 4 == 0:
                        pool.wait_ge(x_landed[k // 4], rounds * 16 + 16)
                        pool.nop(nofuse=True)
                    nc.gpsimd.tensor_copy(x_hi[:, k, :], hid[:, k // 4, 512 * (k % 4):512 * (k % 4) + 512]).then_inc(x_hi_done, 1)

            with pool.Fori(0, HALVES) as half:
                with pool.Fori(0, 2) as e:
                    it = half * 2 + e
                    for k in range(KT):
                        pool.wait_ge(gelu_done, it * KT + (k + 1))
                        pool.nop(nofuse=True)
                        nc.gpsimd.tensor_copy(act_hi[:, k, :], act_f[:, k % 2, :]).then_inc(act_hi_done, 1)
                    high_x(it + 1)

        @block.scalar
        def _(act):
            def high(base, i):
                act.wait_ge(w_used, base + (i + 1))
                if i % 2 == 0:
                    act.wait_ge(w_landed[i // 2 % 2], base * 4 + (i // 4 + 1) * 16)
                nc.scalar.activation(w_hi[:, i % RING, :], w_raw[:, i // 2 % 2, i % 2, :], ACT.Copy).then_inc(w_hi_done, 1)

            act.sem_inc(s_done, S0)
            for i in range(2):
                act.sem_inc(s_stored[i], 16)
            act.dma_start(gain[:], g1T[0]).then_inc(c_landed, 16)
            act.dma_start(shift[:], be1T[0]).then_inc(c_landed, 16)
            act.dma_start(b2[:], b2T[0]).then_inc(c_landed, 16)
            def high_x(k):
                act.wait_ge(x_landed[k // 4], 16)
                nc.scalar.activation(x_hi[:, k, :], hid[:, k // 4, 512 * (k % 4):512 * (k % 4) + 512], ACT.Copy).then_inc(x_hi_done, 1)

            act.wait_ge(x_landed[0], 16)
            for r in range(1, 4):
                act.dma_start(hid[:, r, :].rearrange("p (k t) -> p k t", k=4),
                              xT[4 * r:4 * r + 4].rearrange("k p t -> p k t")).then_inc(x_landed[r], 16)
            for k in range(KT):
                if k < RING:
                    high(0, k)
                high_x(k)
            with act.Fori(0, HALVES) as half:
                with act.Fori(0, 2) as e:
                    it = half * 2 + e
                    base = act.snap(it * ITEMS)
                    with act.Fori(0, 4) as c:
                        gbase = act.snap(base + c * 16)
                        for j in range(RING, 16 + RING):
                            high(gbase, j)
                    act.wait_ge(var_done, it + 1)
                    nc.scalar.activation(std[:], mean_var[:, :, 1], ACT.Sqrt).then_inc(std_done, 1)
                    act.wait_ge(c_landed, it * 48 + 48)
                    for k in range(KT + 2):
                        if k < KT:
                            act.wait_ge(zt_done, it * KT + (k + 1))
                            if k >= 2:
                                act.wait_ge(act_lo_done, it * KT + (k - 1))
                            nc.scalar.activation(act_f[:, k % 2, :], banks[1][k % 4][:], ACT.Gelu,
                                                 bias=shift[:, k:k + 1], scale=gain[:, k:k + 1]).then_inc(gelu_done, 1)
                        if k >= 2:
                            high(base, 64 + RING + k - 2)
                    for n in range(4):
                        if n:
                            for j in range(RING, 16 + RING):
                                if 16 * n + j < 64:
                                    high(base, 64 + 16 * n + j)
                        for f in range(4):
                            r = 4 * n + f
                            if n == 3:
                                high(base, ITEMS + f)
                            act.wait_ge(w_used, base + (64 + 16 * n + 16 + RING))
                            act.wait_ge(s_stored[f % 2], it * (8 * 16) + (r // 2 + 1) * 16)
                            nc.scalar.activation(s_stage[:, f % 2, :], banks[n % 2][f][:], ACT.Identity,
                                                 bias=b2[:, r:r + 1]).then_inc(s_done, 1)
                            act.wait_ge(s_done, it * 16 + (r + 1 + S0))
                            act.dma_start(s_out[bass.ds(half * 4, 4), bass.ds(e, 1), :, f, n, :].rearrange("c e p t -> p (c e) t"),
                                          s_stage[:, f % 2, :].rearrange("p (c t) -> p c t", c=4)).then_inc(s_stored[f % 2], 16)
                    act.wait_ge(s_done, it * 16 + (16 + S0))
                    act.dma_start(gain[:], g1T[bass.ds(1 - e, 1)].rearrange("a p k -> p (a k)")).then_inc(c_landed, 16)
                    act.dma_start(shift[:], be1T[bass.ds(1 - e, 1)].rearrange("a p k -> p (a k)")).then_inc(c_landed, 16)
                    act.dma_start(b2[:], b2T[bass.ds(1 - e, 1)].rearrange("a p k -> p (a k)")).then_inc(c_landed, 16)
            act.wait_ge(c_landed, 5 * 48)
            for i in range(2):
                act.wait_ge(s_stored[i], 4 * 8 * 16 + 16)

        @block.vector
        def _(dve):
            def low(base, i):
                dve.wait_ge(w_hi_done, base + (i + 1))
                nc.vector.tensor_tensor(w_lo[:, i % RING, :], w_raw[:, i // 2 % 2, i % 2, :],
                                        w_hi[:, i % RING, :].bitcast(F32), ALU.subtract).then_inc(w_lo_done, 1)

            dve.sem_inc(w_lo_done, LO0)
            dve.sem_inc(hid_done, HID0)
            def low_x(rounds, k):
                dve.wait_ge(x_hi_done, rounds * KT + (k + 1))
                nc.vector.tensor_tensor(x_lo[:, k, :], hid[:, k // 4, 512 * (k % 4):512 * (k % 4) + 512],
                                        x_hi[:, k, :].bitcast(F32), ALU.subtract).then_inc(x_lo_done, 1)

            AHEAD = 2
            for k in range(KT):
                if k < AHEAD:
                    low(0, k)
                low_x(0, k)
            with dve.Fori(0, HALVES) as half:
                with dve.Fori(0, 2) as e:
                    it = half * 2 + e
                    base = dve.snap(it * ITEMS)
                    with dve.Fori(0, 2) as c2:
                        for cc in range(2):
                            gbase = dve.snap(base + c2 * 32 + 16 * cc)
                            for j in range(AHEAD, 16 + AHEAD):
                                low(gbase, j)
                            dve.wait_ge(b1_landed[cc], it * 32 + c2 * 16 + 16)
                            for t in range(4):
                                if t < 3:
                                    dve.wait_ge(row_done, it * 12 + c2 * 6 + (3 * cc + t + 1))
                                else:
                                    dve.wait_ge(w_used, gbase + (16 + RING))
                                nc.vector.tensor_tensor(hid[:, t, bass.ds(c2 * 1024 + 512 * cc, 512)], banks[cc][t][:],
                                                        b1_row[:, cc, :], ALU.add).then_inc(hid_done, 1)
                                dve.wait_ge(hid_done, it * 16 + c2 * 8 + (4 * cc + t + 1 + HID0))
                                nc.vector.bn_stats(stats[:, t, bass.ds(c2 * 12 + 6 * cc, 6)],
                                                   hid[:, t, bass.ds(c2 * 1024 + 512 * cc, 512)]).then_inc(stat_done, 1)
                    dve.wait_ge(stat_done, it * 20 + 16)
                    dve.nop(nofuse=True)
                    for t in range(4):
                        nc.vector.bn_aggr(mean_var[:, t, :], stats[:, t, :]).then_inc(stat_done, 1)
                    dve.wait_ge(stat_done, it * 20 + 20)
                    nc.vector.tensor_scalar(mean_var[:, :, 1], mean_var[:, :, 1], EPS, None, ALU.add).then_inc(var_done, 1)
                    dve.wait_ge(std_done, it + 1)
                    nc.vector.reciprocal(rstd[:], std[:]).then_inc(rstd_done, 1)
                    dve.wait_ge(rstd_done, it + 1)

                    def normalise(first, last):
                        for t in range(4):
                            nc.vector.tensor_scalar(hid[:, t, first:last], hid[:, t, first:last], mean_var[:, t, 0:1],
                                                    rstd[:, t:t + 1], ALU.subtract, ALU.mult).then_inc(z_done, 1)
                    normalise(0, P)
                    normalise(P, 512)
                    for i in range(AHEAD, RING):
                        low(base, 64 + i)
                    normalise(512, 1024)
                    for k in range(KT + 2):
                        if k < KT:
                            dve.wait_ge(act_hi_done, it * KT + (k + 1))
                            nc.vector.tensor_tensor(act_lo[:, k, :], act_f[:, k % 2, :], act_hi[:, k, :].bitcast(F32),
                                                    ALU.subtract).then_inc(act_lo_done, 1)
                        if k in (1, 5):
                            normalise(1024 + k // 4 * 512, 1536 + k // 4 * 512)
                        if k >= 2:
                            low(base, 64 + RING + k - 2)
                    for n in range(1, 4):
                        for j in range(RING, 16 + RING):
                            if 16 * n + j < 64:
                                low(base, 64 + 16 * n + j)
                            if n == 2:
                                low_x(it + 1, j - RING)
                    for i in range(AHEAD):
                        low(base, ITEMS + i)

        @block.tensor
        def _(pe):
            pe.sem_inc(w_used, RING)
            pe.wait_ge(ident_ready, 2)
            with pe.Fori(0, HALVES) as half:
                with pe.Fori(0, 2) as e:
                    it = half * 2 + e
                    base = pe.snap(it * ITEMS)
                    with pe.Fori(0, 2) as c2:
                        for cc in range(2):
                            pe.wait_ge(hid_done, it * 16 + c2 * 8 + (4 * cc + 4))
                            pe.wait_ge(s_done, it * 16 + (12 + 4 * cc))

                            def row(k, t):
                                s = slice(P * t, P * t + P)
                                return product(nc, banks[cc][t][:], (x_hi[:, k, s], x_lo[:, k, s]),
                                               (w_hi[:, k % RING, :], w_lo[:, k % RING, :]), k == 0, k == KT - 1)

                            for k in range(KT):
                                pe.wait_ge(x_lo_done, it * KT + (k + 1))
                                pe.wait_ge(w_lo_done, base + c2 * 32 + (16 * cc + k + 1 + LO0))
                                if k < KT - 2:
                                    for t in range(4):
                                        mm = row(k, t)
                                    mm.then_inc(w_used, 1)
                            for t in range(4):
                                mm = row(KT - 2, t)
                                if t == 3:
                                    mm.then_inc(w_used, 1)
                                row(KT - 1, t).then_inc(row_done if t < 3 else w_used, 1)

                    def turn(k):
                        pe.wait_ge(z_done, it * 20 + (k // 4 * 4 + (8 if k else 4)))
                        if k >= 4:
                            pe.wait_ge(gelu_done, it * KT + (k - 3))
                        for t in range(4):
                            mm = nc.tensor.transpose(banks[1][k % 4][:, P * t:P * t + P], hid[:, t, P * k:P * k + P], ident[:])
                        mm.then_inc(zt_done, 1)

                    for n in range(4):
                        if n == 0:
                            for k in range(3):
                                turn(k)
                            pe.wait_ge(hid_done, it * 16 + (12 + HID0))
                        elif n == 1:
                            pe.wait_ge(gelu_done, it * KT + KT)
                        else:
                            pe.wait_ge(s_done, it * 16 + (4 * n - 4 + S0))
                        for k in range(KT):
                            pe.wait_ge(w_lo_done, base + (64 + 16 * n + k + 1 + LO0))
                            if n == 0:
                                pe.wait_ge(act_lo_done, it * KT + (k + 1))
                            a = (act_hi[:, k, :], act_lo[:, k, :])
                            for f in range(4):
                                s = slice(P * f, P * f + P)
                                mm = product(nc, banks[n % 2][f][:], (w_hi[:, k % RING, s], w_lo[:, k % RING, s]), a,
                                             k == 0, k == KT - 1)
                            mm.then_inc(w_used, 1)
                            if n == 0 and k + 3 < KT:
                                turn(k + 3)


def projections(nc, s_in, w_qkv, b_qkvT, b_v, qkv_out):
    with ExitStack() as ctx:
        m = Mem(nc, ctx, "proj")
        MATS = 6
        w_hi = m.sb("w_hi", [P, MATS, DT, 512], R32)
        w_lo = m.sb("w_lo", [P, MATS, DT, 512], R32)
        s_raw = m.sb("s_raw", [P, 2, DT, 512])
        s_hi = m.sb("s_hi", [P, 2, 2, DT, 512], R32)
        s_lo = m.sb("s_lo", [P, 2, 2, DT, 512], R32)
        stage_a = m.sb("stage_a", [P, DT, 512])
        stage_d = m.sb("stage_d", [P, DT, 512])
        b_col = m.sb("b_col", [P, 4, DT])
        bv_row = m.sb("bv_row", [P, 2, 512])
        banks = [[m.bank(f"acc{s}{t}") for t in range(4)] for s in range(2)]

        b_landed = m.sem("b_landed")
        w_landed = [m.sem(f"w_landed{i}") for i in range(2)]
        s_landed = [m.sem(f"s_landed{i}") for i in range(2)]
        w_hi_done, w_lo_done = m.sem("w_hi_done"), m.sem("w_lo_done")
        s_hi_done, s_lo_done = m.sem("s_hi_done"), m.sem("s_lo_done")
        mm_done, act_out, dve_out, neg_out = m.sem("mm_done"), m.sem("act_out"), m.sem("dve_out"), m.sem("neg_out")
        act_stored, dve_stored = m.sem("act_stored"), m.sem("dve_stored")
        block = ctx.enter_context(nc.Block())

        def by_group(x):
            return x.rearrange("p (n g t) -> p g n t", n=N, g=4)

        def grouped(x, buf, comp, k):
            return x[:, buf, comp, k, :].rearrange("p (g n t) -> p g n t", n=N, g=4)

        AO, DO, SL, ST, MM = 8, 16, 2, 16, 6

        @block.sync
        def _(sp):
            sp.dma_start(b_col[:], b_qkvT).then_inc(b_landed, 16)
            sp.dma_start(bv_row[:], b_v.partition_broadcast(P)).then_inc(b_landed, 16)

            def load_s(c):
                for comp in range(2):
                    sp.wait_ge(s_lo_done, c * 2 + (comp + 1))
                    sp.dma_start(s_raw[:, comp, :, :].rearrange("p k (n t) -> p k n t", n=N),
                                 s_in[bass.ds(c % CH, 1), comp].rearrange("a p k n t -> p (a k) n t")).then_inc(s_landed[comp], 16)

            for mat in range(MATS):
                if mat >= 2:
                    sp.wait_ge(w_lo_done, mat - 1)
                sp.dma_start((stage_a, stage_d)[mat % 2][:], w_qkv[mat]).then_inc(w_landed[mat % 2], 16)
                if mat == 0:
                    load_s(0)
            with sp.Fori(0, CH) as c:
                load_s(c + 1)
                for g in range(4):
                    sp.wait_ge(dve_out, c * 16 + (4 * g + 4 + DO))
                    sp.dma_start(qkv_out[bass.ds(c, 1), 2 + g].rearrange("a p k j -> p (a k) j"), stage_d[:]).then_inc(dve_stored, 16)
            sp.wait_ge(dve_stored, CH * 4 * 16 + ST)
            for comp in range(2):
                sp.wait_ge(s_landed[comp], (CH + 1) * 16)

        @block.scalar
        def _(act):
            act.sem_inc(act_out, AO)
            act.sem_inc(act_stored, ST)

            def high_s(c, buf):
                for comp in range(2):
                    act.wait_ge(s_landed[comp], c * 16 + 16)
                    for k in range(DT):
                        ins = nc.scalar.activation(grouped(s_hi, buf, comp, k), by_group(s_raw[:, comp, k, :]), ACT.Copy)
                    ins.then_inc(s_hi_done, 1)

            def high_w(mat):
                act.wait_ge(w_landed[mat % 2], 16 * (mat // 2 + 1))
                nc.scalar.activation(w_hi[:, mat, :, :], (stage_a, stage_d)[mat % 2][:], ACT.Copy).then_inc(w_hi_done, 1)

            high_w(0)
            high_s(0, 0)
            for mat in range(1, MATS):
                high_w(mat)
            act.wait_ge(b_landed, 32)
            act.wait_ge(w_lo_done, MATS)
            with act.Fori(0, CH // 2) as c2:
                for u in range(2):
                    c = act.snap(c2 * 2 + u)
                    act.wait_ge(mm_done, c * 6 + MM)
                    high_s(c + 1, 1 - u)
                    for g in range(2):
                        act.wait_ge(mm_done, c * 6 + (g + 1 + MM))
                        act.wait_ge(act_stored, c * 48 + (16 * g + ST))
                        for f in range(4):
                            nc.scalar.activation(stage_a[:, f, :], banks[g][f][:], ACT.Identity,
                                                 bias=b_col[:, g, f:f + 1]).then_inc(act_out, 1)
                        act.wait_ge(act_out, c * 8 + (4 * g + 4 + AO))
                        act.dma_start(qkv_out[bass.ds(c, 1), g].rearrange("a p k j -> p (a k) j"), stage_a[:]).then_inc(act_stored, 16)
                    act.wait_ge(dve_out, c * 16 + (8 + DO))
                    act.wait_ge(act_stored, c * 48 + (32 + ST))
                    nc.scalar.activation(stage_a[:], stage_d[:], ACT.Copy, scale=-1.0).then_inc(neg_out, 1)
                    act.wait_ge(neg_out, c + 1)
                    act.dma_start(qkv_out[bass.ds(c, 1), 6].rearrange("a p k j -> p (a k) j"), stage_a[:]).then_inc(act_stored, 16)
            act.wait_ge(act_stored, CH * 48 + ST)

        @block.vector
        def _(dve):
            dve.sem_inc(s_lo_done, SL)
            dve.sem_inc(dve_out, DO)
            dve.sem_inc(dve_stored, ST)

            def low_s(c, buf):
                for comp in range(2):
                    dve.wait_ge(s_hi_done, c * 2 + (comp + 1))
                    for k in range(DT):
                        ins = nc.vector.tensor_tensor(grouped(s_lo, buf, comp, k), by_group(s_raw[:, comp, k, :]),
                                                      grouped(s_hi, buf, comp, k).bitcast(F32), ALU.subtract)
                    ins.then_inc(s_lo_done, 1)

            def low_w(mat):
                dve.wait_ge(w_hi_done, mat + 1)
                nc.vector.tensor_tensor(w_lo[:, mat, :, :], (stage_a, stage_d)[mat % 2][:],
                                        w_hi[:, mat, :, :].bitcast(F32), ALU.subtract).then_inc(w_lo_done, 1)

            low_w(0)
            low_s(0, 0)
            for mat in range(1, MATS):
                low_w(mat)
            dve.wait_ge(b_landed, 32)
            with dve.Fori(0, CH // 2) as c2:
                for u in range(2):
                    c = dve.snap(c2 * 2 + u)
                    for g in range(4):
                        dve.wait_ge(mm_done, c * 6 + (g + 3 + MM))
                        dve.wait_ge(dve_stored, c * 64 + (16 * g + ST))
                        if g == 2:
                            dve.wait_ge(neg_out, c + 1)
                        for f in range(4):
                            if g < 2:
                                nc.vector.tensor_scalar(stage_d[:, f, :], banks[g % 2][f][:], b_col[:, 2 + g, f:f + 1], None,
                                                        ALU.add).then_inc(dve_out, 1)
                            else:
                                nc.vector.tensor_tensor(stage_d[:, f, :], banks[g % 2][f][:], bv_row[:, g - 2, :],
                                                        ALU.add).then_inc(dve_out, 1)
                        if g == 1:
                            low_s(c + 1, 1 - u)

        @block.tensor
        def _(pe):
            pe.sem_inc(mm_done, MM)
            with pe.Fori(0, CH // 2) as c2:
                for u in range(2):
                    c = pe.snap(c2 * 2 + u)
                    for g in range(6):
                        if g in (2, 3):
                            pe.wait_ge(act_out, c * 8 + (4 * g - 4 + AO))
                        else:
                            pe.wait_ge(dve_out, c * 16 + {0: 12, 1: 16, 4: 4 + DO, 5: 8 + DO}[g])
                        if u == 0:
                            pe.wait_ge(w_lo_done, g + 1)
                        comp = g % 2
                        pe.wait_ge(s_lo_done, c * 2 + (comp + 1 + SL))
                        for k in range(DT):
                            for t in range(4):
                                s = slice(P * t, P * t + P)
                                if g < 4:
                                    a = (w_hi[:, g, k, s], w_lo[:, g, k, s])
                                    b = (s_hi[:, u, comp, k, :], s_lo[:, u, comp, k, :])
                                else:
                                    a = (s_hi[:, u, comp, k, s], s_lo[:, u, comp, k, s])
                                    b = (w_hi[:, g, k, :], w_lo[:, g, k, :])
                                mm = product(nc, banks[g % 2][t][:], a, b, k == 0, k == DT - 1)
                        mm.then_inc(mm_done, 1)


def attention(nc, qkv_in, w_o, b_oT, attn_out):
    with ExitStack() as ctx:
        m = Mem(nc, ctx, "attn")
        G = P // 32
        SCALE = float(HD) ** -0.5
        w_hi = m.sb("w_hi", [P, 2, DT, 512], R32)
        w_lo = m.sb("w_lo", [P, 2, DT, 512], R32)
        q = m.sb("q", [P, H, 512])
        kk = m.sb("kk", [P, H, 2, 512])
        v = m.sb("v", [P, G, H, 2, HD])
        o_hi = m.sb("o_hi", [P, 2, DT, 512], R32)
        o_lo = m.sb("o_lo", [P, 2, DT, 512], R32)
        stage = m.sb("stage", [P, 2, DT, 512])
        masked = m.sb("masked", [P, 2, 512])
        mask = m.sb("mask", [P, 32])
        score = m.sb("score", [P, H * G * 8])
        square = m.sb("square", [P, H * G * 8])
        mag = m.sb("mag", [P, H * G, N])
        top = m.sb("top", [P, H * G])
        total = m.sb("total", [P, H * G])
        weight = m.sb("weight", [P, H * G, N])
        turned = m.sb("turned", [P, H * G, N])
        spread = m.sb("spread", [P, 8, 512])
        b_col = m.sb("b_col", [P, 2, DT])
        banks = [m.bank(f"bank{i}") for i in range(8)]

        b_landed, w_landed = m.sem("b_landed"), m.sem("w_landed")
        q_landed, v_landed = [m.sem(f"q_landed{i}") for i in range(2)], m.sem("v_landed")
        w_hi_done, w_lo_done, mask_done = m.sem("w_hi_done"), m.sem("w_lo_done"), m.sem("mask_done")
        pair_done, masked_done, score_done = m.sem("pair_done"), m.sem("masked_done"), m.sem("score_done")
        step, mag_done, exp_done, turned_done = m.sem("step"), m.sem("mag_done"), m.sem("exp_done"), m.sem("turned_done")
        sum_done = m.sem("sum_done")
        spread_low, spread_high, av_done, o_hi_done, o_lo_done = m.sem("spread_low"), m.sem("spread_high"), m.sem("av_done"), m.sem("o_hi_done"), m.sem("o_lo_done")
        wo_done, out_done = m.sem("wo_done"), m.sem("out_done")
        stored = [m.sem(f"stored{i}") for i in range(2)]
        block = ctx.enter_context(nc.Block())

        HEADS = [0, 2, 4, 6, 1, 3, 5, 7]
        STEPS = 6
        OD, ST = 8, 16

        @block.sync
        def _(sp):
            sp.dma_start(b_col[:], b_oT).then_inc(b_landed, 16)

            def rows(c, kind, half):
                return qkv_in[bass.ds(c, 1), kind, 64 * half:64 * half + 64].rearrange("a p f j -> p (a f) j")

            def load(c, waits):
                if waits:
                    sp.wait_ge(pair_done, c * 16)
                for half in range(2):
                    for comp in range(2):
                        part = slice(64 * comp, 64 * comp + 64)
                        sp.dma_start(q[part, half::2, :], rows(c, comp, half)).then_inc(q_landed[half], 16)
                        sp.dma_start(kk[part, half::2, 0, :], rows(c, 2 + comp, half)).then_inc(q_landed[half], 16)
                        sp.dma_start(kk[part, half::2, 1, :], rows(c, (6, 2)[comp], half)).then_inc(q_landed[half], 16)
                if waits:
                    sp.wait_ge(av_done, c * 8)
                for comp in range(2):
                    sp.dma_start(v[:, :, :, comp, :].rearrange("p g h d -> p (g h) d"),
                                 qkv_in[bass.ds(c, 1), 4 + comp].rearrange("a p g (h d) -> p (a g h) d", h=H)).then_inc(v_landed, 16)

            load(0, False)
            for mat in range(2):
                sp.dma_start(stage[:, mat, :, :], w_o[mat]).then_inc(w_landed, 16)
            with sp.Fori(1, CH) as c:
                load(c, True)

        def chunks(eng, first, rest, tail=None):
            first(0)
            with eng.Fori(1, CH) as c:
                rest(c)
            if tail:
                tail()

        def spread_heads(eng, hh, g):
            w = turned[:].rearrange("p (h g) n -> p h g n", g=G)[:, 4 * hh:4 * hh + 4, g, :]
            for j in range(4):
                ins = eng.tensor_tensor(spread[:, 4 * hh + g, P * j:P * j + P].rearrange("p (n t) -> p n t", n=N),
                                        w[:, j, :].unsqueeze(2).to_broadcast([P, N, 32]),
                                        mask[:].unsqueeze(1).to_broadcast([P, N, 32]), ALU.mult)
            return ins

        @block.gpsimd
        def _(pool):
            nc.gpsimd.memset(mask[:], 0.0).then_inc(mask_done, 1)
            pool.wait_ge(mask_done, 1)
            for n in range(N):
                if n:
                    pool.wait_ge(mask_done, n + 1)
                nc.gpsimd.affine_select(out=mask[:], in_=mask[:], compare_op=ALU.not_equal, fill=1.0, base=-32 * n,
                                        pattern=[[-1, 32]], channel_multiplier=1).then_inc(mask_done, 1)
            pool.wait_ge(mask_done, 5)

            def spread_out(c):
                pool.wait_ge(turned_done, (c + 1) * 16)
                for g in range(G):
                    spread_heads(nc.gpsimd, 1, g).then_inc(spread_high, 1)

            chunks(pool, spread_out, spread_out)

        @block.scalar
        def _(act):
            act.sem_inc(out_done, OD)
            for comp in range(2):
                act.sem_inc(stored[comp], ST)

            def magnitudes(c):
                act.wait_ge(step, c * STEPS + 2)
                nc.scalar.activation(mag[:], mag[:], ACT.Sqrt).then_inc(mag_done, 1)
                act.wait_ge(step, c * STEPS + 4)
                nc.scalar.activation(weight[:], mag[:], ACT.Exp, scale=SCALE).then_inc(exp_done, 1)

            def values(c):
                for h in range(H):
                    act.wait_ge(av_done, c * 8 + (h + 1))
                    for comp in range(2):
                        part, to = slice(64 * comp, 64 * comp + 64), slice(64 * (h % 2), 64 * (h % 2) + 64)
                        nc.scalar.activation(o_hi[to, comp, h // 2, :], banks[4 + h % 4][part, :], ACT.Copy).then_inc(o_hi_done, 1)

            def outputs(c):
                for comp in range(2):
                    act.wait_ge(wo_done, c * 2 + (comp + 1))
                    act.wait_ge(stored[comp], c * 16 + ST)
                    for f in range(4):
                        nc.scalar.activation(stage[:, comp, f, :].rearrange("p (n g t) -> p n g t", n=N, g=G),
                                             banks[4 - 4 * comp + f][:].rearrange("p (g n t) -> p n g t", n=N, g=G), ACT.Identity,
                                             bias=b_col[:, comp, f:f + 1]).then_inc(out_done, 1)
                    act.wait_ge(out_done, c * 8 + (4 * comp + 4 + OD))
                    act.dma_start(attn_out[bass.ds(c, 1), comp].rearrange("a p f j -> p (a f) j"),
                                  stage[:, comp, :, :]).then_inc(stored[comp], 16)

            def first(c):
                magnitudes(c)
                for mat in range(2):
                    act.wait_ge(w_landed, 32)
                    nc.scalar.activation(w_hi[:, mat, :, :], stage[:, mat, :, :], ACT.Copy).then_inc(w_hi_done, 1)
                act.wait_ge(b_landed, 16)
                values(c)
                act.wait_ge(w_lo_done, 2)

            def rest(c):
                magnitudes(c)
                outputs(c - 1)
                values(c)

            chunks(act, first, rest, lambda: outputs(CH - 1))
            for comp in range(2):
                act.wait_ge(stored[comp], CH * 16 + ST)

        @block.vector
        def _(dve):
            dve.wait_ge(mask_done, 5)

            def scores(c):
                for i in range(16):
                    dve.wait_ge(pair_done, c * 16 + (i + 1))
                    nc.vector.tensor_tensor(masked[:, i % 2, :].rearrange("p (a t) -> p a t", t=32),
                                            banks[i % 4][:].rearrange("p (a t) -> p a t", t=32),
                                            mask[:].unsqueeze(1).to_broadcast([P, 16, 32]), ALU.mult).then_inc(masked_done, 1)
                    dve.wait_ge(masked_done, c * 16 + (i + 1))
                    at = 16 * (2 * HEADS[i // 2] + i % 2)
                    nc.vector.tensor_reduce(score[:, at:at + 16], masked[:, i % 2, :].rearrange("p (a t) -> p a t", t=32),
                                            AX.X, ALU.add).then_inc(score_done, 1)

            def softmax(c):
                b = c * STEPS
                dve.wait_ge(score_done, c * 16 + 16)
                nc.vector.tensor_tensor(square[:], score[:], score[:], ALU.mult).then_inc(step, 1)
                dve.wait_ge(step, b + 1)
                parts = square[:].rearrange("p (a w n) -> p a w n", w=2, n=N)
                nc.vector.scalar_tensor_tensor(out=mag[:], in0=parts[:, :, 0, :], scalar=1e-8, in1=parts[:, :, 1, :],
                                               op0=ALU.add, op1=ALU.add).then_inc(step, 1)
                dve.wait_ge(mag_done, c + 1)
                nc.vector.tensor_reduce(top[:], mag[:], AX.X, ALU.max).then_inc(step, 1)
                dve.wait_ge(step, b + 3)
                nc.vector.tensor_tensor(mag[:], mag[:], top[:].unsqueeze(2).to_broadcast([P, H * G, N]),
                                        ALU.subtract).then_inc(step, 1)
                dve.wait_ge(exp_done, c + 1)
                nc.vector.tensor_reduce(total[:], weight[:], AX.X, ALU.add).then_inc(sum_done, 1)
                dve.wait_ge(sum_done, c + 1)
                nc.vector.reciprocal(total[:], total[:]).then_inc(step, 1)
                dve.wait_ge(step, b + 5)
                nc.vector.tensor_tensor(weight[:], weight[:], total[:].unsqueeze(2).to_broadcast([P, H * G, N]),
                                        ALU.mult).then_inc(step, 1)
                dve.wait_ge(step, b + 6)
                for n in range(N):
                    for k in range(N):
                        nc.vector.tensor_copy(turned[32 * k:32 * k + 32, :, n], weight[32 * n:32 * n + 32, :, k]).then_inc(turned_done, 1)
                dve.wait_ge(turned_done, (c + 1) * 16)
                for g in range(G):
                    spread_heads(nc.vector, 0, g).then_inc(spread_low, 1)

            def values(c):
                for h in range(H):
                    for comp in range(2):
                        dve.wait_ge(o_hi_done, c * 16 + (2 * h + comp + 1))
                        part, to = slice(64 * comp, 64 * comp + 64), slice(64 * (h % 2), 64 * (h % 2) + 64)
                        nc.vector.tensor_tensor(o_lo[to, comp, h // 2, :], banks[4 + h % 4][part, :],
                                                o_hi[to, comp, h // 2, :].bitcast(F32), ALU.subtract).then_inc(o_lo_done, 1)

            def whole(c):
                scores(c)
                softmax(c)
                values(c)

            def first(c):
                scores(c)
                softmax(c)
                for mat in range(2):
                    dve.wait_ge(w_hi_done, mat + 1)
                    nc.vector.tensor_tensor(w_lo[:, mat, :, :], stage[:, mat, :, :], w_hi[:, mat, :, :].bitcast(F32),
                                            ALU.subtract).then_inc(w_lo_done, 1)
                values(c)

            chunks(dve, first, whole)

        @block.tensor
        def _(pe):
            def scores(c, between):
                for i in range(16):
                    h, pair = HEADS[i // 2], i % 2
                    if i % 8 == 0:
                        pe.wait_ge(q_landed[h % 2], (c + 1) * (6 * 16))
                    if i >= 4 or type(c) is not int:
                        pe.wait_ge(masked_done, c * 16 + (i - 3))
                    if i == 0:
                        pe.wait_ge(out_done, c * 8)
                    for gi in range(2):
                        s = slice(P * (2 * pair + gi), P * (2 * pair + gi) + P)
                        mm = nc.tensor.matmul(banks[i % 4][:, 256 * gi:256 * gi + 256].rearrange("p (w r) -> p w r", w=2),
                                              q[:, h, s], kk[:, h, :, s], start=True, stop=True)
                    mm.then_inc(pair_done, 1)
                    between(i)

            def values(c):
                pe.wait_ge(v_landed, (c + 1) * 32)
                if type(c) is not int:
                    pe.wait_ge(out_done, c * 8 + 4)
                for hh, spread_done in enumerate((spread_low, spread_high)):
                    for g in range(G):
                        pe.wait_ge(spread_done, c * G + (g + 1))
                        for j in range(4):
                            h = 4 * hh + j
                            if hh and not g:
                                pe.wait_ge(o_lo_done, c * 16 + (2 * j + 2))
                            mm = nc.tensor.matmul(banks[4 + j][:, P * g:P * g + P], v[:, g, h, :, :].rearrange("p w d -> p (w d)"),
                                                  spread[:, 4 * hh + g, P * j:P * j + P], start=True, stop=True)
                            if g == G - 1:
                                mm.then_inc(av_done, 1)

            def output(c, comp, k, f):
                if not comp and not k:
                    pe.wait_ge(o_lo_done, c * 16 + (2 * (4 + f) + 2))
                s = slice(P * f, P * f + P)
                mm = product(nc, banks[4 - 4 * comp + f][:], (w_hi[:, comp, k, s], w_lo[:, comp, k, s]),
                             (o_hi[:, comp, k, :], o_lo[:, comp, k, :]), k == 0, k == DT - 1)
                if (k, f) == (DT - 1, 3):
                    mm.then_inc(wo_done, 1)

            def outputs(c, comp):
                if comp:
                    pe.wait_ge(masked_done, CH * 16 if type(c) is int else (c + 2) * 16)
                for k in range(DT):
                    for f in range(4):
                        output(c, comp, k, f)

            def first(c):
                scores(c, lambda i: None)
                values(c)
                pe.wait_ge(w_lo_done, 2)

            def rest(c):
                def between(i):
                    for at in range(16):
                        if 4 + at * 12 // 16 == i:
                            output(c - 1, 0, at // 4, at % 4)

                scores(c, between)
                outputs(c - 1, 1)
                values(c)

            def tail():
                outputs(CH - 1, 0)
                outputs(CH - 1, 1)

            chunks(pe, first, rest, tail)


def superposition(nc, attn_in, w_int, ids, tables, sup_out):
    with ExitStack() as ctx:
        m = Mem(nc, ctx, "sup")
        W = D // N
        w_hi = m.sb("w_hi", [P, 2 * N, DT, 512], R32)
        w_lo = m.sb("w_lo", [P, 2 * N, DT, 512], R32)
        a_raw = m.sb("a_raw", [P, 2, 2, DT, P])
        a_hi = m.sb("a_hi", [P, 2, 2, DT, P], R32)
        a_lo = m.sb("a_lo", [P, 2, 2, DT, P], R32)
        ri = m.sb("ri", [P, 2, N, 2, 512])
        part = m.sb("part", [P, 512])
        mag = m.sb("mag", [P, 2, N, W])
        u = m.sb("u", [P, 2, N, W])
        cos = m.sb("cos", [P, 6, W])
        cos_i = m.sb("cos_i", [P, 6, W])
        g = m.sb("g", [P, N, W])
        sup = m.sb("sup", [P, 2, 512])
        index = m.sb("index", [P, CH, N], I32)
        strengths = m.sb("strengths", [P, CH, N, N])
        strength = m.sb("strength", [P, N, N])
        norm = m.sb("norm", [P, 3])
        eps = m.sb("eps", [P, 1])
        banks = [m.bank(f"bank{i}") for i in range(6)]

        index_landed, strengths_landed = m.sem("index_landed"), m.sem("strengths_landed")
        w_landed = [m.sem(f"w_landed{i}") for i in range(4)]
        a_landed = [m.sem(f"a_landed{i}") for i in range(2)]
        w_hi_done, w_lo_done, a_hi_done, a_lo_done = m.sem("w_hi_done"), m.sem("w_lo_done"), m.sem("a_hi_done"), m.sem("a_lo_done")
        mm_done, part_done, i_out, r_out = m.sem("mm_done"), m.sem("part_done"), m.sem("i_out"), m.sem("r_out")
        sq_done, m2_done, mag_done, inv_done = m.sem("sq_done"), m.sem("m2_done"), m.sem("mag_done"), m.sem("inv_done")
        unit_r, unit_i, cos_r_done, cos_i_done = m.sem("unit_r"), m.sem("unit_i"), m.sem("cos_r_done"), m.sem("cos_i_done")
        cos_sum, cos_done, strength_done = m.sem("cos_sum"), m.sem("cos_done"), m.sem("strength_done")
        g_begun, g_step, r_step, i_step = m.sem("g_begun"), m.sem("g_step"), m.sem("r_step"), m.sem("i_step")
        eps_set, norm_sum, norm_root, norm_done, sup_done = (m.sem(x) for x in (
            "eps_set", "norm_sum", "norm_root", "norm_done", "sup_done"))
        stored = m.sem("stored")
        block = ctx.enter_context(nc.Block())
        MM, OUT, STEP, UNIT, SUM, ST = 3, 2, 3, 2, 2, 16

        PAIRS = [(0, 1), (1, 2), (2, 3), (0, 2), (1, 3), (0, 3)]
        OTHERS = [(1, 2, 3), (0, 2, 3), (1, 0, 3), (2, 0, 1)]

        def pair(i, j):
            return cos[:, PAIRS.index((min(i, j), max(i, j))), :]

        def products(eng, out, x):
            eng.tensor_tensor(out[:, 0:3], x[:, 0:3], x[:, 1:4], ALU.mult)
            eng.tensor_tensor(out[:, 3:5], x[:, 0:2], x[:, 2:4], ALU.mult)
            return eng.tensor_tensor(out[:, 5:6], x[:, 0:1], x[:, 3:4], ALU.mult)

        def units(eng, unit, magnitude, quarter):
            def work(c, par, n, known):
                def do():
                    if n == 0:
                        if known >= 2:
                            quarter(c - 2, par, N - 1, magnitude, c - 1)
                        elif known == 1:
                            magnitude(c - 1, 1 - par, 0)
                    elif known >= 1:
                        quarter(c - 1, 1 - par, n - 1, magnitude, c - 1)
                return do

            for c in (0, 1):
                for n in range(N):
                    unit(c, c, n, work(c, c, n, c))
            with eng.Fori(1, CH // 2) as c2:
                for par in (0, 1):
                    c = eng.snap(c2 * 2 + par)
                    for n in range(N):
                        unit(c, par, n, work(c, par, n, 2))
            for n in range(N):
                work(CH, 0, n, 2)()
            quarter(CH - 1, 1, N - 1, None, None)

        def slot(mat):
            return ri[:, mat // 2 % 2, 2 * (mat % 2):2 * (mat % 2) + 2].rearrange("p n w j -> p (n w j)")

        @block.sync
        def _(sp):
            def load_a(c, n):
                for comp in range(2):
                    sp.dma_start(a_raw[:, n % 2, comp], attn_in[bass.ds(c, 1), comp, :, :, P * n:P * n + P].rearrange("a p f t -> p (a f) t")
                                 ).then_inc(a_landed[n % 2], 16)

            def load_w(mat):
                sp.dma_start(slot(mat), w_int[mat]).then_inc(w_landed[mat % 4], 16)

            load_a(0, 0)
            for mat in range(4):
                load_w(mat)
            load_a(0, 1)
            sp.dma_start(index[:], ids).then_inc(index_landed, 16)
            for mat in range(4, 8):
                sp.wait_ge(w_lo_done, mat - 3)
                load_w(mat)
            with sp.Fori(0, CH) as c:
                for n in range(N):
                    sp.wait_ge(a_lo_done, c * N + (n + 1))
                    load_a(c if n < 2 else (c + 1) % CH, (n + 2) % N)
            for s in range(2):
                sp.wait_ge(a_landed[s], (CH * 2 + 1) * 32)

        @block.gpsimd
        def _(pool):
            def low_a(c, n):
                pool.wait_ge(a_hi_done, c * N + (n + 1))
                nc.gpsimd.tensor_tensor(a_lo[:, n % 2], a_raw[:, n % 2], a_hi[:, n % 2].bitcast(F32),
                                        ALU.subtract).then_inc(a_lo_done, 1)

            def magnitude(c, par, q):
                pool.wait_ge(sq_done, c * N + (q + 1))
                nc.gpsimd.tensor_tensor(mag[:, q % 2], mag[:, q % 2], u[:, 1], ALU.add).then_inc(m2_done, 1)

            def quarter(c, par, q, magnitude, of):
                s = c * N + q
                ci = ri[:, par, :, 1, W * q:W * q + W]
                if magnitude:
                    magnitude(of, None, (q + 1) % N)
                    pool.wait_ge(m2_done, s + 2)
                pool.wait_ge(inv_done, s + 1)
                nc.gpsimd.tensor_tensor(u[:, 1], ci, mag[:, q % 2], ALU.mult).then_inc(unit_i, 1)
                pool.wait_ge(unit_i, s + (1 + UNIT))
                pool.wait_ge(cos_sum, s * 2 + SUM)
                products(nc.gpsimd, cos_i, u[:, 1]).then_inc(cos_i_done, 1)
                if due_low:
                    low_a(*due_low.pop())
                pool.wait_ge(g_step, s * 8 + 8)
                nc.gpsimd.tensor_tensor(ci, ci, g[:], ALU.mult).then_inc(i_step, 1)
                pool.wait_ge(i_step, s * 3 + (STEP + 1))
                nc.gpsimd.tensor_tensor(ci[:, 0:2], ci[:, 0:2], ci[:, 2:4], ALU.add).then_inc(i_step, 1)
                pool.wait_ge(i_step, s * 3 + (STEP + 2))
                if q == 0:
                    pool.wait_ge(stored, c * 16 + ST)
                nc.gpsimd.tensor_tensor(sup[:, 1, W * q:W * q + W], ci[:, 0, :], ci[:, 1, :], ALU.add).then_inc(i_step, 1)

            due_low = []

            def unit(c, par, n, work):
                if type(c) is not int or c:
                    due_low.append((c + (n + 1) // N, (n + 1) % N))
                work()
                if due_low:
                    low_a(*due_low.pop())

            pool.sem_inc(i_step, STEP)
            pool.sem_inc(unit_i, UNIT)
            pool.sem_inc(cos_i_done, 1)
            nc.gpsimd.memset(eps[:], 1e-8).then_inc(eps_set, 1)
            pool.wait_ge(index_landed, 16)
            for c in range(CH):
                for f in range(N):
                    nc.gpsimd.indirect_dma_start(out=strengths[:, c, f, :], out_offset=None, in_=tables[f],
                                                 in_offset=bass.IndirectOffsetOnAxis(ap=index[:, c, f:f + 1], axis=0)
                                                 ).then_inc(strengths_landed, 16)
            units(pool, unit, magnitude, quarter)

        @block.scalar
        def _(act):
            act.sem_inc(i_out, OUT)
            act.sem_inc(stored, ST)

            def high_a(c, n):
                act.wait_ge(a_landed[n % 2], c * 64 + 32 * (n // 2 + 1))
                act.wait_ge(mm_done, c * 12 + (3 * n - 3 + MM))
                nc.scalar.activation(a_hi[:, n % 2], a_raw[:, n % 2], ACT.Copy).then_inc(a_hi_done, 1)

            def high_w(mat):
                act.wait_ge(w_landed[mat % 4], 16 * (mat // 4 + 1))
                nc.scalar.activation(w_hi[:, mat, :, :].rearrange("p k j -> p (k j)"), slot(mat), ACT.Copy).then_inc(w_hi_done, 1)

            def magnitude(c, par, q):
                s, cols = c * N + q, slice(W * q, W * q + W)
                if q == 0:
                    act.wait_ge(r_out, c * 4 + (4 + OUT))
                    act.wait_ge(i_out, c * 4 + (4 + OUT))
                act.wait_ge(unit_r, s + (UNIT - 1))
                act.wait_ge(unit_i, s + (UNIT - 1))
                if type(c) is not int or s:
                    act.wait_ge(cos_i_done, s)
                nc.scalar.activation(mag[:, q % 2], ri[:, par, :, 0, cols], ACT.Square)
                nc.scalar.activation(u[:, 1], ri[:, par, :, 1, cols], ACT.Square).then_inc(sq_done, 1)
                act.wait_ge(m2_done, s + 1)
                nc.scalar.activation(mag[:, q % 2], mag[:, q % 2], ACT.Sqrt).then_inc(mag_done, 1)

            def begin_g(c, q):
                s = c * N + q
                act.wait_ge(r_step, s * 3 + 1)
                act.wait_ge(i_step, s * 3 + 1)
                if q == 0:
                    act.wait_ge(strengths_landed, CH * N * 16)
                    nc.scalar.activation(strength[:], strengths[:, bass.ds(c, 1)].rearrange("p a i j -> p (a i) j"),
                                         ACT.Copy).then_inc(strength_done, 1)
                    act.wait_ge(strength_done, c + 1)
                act.wait_ge(cos_done, s * 2 + 1)
                for j in range(N):
                    i = OTHERS[j][0]
                    nc.scalar.activation(g[:, j, :], pair(i, j), ACT.Identity, bias=strength[:, j, j:j + 1],
                                         scale=strength[:, i, j:j + 1]).then_inc(g_begun, 1)

            def norm_of(c, outs):
                act.wait_ge(r_step, c * 12 + (12 + STEP))
                act.wait_ge(i_step, c * 12 + (12 + STEP))
                act.wait_ge(r_out, outs + OUT)
                for w in range(2):
                    if w:
                        act.wait_ge(norm_sum, c * 3 + 1)
                    nc.scalar.activation(part[:], sup[:, w, :], ACT.Square,
                                         accum_out=norm[:, w:w + 1]).then_inc(norm_sum, 1)
                act.wait_ge(norm_sum, c * 3 + 2)
                nc.scalar.activation(norm[:, 1:2], norm[:, 1:2], ACT.Identity, bias=eps[:, 0:1]).then_inc(norm_sum, 1)
                act.wait_ge(norm_sum, c * 3 + 3)
                nc.scalar.activation(norm[:, 0:1], norm[:, 0:1], ACT.Sqrt, bias=norm[:, 1:2]).then_inc(norm_root, 1)
                act.wait_ge(norm_done, c + 1)
                flat = sup[:].rearrange("p w j -> p (w j)")
                nc.scalar.activation(flat, flat, ACT.Copy, scale=norm[:, 2:3]).then_inc(sup_done, 1)
                act.wait_ge(sup_done, c + 1)
                act.dma_start(sup_out[bass.ds(c, 1)].rearrange("a p j -> p (a j)"), flat).then_inc(stored, 16)

            def quarter(c, par, q, magnitude, of):
                if magnitude:
                    magnitude(of, par if q < N - 1 else 1 - par, (q + 1) % N)
                if q == 0 and (type(c) is not int or c):
                    norm_of(c - 1, CH * N if type(c) is int and c == CH - 1 else c * 4 + 5)
                begin_g(c, q)

            act.wait_ge(a_landed[0], 32)
            nc.scalar.activation(a_hi[:, 0], a_raw[:, 0], ACT.Copy).then_inc(a_hi_done, 1)
            for mat in range(8):
                high_w(mat)
                if mat == 1:
                    high_a(0, 1)
            act.wait_ge(eps_set, 1)
            act.wait_ge(w_lo_done, 8)

            def unit(c, par, n, work):
                if type(c) is not int or c or n:
                    high_a(c + (n + 1) // N, (n + 1) % N)
                work()
                act.wait_ge(mm_done, c * 12 + (3 * n + 2 + MM))
                act.wait_ge(r_out, c * 4 + (n + OUT))
                nc.scalar.activation(part[:], banks[n % 2 * 3 + 1][:], ACT.Copy).then_inc(part_done, 1)
                act.wait_ge(mm_done, c * 12 + (3 * n + 3 + MM))
                if n == 0 and (type(c) is not int or c >= 2):
                    act.wait_ge(i_step, c * 12 + (STEP - 12))
                nc.scalar.activation(ri[:, par, n, 1, :], banks[n % 2 * 3 + 2][:], ACT.Copy).then_inc(i_out, 1)

            units(act, unit, magnitude, quarter)
            norm_of(CH - 1, CH * N)
            act.wait_ge(stored, CH * 16 + ST)

        @block.vector
        def _(dve):
            dve.sem_inc(r_out, OUT)
            dve.sem_inc(r_step, STEP)
            dve.sem_inc(unit_r, UNIT)
            dve.sem_inc(cos_sum, SUM)

            def low_w(mat):
                dve.wait_ge(w_hi_done, mat + 1)
                nc.vector.tensor_tensor(w_lo[:, mat, :, :].rearrange("p k j -> p (k j)"), slot(mat),
                                        w_hi[:, mat, :, :].rearrange("p k j -> p (k j)").bitcast(F32),
                                        ALU.subtract).then_inc(w_lo_done, 1)

            def low_a(c, n):
                dve.wait_ge(a_hi_done, c * N + (n + 1))
                nc.vector.tensor_tensor(a_lo[:, n % 2], a_raw[:, n % 2], a_hi[:, n % 2].bitcast(F32),
                                        ALU.subtract).then_inc(a_lo_done, 1)

            def norm_of(c):
                dve.wait_ge(norm_root, c + 1)
                nc.vector.reciprocal(norm[:, 2:3], norm[:, 0:1]).then_inc(norm_done, 1)

            def magnitude(c, par, q):
                dve.wait_ge(mag_done, c * N + (q + 1))
                nc.vector.reciprocal(mag[:, q % 2], mag[:, q % 2]).then_inc(inv_done, 1)

            def quarter(c, par, q, magnitude, of):
                s = c * N + q
                cr = ri[:, par, :, 0, W * q:W * q + W]
                dve.wait_ge(inv_done, s + 1)
                nc.vector.tensor_tensor(u[:, 0], cr, mag[:, q % 2], ALU.mult).then_inc(unit_r, 1)
                dve.wait_ge(unit_r, s + (1 + UNIT))
                products(nc.vector, cos, u[:, 0]).then_inc(cos_r_done, 1)
                if magnitude:
                    magnitude(of, None, (q + 1) % N)
                if q == 0 and (type(c) is not int or c):
                    norm_of(c - 1)
                dve.wait_ge(cos_r_done, s + 1)
                dve.wait_ge(cos_i_done, s + 2)
                for some in (slice(0, 3), slice(3, 6)):
                    nc.vector.tensor_tensor(cos[:, some], cos[:, some], cos_i[:, some], ALU.add).then_inc(cos_sum, 1)
                for i, some in enumerate((slice(0, 3), slice(3, 6))):
                    dve.wait_ge(cos_sum, s * 2 + (i + 1 + SUM))
                    nc.vector.tensor_scalar(cos[:, some], cos[:, some], 1.0, None, ALU.min).then_inc(cos_done, 1)
                dve.wait_ge(cos_done, s * 2 + 2)
                for k in (1, 2):
                    for j in range(N):
                        i = OTHERS[j][k]
                        if k == 1:
                            dve.wait_ge(g_begun, s * 4 + (j + 1))
                        else:
                            dve.wait_ge(g_step, s * 8 + (j + 1))
                        nc.vector.scalar_tensor_tensor(out=g[:, j, :], in0=pair(i, j), scalar=strength[:, i, j:j + 1],
                                                       in1=g[:, j, :], op0=ALU.mult, op1=ALU.add).then_inc(g_step, 1)
                dve.wait_ge(g_step, s * 8 + 8)
                nc.vector.tensor_tensor(cr, cr, g[:], ALU.mult).then_inc(r_step, 1)
                dve.wait_ge(r_step, s * 3 + (STEP + 1))
                nc.vector.tensor_tensor(cr[:, 0:2], cr[:, 0:2], cr[:, 2:4], ALU.add).then_inc(r_step, 1)
                dve.wait_ge(r_step, s * 3 + (STEP + 2))
                if q == 0:
                    dve.wait_ge(stored, c * 16 + ST)
                nc.vector.tensor_tensor(sup[:, 0, W * q:W * q + W], cr[:, 0, :], cr[:, 1, :], ALU.add).then_inc(r_step, 1)

            low_a(0, 0)
            for mat in range(8):
                low_w(mat)
                if mat == 1:
                    low_a(0, 1)

            def unit(c, par, n, work):
                if type(c) is int and not c and n:
                    low_a(c + (n + 1) // N, (n + 1) % N)
                work()
                dve.wait_ge(mm_done, c * 12 + (3 * n + 1 + MM))
                dve.wait_ge(part_done, c * 4 + (n + 1))
                if n == 0 and (type(c) is not int or c >= 2):
                    dve.wait_ge(r_step, c * 12 + (STEP - 12))
                nc.vector.tensor_tensor(ri[:, par, n, 0, :], banks[n % 2 * 3][:], part[:], ALU.subtract).then_inc(r_out, 1)

            units(dve, unit, magnitude, quarter)
            norm_of(CH - 1)

        @block.tensor
        def _(pe):
            pe.sem_inc(mm_done, MM)

            def chunk(c, first):
                for n in range(N):
                    pe.wait_ge(a_lo_done, c * N + (n + 1))
                    pe.wait_ge(r_out, c * 4 + (n - 1 + OUT))
                    pe.wait_ge(i_out, c * 4 + (n - 1 + OUT))
                    for x, terms in enumerate((((0, 0),), ((1, 1),), ((0, 1), (1, 0)))):
                        if first and x < 2:
                            pe.wait_ge(w_lo_done, 2 * n + x + 1)
                        for i, (comp, w) in enumerate(terms):
                            for k in range(DT):
                                mm = product(nc, banks[n % 2 * 3 + x][:], (a_hi[:, n % 2, comp, k, :], a_lo[:, n % 2, comp, k, :]),
                                             (w_hi[:, 2 * n + w, k, :], w_lo[:, 2 * n + w, k, :]),
                                             i == 0 and k == 0, i == len(terms) - 1 and k == DT - 1)
                        mm.then_inc(mm_done, 1)

            chunk(0, True)
            with pe.Fori(1, CH) as c:
                chunk(c, False)


def tower(nc, sup_in, xT, w_tail, b_post, g_postT, be_postT, b1T, b2T, w3, y_out):
    with ExitStack() as ctx:
        m = Mem(nc, ctx, "tower")
        RAW, RING = 3, 6
        sup = m.sb("sup", [P, 4, 2 * D])
        sup_hi = m.sb("sup_hi", [P, 2 * DT, HALF], R32)
        sup_lo = m.sb("sup_lo", [P, 2 * DT, HALF], R32)
        w_raw = m.sb("w_raw", [P, RAW, 2, 512])
        w_hi = m.sb("w_hi", [P, RING, 512], R32)
        w_lo = m.sb("w_lo", [P, RING, 512], R32)
        x_raw = m.sb("x_raw", [P, 4, HALF])
        x_hi = m.sb("x_hi", [P, 4, HALF], R32)
        x_lo = m.sb("x_lo", [P, 4, HALF], R32)
        square = m.sb("square", [P, 2, HALF])
        f32 = m.sb("f32", [P, DT, HALF])
        y_hi = [m.sb(f"y_hi{i}", [P, DT, HALF], R32) for i in range(3)]
        y_lo = [m.sb(f"y_lo{i}", [P, DT, HALF], R32) for i in range(3)]
        post = m.sb("post", [P, 4, D])
        h2 = m.sb("h2", [P, 2, HALF])
        y = m.sb("y", [1, HALF])
        ident = m.sb("ident", [P, P])
        post_row = m.sb("post_row", [P, D])
        stats = m.sb("stats", [P, 4, 6])
        mean_var = m.sb("mean_var", [P, 4, 2])
        std = m.sb("std", [P, 4])
        rstd = m.sb("rstd", [P, 4])
        gain = m.sb("gain", [P, DT])
        shift = m.sb("shift", [P, DT])
        b1 = m.sb("b1", [P, DT])
        b2 = m.sb("b2", [P, 2])
        w3_col = m.sb("w3_col", [P, 2])
        banks = [m.bank(f"bank{i}") for i in range(8)]

        TILES = ([("mr", k, 1) for k in range(4)] + [("mr", 4 + k, -1) for k in range(4)]
                 + [("mi", 4 + k, 1) for k in range(4)] + [("mi", k, 1) for k in range(4)]
                 + [("x", k, 1) for k in range(8)] + [("post", k, 1) for k in range(4)]
                 + [("x", 8 + k, 1) for k in range(8)] + [("z", k, 1) for k in range(4)]
                 + [("top2", k, 1) for k in range(2)])
        PAIRS = [0, 1, 2, 3, 0, 1, 2, 3, 6, 7, 8, 9, 4, 5, 10, 11, 12, 13, 14, 15, 16]
        NT = len(TILES)
        FIRST = {layer: [t[0] for t in TILES].index(layer) for layer in ("mr", "mi", "x", "post", "z", "top2")}
        X_AT = [i for i, t in enumerate(TILES) if t[0] == "x"]

        c_landed, ident_ready = m.sem("c_landed"), m.sem("ident_ready")
        sup_landed = m.sem("sup_landed")
        w_landed = [m.sem(f"w_landed{i}") for i in range(RAW)]
        x_landed = [m.sem(f"x_landed{i}") for i in range(4)]
        w_hi_done, w_lo_done, w_used = m.sem("w_hi_done"), m.sem("w_lo_done"), m.sem("w_used")
        x_hi_done, x_lo_done = m.sem("x_hi_done"), m.sem("x_lo_done")
        turned, sup_hi_done, sup_lo_done = m.sem("turned"), m.sem("sup_hi_done"), m.sem("sup_lo_done")
        sq_done, power, amp_done = m.sem("sq_done"), m.sem("power"), m.sem("amp_done")
        f32_done, y_hi_done, y_lo_done = m.sem("f32_done"), m.sem("y_hi_done"), m.sem("y_lo_done")
        post_done, stat_done, var_done, std_done, rstd_done, z_done, zt_done = (m.sem(x) for x in (
            "post_done", "stat_done", "var_done", "std_done", "rstd_done", "z_done", "zt_done"))
        h2_done, top_done, y_done, y_stored = m.sem("h2_done"), m.sem("top_done"), m.sem("y_done"), m.sem("y_stored")
        block = ctx.enter_context(nc.Block())

        LO, XL, SL, ST = 2 * RAW, 4, 8, 16

        @block.sync
        def _(sp):
            for to, of in ((post_row[:], b_post.partition_broadcast(P)), (gain[:], g_postT), (shift[:], be_postT),
                           (b1[:], b1T), (b2[:], b2T), (w3_col[:], w3)):
                sp.dma_start(to, of).then_inc(c_landed, 16)
            with sp.Fori(0, HALVES) as hf:
                sp.wait_ge(sup_lo_done, hf * 8 + SL)
                sp.dma_start(sup[:], sup_in[bass.ds(hf * 4, 4)].rearrange("t p j -> p t j")).then_inc(sup_landed, 16)
                for pair in range(NT // 2):
                    sp.wait_ge(w_lo_done, hf * NT + (2 * pair + 2 - 2 * RAW + LO))
                    sp.dma_start(w_raw[:, pair % RAW], w_tail[PAIRS[pair]]).then_inc(w_landed[pair % RAW], 16)
                    for i in (2 * pair, 2 * pair + 1):
                        if i in X_AT:
                            k = X_AT.index(i)
                            sp.wait_ge(x_lo_done, hf * KT + (k - 3 + XL))
                            sp.dma_start(x_raw[:, k % 4, :], xT[bass.ds(hf * KT + k, 1)].rearrange("a p t -> p (a t)")).then_inc(x_landed[k % 4], 16)

        @block.gpsimd
        def _(pool):
            nc.gpsimd.memset(ident[:], 0.0).then_inc(ident_ready, 1)
            pool.wait_ge(ident_ready, 1)
            nc.gpsimd.affine_select(out=ident[:], in_=ident[:], compare_op=ALU.not_equal, fill=1.0, base=0,
                                    pattern=[[-1, P]], channel_multiplier=1).then_inc(ident_ready, 1)

        @block.scalar
        def _(act):
            def high(hf, i):
                act.wait_ge(w_landed[i // 2 % RAW], hf * (NT // 2 // RAW * 16) + (i // 2 // RAW + 1) * 16)
                act.wait_ge(w_used, hf * NT + (i + 1))
                nc.scalar.activation(w_hi[:, i % RING, :], w_raw[:, i // 2 % RAW, i % 2, :], ACT.Copy,
                                     scale=float(TILES[i][2])).then_inc(w_hi_done, 1)
                if i in X_AT:
                    k = X_AT.index(i)
                    if k >= 4:
                        act.wait_ge(w_used, hf * NT + (X_AT[k - 4] + 1 + RING))
                    act.wait_ge(x_landed[k % 4], hf * 64 + (k // 4 + 1) * 16)
                    nc.scalar.activation(x_hi[:, k % 4, :], x_raw[:, k % 4, :], ACT.Copy).then_inc(x_hi_done, 1)

            def split_high(hf, layer, k):
                act.wait_ge(f32_done, hf * 12 + (4 * layer + k + 1))
                nc.scalar.activation(y_hi[layer][:, k, :], f32[:, k, :], ACT.Copy).then_inc(y_hi_done, 1)

            act.sem_inc(y_stored, ST)
            act.wait_ge(c_landed, 6 * 16)
            with act.Fori(0, HALVES) as hf:
                for k in range(8):
                    act.wait_ge(turned, hf * 8 + (k + 1))
                    nc.scalar.activation(sup_hi[:, k, :], banks[4 + k % 4][:], ACT.Copy).then_inc(sup_hi_done, 1)
                    if k < RING:
                        high(hf, k)
                for i in range(RING, FIRST["x"]):
                    high(hf, i)
                act.wait_ge(w_used, hf * NT + (FIRST["x"] + RING))
                for f in range(4):
                    if f:
                        act.wait_ge(power, hf * 4 + f)
                    nc.scalar.activation(square[:, 0, :], banks[f][:], ACT.Square)
                    nc.scalar.activation(square[:, 1, :], banks[4 + f][:], ACT.Square).then_inc(sq_done, 1)
                    high(hf, FIRST["x"] + f)
                    act.wait_ge(power, hf * 4 + (f + 1))
                    nc.scalar.activation(f32[:, f, :], f32[:, f, :], ACT.Sqrt).then_inc(f32_done, 1)
                    split_high(hf, 0, f)
                for i in range(FIRST["x"] + 4, FIRST["post"] + 4 + 7):
                    high(hf, i)
                act.wait_ge(var_done, hf + 1)
                nc.scalar.activation(std[:], mean_var[:, :, 1], ACT.Sqrt).then_inc(std_done, 1)
                high(hf, FIRST["post"] + 11)
                for k in range(4):
                    act.wait_ge(zt_done, hf * 4 + (k + 1))
                    nc.scalar.activation(f32[:, k, :], banks[k][:], ACT.Gelu, bias=shift[:, k:k + 1],
                                         scale=gain[:, k:k + 1]).then_inc(f32_done, 1)
                    split_high(hf, 1, k)
                    high(hf, FIRST["z"] + k)
                for k in range(2):
                    high(hf, FIRST["top2"] + k)
                act.wait_ge(w_used, hf * NT + (FIRST["top2"] + RING))
                for f in range(4):
                    nc.scalar.activation(f32[:, f, :], banks[4 + f][:], ACT.Relu, bias=b1[:, f:f + 1]).then_inc(f32_done, 1)
                    split_high(hf, 2, f)
                act.wait_ge(w_used, hf * NT + (NT + RING))
                for f in range(2):
                    nc.scalar.activation(h2[:, f, :], banks[f][:], ACT.Relu, bias=b2[:, f:f + 1]).then_inc(h2_done, 1)
                act.wait_ge(top_done, hf + 1)
                act.wait_ge(y_stored, hf * 16 + ST)
                nc.scalar.activation(y[:], banks[2][0:1, :], ACT.Copy).then_inc(y_done, 1)
                act.wait_ge(y_done, hf + 1)
                act.dma_start(y_out[bass.ds(hf * HALF, HALF), :].rearrange("t a -> a t"), y[:]).then_inc(y_stored, 16)
            act.wait_ge(y_stored, HALVES * 16 + ST)

        @block.vector
        def _(dve):
            def low(hf, i):
                raw, hi, lo = w_raw[:, i // 2 % RAW, i % 2, :], w_hi[:, i % RING, :].bitcast(F32), w_lo[:, i % RING, :]
                dve.wait_ge(w_hi_done, hf * NT + (i + 1))
                if TILES[i][2] < 0:
                    nc.vector.scalar_tensor_tensor(out=lo, in0=raw, scalar=-1.0, in1=hi, op0=ALU.mult,
                                                   op1=ALU.subtract).then_inc(w_lo_done, 1)
                else:
                    nc.vector.tensor_tensor(lo, raw, hi, ALU.subtract).then_inc(w_lo_done, 1)
                if i in X_AT:
                    k = X_AT.index(i)
                    dve.wait_ge(x_hi_done, hf * KT + (k + 1))
                    nc.vector.tensor_tensor(x_lo[:, k % 4, :], x_raw[:, k % 4, :], x_hi[:, k % 4, :].bitcast(F32),
                                            ALU.subtract).then_inc(x_lo_done, 1)

            def split_low(hf, layer, k):
                dve.wait_ge(y_hi_done, hf * 12 + (4 * layer + k + 1))
                nc.vector.tensor_tensor(y_lo[layer][:, k, :], f32[:, k, :], y_hi[layer][:, k, :].bitcast(F32),
                                        ALU.subtract).then_inc(y_lo_done, 1)

            dve.sem_inc(w_lo_done, LO)
            dve.sem_inc(x_lo_done, XL)
            dve.sem_inc(sup_lo_done, SL)
            dve.wait_ge(c_landed, 6 * 16)
            with dve.Fori(0, HALVES) as hf:
                for k in range(8):
                    dve.wait_ge(sup_hi_done, hf * 8 + (k + 1))
                    nc.vector.tensor_tensor(sup_lo[:, k, :], banks[4 + k % 4][:], sup_hi[:, k, :].bitcast(F32),
                                            ALU.subtract).then_inc(sup_lo_done, 1)
                    if k < RING:
                        low(hf, k)
                for i in range(RING, FIRST["x"]):
                    low(hf, i)
                for f in range(4):
                    dve.wait_ge(sq_done, hf * 4 + (f + 1))
                    nc.vector.tensor_tensor(f32[:, f, :], square[:, 0, :], square[:, 1, :], ALU.add).then_inc(power, 1)
                    low(hf, FIRST["x"] + f)
                    split_low(hf, 0, f)
                for i in range(FIRST["x"] + 4, FIRST["post"] + 4 + 7):
                    low(hf, i)
                dve.wait_ge(w_used, hf * NT + (FIRST["post"] + 4 + RING))
                for t in range(4):
                    nc.vector.tensor_tensor(post[:, t, :], banks[t][:], post_row[:], ALU.add).then_inc(post_done, 1)
                for t in range(4):
                    dve.wait_ge(post_done, hf * 4 + (t + 1))
                    nc.vector.bn_stats(stats[:, t, :], post[:, t, :]).then_inc(stat_done, 1)
                dve.wait_ge(stat_done, hf * 8 + 4)
                dve.nop(nofuse=True)
                for t in range(4):
                    nc.vector.bn_aggr(mean_var[:, t, :], stats[:, t, :]).then_inc(stat_done, 1)
                dve.wait_ge(stat_done, hf * 8 + 8)
                nc.vector.tensor_scalar(mean_var[:, :, 1], mean_var[:, :, 1], EPS, None, ALU.add).then_inc(var_done, 1)
                dve.wait_ge(std_done, hf + 1)
                nc.vector.reciprocal(rstd[:], std[:]).then_inc(rstd_done, 1)
                dve.wait_ge(rstd_done, hf + 1)
                for t in range(4):
                    nc.vector.tensor_scalar(post[:, t, :], post[:, t, :], mean_var[:, t, 0:1], rstd[:, t:t + 1], ALU.subtract,
                                            ALU.mult).then_inc(z_done, 1)
                low(hf, FIRST["post"] + 11)
                for k in range(4):
                    split_low(hf, 1, k)
                    low(hf, FIRST["z"] + k)
                for k in range(2):
                    low(hf, FIRST["top2"] + k)
                for f in range(4):
                    split_low(hf, 2, f)

        @block.tensor
        def _(pe):
            pe.sem_inc(w_used, RING)
            pe.wait_ge(ident_ready, 2)
            pe.wait_ge(c_landed, 6 * 16)
            with pe.Fori(0, HALVES) as hf:
                def w(i, cols=slice(0, 512)):
                    return (w_hi[:, i % RING, cols], w_lo[:, i % RING, cols])

                pe.wait_ge(sup_landed, hf * 16 + 16)
                for k in range(8):
                    if k < 4:
                        pe.wait_ge(sup_lo_done, hf * 8 + SL)
                    else:
                        pe.wait_ge(sup_lo_done, hf * 8 + (k - 3 + SL))
                    for t in range(4):
                        mm = nc.tensor.transpose(banks[4 + k % 4][:, P * t:P * t + P], sup[:, t, P * k:P * k + P], ident[:])
                    mm.then_inc(turned, 1)
                for i, (layer, k, _) in enumerate(TILES):
                    if i == FIRST["z"]:
                        for j in range(4):
                            pe.wait_ge(z_done, hf * 4 + 4)
                            for t in range(4):
                                mm = nc.tensor.transpose(banks[j][:, P * t:P * t + P], post[:, t, P * j:P * j + P], ident[:])
                            mm.then_inc(zt_done, 1)
                    pe.wait_ge(w_lo_done, hf * NT + (i + 1 + LO))
                    if i == FIRST["mi"]:
                        pe.wait_ge(sup_lo_done, hf * 8 + (8 + SL))
                    if layer == "mr":
                        pe.wait_ge(sup_lo_done, hf * 8 + (k + 1 + SL))
                    if layer == "x":
                        if k == 0:
                            pe.wait_ge(sq_done, hf * 4 + 4)
                        pe.wait_ge(x_lo_done, hf * KT + (k + 1 + XL))
                    if layer == "post":
                        pe.wait_ge(y_lo_done, hf * 12 + (k + 1))
                    if layer == "z":
                        pe.wait_ge(y_lo_done, hf * 12 + (4 + k + 1))
                    if layer == "top2":
                        pe.wait_ge(y_lo_done, hf * 12 + (8 + 2 * k + 2))
                        for kk in range(2):
                            for f in range(2):
                                c = 256 * kk + P * f
                                kt = 2 * k + kk
                                mm = product(nc, banks[f][:], w(i, slice(c, c + P)), (y_hi[2][:, kt, :], y_lo[2][:, kt, :]),
                                             kt == 0, kt == 3)
                        mm.then_inc(w_used, 1)
                        continue
                    for f in range(4):
                        s = slice(P * f, P * f + P)
                        if layer == "mr":
                            mm = product(nc, banks[f][:], w(i, s), (sup_hi[:, k, :], sup_lo[:, k, :]), k == 0, k == 7)
                        elif layer == "mi":
                            mm = product(nc, banks[4 + f][:], w(i, s), (sup_hi[:, k, :], sup_lo[:, k, :]), k == 4, k == 3)
                        elif layer == "post":
                            mm = product(nc, banks[f][:], (y_hi[0][:, k, s], y_lo[0][:, k, s]), w(i), k == 0, k == 3)
                        elif layer == "x":
                            mm = product(nc, banks[4 + f][:], w(i, s), (x_hi[:, k % 4, :], x_lo[:, k % 4, :]), k == 0, False)
                        else:
                            mm = product(nc, banks[4 + f][:], w(i, s), (y_hi[1][:, k, :], y_lo[1][:, k, :]), False, k == 3)
                    mm.then_inc(w_used, 1)
                for f in range(2):
                    pe.wait_ge(h2_done, hf * 2 + (f + 1))
                    mm = nc.tensor.matmul(banks[2][0:1, :], w3_col[:, f:f + 1], h2[:, f, :], start=(f == 0), stop=(f == 1))
                mm.then_inc(top_done, 1)


def kernel(**inputs):
    import concourse.bacc as bacc
    from concourse.bass_utils import run_bass_kernel_spmd

    p = {k.removeprefix("L0_rec_"): np.asarray(v) for k, v in inputs.items()}

    def tiles(w):
        return w.reshape(w.shape[0], -1, P).transpose(2, 1, 0)

    def pairs(w):
        return w.reshape(-1, 2, P, w.shape[1]).transpose(0, 2, 1, 3)

    def columns(*vectors):
        return np.stack(vectors).reshape(len(vectors), -1, P).transpose(2, 0, 1)

    enc = ("er", "ei")
    top1 = p["W_top1"]
    host = {
        "xT": p["r_x"].reshape(HALVES, HALF, KT, P).transpose(0, 2, 3, 1).reshape(HALVES * KT, P, HALF),
        "w_enc": np.stack([p[f"{e}_{w}"].reshape(4, 512, KT // 2, 2, P).transpose(0, 2, 4, 3, 1)
                           for e in enc for w in ("W1", "W2")]).reshape(-1, P, 2, 512),
        "b1": np.stack([p[f"{e}_b1"] for e in enc]).reshape(-1, 512),
        "g1T": columns(*[p[f"{e}_g1"] for e in enc]).transpose(1, 0, 2),
        "be1T": columns(*[p[f"{e}_be1"] for e in enc]).transpose(1, 0, 2),
        "b2T": columns(*[p[f"{e}_b2"] for e in enc]).transpose(1, 0, 2),
        "w_qkv": np.stack([tiles(p[n]) for n in ("Wq_r", "Wq_i", "Wk_r", "Wk_i", "Wv_r", "Wv_i")]),
        "b_qkT": columns(p["bq_r"], p["bq_i"], p["bk_r"], p["bk_i"]),
        "b_v": np.stack([p["bv_r"], p["bv_i"]]),
        "w_o": np.stack([tiles(p["Wo_r"]), tiles(p["Wo_i"])]),
        "b_oT": columns(p["bo_r"], p["bo_i"]),
        "w_int": np.stack([tiles(p[w][n]).reshape(P, DT * 512) for n in range(N) for w in ("int_Wr", "int_Wi")]),
        "ids": p["ids"].reshape(CH, P, N).transpose(1, 0, 2),
        "w_tail": np.concatenate([pairs(p["meas_Mr"].T), pairs(p["meas_Mi"].T), pairs(p["post_W"].T), pairs(top1[D:]),
                                  pairs(top1[:D]),
                                  p["W_top2"].reshape(1, 2, 2, P, 256).transpose(0, 3, 1, 2, 4).reshape(1, P, 2, 512)]),
        "b_post": p["post_b"],
        "g_postT": columns(p["post_g"])[:, 0],
        "be_postT": columns(p["post_be"])[:, 0],
        "b_top1T": columns(p["b_top1"])[:, 0],
        "b_top2T": columns(p["b_top2"])[:, 0],
        "w3": p["W_top3"].reshape(2, P).T,
    }
    for f in range(N):
        host[f"tbl_{f}"] = p[f"tbl_{f}"]
    nc = bacc.Bacc("TRN2", target_bir_lowering=False, num_devices=1)
    arrays, d = {}, {}
    for name, a in host.items():
        arrays[f"in_{name}"] = np.ascontiguousarray(a)
        d[name] = nc.dram_tensor(f"in_{name}", a.shape, mybir.dt.from_np(a.dtype), kind="ExternalInput").ap()

    def scratch(name, shape):
        return nc.dram_tensor(name, shape, F32, kind="Internal").ap()

    s = scratch("s", (CH, 2, P, DT, N, P))
    qkv = scratch("qkv", (CH, 7, P, DT, 512))
    attn = scratch("attn", (CH, 2, P, DT, 512))
    sup = scratch("sup", (CH, P, 2 * D))
    y = nc.dram_tensor("out_y", (TOK, 1), F32, kind="ExternalOutput").ap()
    encoders(nc, d["xT"], d["w_enc"], d["b1"], d["g1T"], d["be1T"], d["b2T"], s)
    projections(nc, s, d["w_qkv"], d["b_qkT"], d["b_v"], qkv)
    attention(nc, qkv, d["w_o"], d["b_oT"], attn)
    superposition(nc, attn, d["w_int"], d["ids"], [d[f"tbl_{f}"] for f in range(N)], sup)
    tower(nc, sup, d["xT"], d["w_tail"], d["b_post"], d["g_postT"], d["be_postT"], d["b_top1T"], d["b_top2T"], d["w3"], y)
    return run_bass_kernel_spmd(nc, [arrays], core_ids=[0]).results[0]["out_y"]
```

```python
from contextlib import ExitStack

import numpy as np

import concourse.bass as bass
from concourse import mybir

F32 = mybir.dt.float32
R32 = mybir.dt.float32r
I32 = mybir.dt.int32
ACT = mybir.ActivationFunctionType
ALU = mybir.AluOpType
AX = mybir.AxisListType

P = 128
TOK = 1024
IN = 2048
N = 4
D = 512
H = 8
HD = D // H
HALF = 512
HALVES = TOK // HALF
KT = IN // P
DT = D // P
CH = TOK // P
EPS = 1e-5
RING = 4


class Mem:

    def __init__(self, nc, ctx, phase):
        self.nc, self.ctx, self.phase = nc, ctx, phase

    def sb(self, name, shape, dt=F32):
        return self.ctx.enter_context(self.nc.sbuf_tensor(f"{self.phase}_{name}", shape, dt))

    def bank(self, name):
        return self.ctx.enter_context(self.nc.psum_tensor(f"{self.phase}_{name}", [P, 512], F32))

    def sem(self, name):
        return self.ctx.enter_context(self.nc.semaphore(f"{self.phase}_{name}"))


def product(nc, out, a, b, first, last):
    (ah, al), (bh, bl) = a, b
    nc.tensor.matmul(out, ah, bh, start=first, stop=False)
    nc.tensor.matmul(out, ah, bl, start=False, stop=False)
    return nc.tensor.matmul(out, al, bh, start=False, stop=last)


def encoders(nc, xT, w_enc, b1, g1T, be1T, b2T, s_out):
    with ExitStack() as ctx:
        m = Mem(nc, ctx, "enc")
        x_hi = m.sb("x_hi", [P, KT, HALF], R32)
        x_lo = m.sb("x_lo", [P, KT, HALF], R32)
        hid = m.sb("hid", [P, 4, IN])
        act_hi = m.sb("act_hi", [P, KT, HALF], R32)
        act_lo = m.sb("act_lo", [P, KT, HALF], R32)
        act_f = m.sb("act_f", [P, 2, HALF])
        w_raw = m.sb("w_raw", [P, 2, 2, 512])
        w_hi = m.sb("w_hi", [P, RING, 512], R32)
        w_lo = m.sb("w_lo", [P, RING, 512], R32)
        b1_row = m.sb("b1_row", [P, 2, 512])
        s_stage = m.sb("s_stage", [P, 2, HALF])
        ident = m.sb("ident", [P, P])
        stats = m.sb("stats", [P, 4, 4 * 6])
        mean_var = m.sb("mean_var", [P, 4, 2])
        std = m.sb("std", [P, 4])
        eps = m.sb("eps", [P, 1])
        rstd = m.sb("rstd", [P, 4])
        gain = m.sb("gain", [P, KT])
        shift = m.sb("shift", [P, KT])
        b2 = m.sb("b2", [P, KT])
        banks = [[m.bank(f"acc{s}{t}") for t in range(4)] for s in range(2)]

        x_landed = [m.sem(f"x_landed{i}") for i in range(4)]
        w_landed = [m.sem(f"w_landed{i}") for i in range(2)]
        b1_landed = [m.sem(f"b1_landed{i}") for i in range(2)]
        c_landed = m.sem("c_landed")
        x_hi_done, x_lo_done = m.sem("x_hi_done"), m.sem("x_lo_done")
        w_hi_done, w_lo_done, w_used = m.sem("w_hi_done"), m.sem("w_lo_done"), m.sem("w_used")
        hid_done, s_done, s_stored = m.sem("hid_done"), m.sem("s_done"), [m.sem(f"s_stored{i}") for i in range(2)]
        ident_ready, eps_set, std_done, rstd_done = m.sem("ident_ready"), m.sem("eps_set"), m.sem("std_done"), m.sem("rstd_done")
        row_done = m.sem("row_done")
        stat_done, z_done, zt_done, gelu_done = m.sem("stat_done"), m.sem("z_done"), m.sem("zt_done"), m.sem("gelu_done")
        act_hi_done, act_lo_done = m.sem("act_hi_done"), m.sem("act_lo_done")
        block = ctx.enter_context(nc.Block())

        ITEMS = 2 * 4 * KT
        LO0, HID0, S0 = 4, 8, 16

        @block.sync
        def _(sp):
            def load_x(half, rows=range(4)):
                for r in rows:
                    sp.dma_start(hid[:, r, :].rearrange("p (k t) -> p k t", k=4),
                                 xT[bass.ds(half * KT + 4 * r, 4)].rearrange("k p t -> p k t")).then_inc(x_landed[r], 16)

            load_x(0, [0])
            with sp.Fori(0, HALVES) as half:
                with sp.Fori(0, 2) as e:
                    it = half * 2 + e
                    with sp.Fori(0, 2) as c2:
                        for cc in range(2):
                            sp.wait_ge(hid_done, it * 16 + c2 * 8 + (4 * cc + 4))
                            sp.dma_start(b1_row[:, cc, :], b1[bass.ds(e * 4 + c2 * 2 + cc, 1)].rearrange("a j -> (a j)").partition_broadcast(P)).then_inc(b1_landed[cc], 16)
                            for q in range(8):
                                sp.wait_ge(w_lo_done, it * ITEMS + c2 * 32 + (16 * cc + 2 * q + 2))
                                sp.dma_start(w_raw[:, q % 2, :, :], w_enc[bass.ds(e * 64 + c2 * 16 + (8 * cc + q), 1)].rearrange("a p k j -> p (a k) j")).then_inc(w_landed[q % 2], 16)
                    for first, pairs in ((0, 5), (5, 11)):
                        with sp.Fori(first, first + pairs) as q2:
                            for qq in range(2):
                                sp.wait_ge(w_lo_done, it * ITEMS + q2 * 4 + (64 + 2 * qq + 2))
                                sp.dma_start(w_raw[:, qq, :, :], w_enc[bass.ds(e * 64 + q2 * 2 + (32 + qq), 1)].rearrange("a p k j -> p (a k) j")).then_inc(w_landed[qq], 16)
                        if not first:
                            sp.wait_ge(zt_done, it * KT + KT)
                            load_x((half + e) % 2)
            for q in range(2):
                sp.wait_ge(w_lo_done, 4 * ITEMS + 2 * q + 2)
                sp.dma_start(w_raw[:, q, :, :], w_enc[q]).then_inc(w_landed[q], 16)
            for r in range(4):
                sp.wait_ge(x_landed[r], 5 * 16)

        @block.gpsimd
        def _(pool):
            nc.gpsimd.memset(eps[:], EPS).then_inc(eps_set, 1)
            nc.gpsimd.memset(ident[:], 0.0).then_inc(ident_ready, 1)
            pool.wait_ge(ident_ready, 1)
            nc.gpsimd.affine_select(out=ident[:], in_=ident[:], compare_op=ALU.not_equal, fill=1.0, base=0,
                                    pattern=[[-1, P]], channel_multiplier=1).then_inc(ident_ready, 1)

            def high_x(rounds):
                for k in range(KT):
                    if k % 4 == 0:
                        pool.wait_ge(x_landed[k // 4], rounds * 16 + 16)
                        pool.nop(nofuse=True)
                    nc.gpsimd.tensor_copy(x_hi[:, k, :], hid[:, k // 4, 512 * (k % 4):512 * (k % 4) + 512]).then_inc(x_hi_done, 1)

            with pool.Fori(0, HALVES) as half:
                with pool.Fori(0, 2) as e:
                    it = half * 2 + e
                    for k in range(KT):
                        pool.wait_ge(gelu_done, it * KT + (k + 1))
                        pool.nop(nofuse=True)
                        nc.gpsimd.tensor_copy(act_hi[:, k, :], act_f[:, k % 2, :]).then_inc(act_hi_done, 1)
                    high_x(it + 1)

        @block.scalar
        def _(act):
            def high(base, i):
                act.wait_ge(w_used, base + (i + 1))
                if i % 2 == 0:
                    act.wait_ge(w_landed[i // 2 % 2], base * 4 + (i // 4 + 1) * 16)
                nc.scalar.activation(w_hi[:, i % RING, :], w_raw[:, i // 2 % 2, i % 2, :], ACT.Copy).then_inc(w_hi_done, 1)

            act.sem_inc(s_done, S0)
            for i in range(2):
                act.sem_inc(s_stored[i], 16)
            act.dma_start(gain[:], g1T[0]).then_inc(c_landed, 16)
            act.dma_start(shift[:], be1T[0]).then_inc(c_landed, 16)
            act.dma_start(b2[:], b2T[0]).then_inc(c_landed, 16)

            def high_x(k):
                act.wait_ge(x_landed[k // 4], 16)
                nc.scalar.activation(x_hi[:, k, :], hid[:, k // 4, 512 * (k % 4):512 * (k % 4) + 512], ACT.Copy).then_inc(x_hi_done, 1)

            act.wait_ge(eps_set, 1)
            act.wait_ge(x_landed[0], 16)
            for r in range(1, 4):
                act.dma_start(hid[:, r, :].rearrange("p (k t) -> p k t", k=4),
                              xT[4 * r:4 * r + 4].rearrange("k p t -> p k t")).then_inc(x_landed[r], 16)
            for k in range(KT):
                if k < RING:
                    high(0, k)
                high_x(k)
            with act.Fori(0, HALVES) as half:
                with act.Fori(0, 2) as e:
                    it = half * 2 + e
                    base = act.snap(it * ITEMS)
                    with act.Fori(0, 4) as c:
                        gbase = act.snap(base + c * 16)
                        for j in range(RING, 16 + RING):
                            high(gbase, j)
                    act.wait_ge(stat_done, it * 20 + 20)
                    nc.scalar.activation(std[:], mean_var[:, :, 1], ACT.Sqrt, bias=eps[:, 0:1]).then_inc(std_done, 1)
                    act.wait_ge(c_landed, it * 48 + 48)
                    for k in range(KT + 2):
                        if k < KT:
                            act.wait_ge(zt_done, it * KT + (k + 1))
                            if k >= 2:
                                act.wait_ge(act_lo_done, it * KT + (k - 1))
                            nc.scalar.activation(act_f[:, k % 2, :], banks[1][k % 4][:], ACT.Gelu,
                                                 bias=shift[:, k:k + 1], scale=gain[:, k:k + 1]).then_inc(gelu_done, 1)
                        if k >= 2:
                            high(base, 64 + RING + k - 2)

                    def out_of_psum(n, f):
                        r = 4 * n + f
                        act.wait_ge(w_used, base + (64 + 16 * n + 16 + RING))
                        act.wait_ge(s_stored[f % 2], it * (8 * 16) + (r // 2 + 1) * 16)
                        nc.scalar.activation(s_stage[:, f % 2, :], banks[n % 2][f][:], ACT.Identity,
                                             bias=b2[:, r:r + 1]).then_inc(s_done, 1)
                        act.wait_ge(s_done, it * 16 + (r + 1 + S0))
                        act.dma_start(s_out[bass.ds(half * 4, 4), bass.ds(e, 1), :, f, n, :].rearrange("c e p t -> p (c e) t"),
                                      s_stage[:, f % 2, :].rearrange("p (c t) -> p c t", c=4)).then_inc(s_stored[f % 2], 16)

                    for n in range(3):
                        for j in range(16):
                            if 16 * (n + 1) + j + RING < 64:
                                high(base, 64 + 16 * (n + 1) + j + RING)
                            if j % 3 == 1 and j < 12:
                                out_of_psum(n, j // 3)
                    for f in range(4):
                        high(base, ITEMS + f)
                        out_of_psum(3, f)
                    act.wait_ge(s_done, it * 16 + (16 + S0))
                    act.dma_start(gain[:], g1T[bass.ds(1 - e, 1)].rearrange("a p k -> p (a k)")).then_inc(c_landed, 16)
                    act.dma_start(shift[:], be1T[bass.ds(1 - e, 1)].rearrange("a p k -> p (a k)")).then_inc(c_landed, 16)
                    act.dma_start(b2[:], b2T[bass.ds(1 - e, 1)].rearrange("a p k -> p (a k)")).then_inc(c_landed, 16)
            act.wait_ge(c_landed, 5 * 48)
            for i in range(2):
                act.wait_ge(s_stored[i], 4 * 8 * 16 + 16)

        @block.vector
        def _(dve):
            def low(base, i):
                dve.wait_ge(w_hi_done, base + (i + 1))
                nc.vector.tensor_tensor(w_lo[:, i % RING, :], w_raw[:, i // 2 % 2, i % 2, :],
                                        w_hi[:, i % RING, :].bitcast(F32), ALU.subtract).then_inc(w_lo_done, 1)

            dve.sem_inc(w_lo_done, LO0)
            dve.sem_inc(hid_done, HID0)

            def low_x(rounds, k):
                dve.wait_ge(x_hi_done, rounds * KT + (k + 1))
                nc.vector.tensor_tensor(x_lo[:, k, :], hid[:, k // 4, 512 * (k % 4):512 * (k % 4) + 512],
                                        x_hi[:, k, :].bitcast(F32), ALU.subtract).then_inc(x_lo_done, 1)

            AHEAD = 2
            for k in range(KT):
                if k < AHEAD:
                    low(0, k)
                low_x(0, k)
            with dve.Fori(0, HALVES) as half:
                with dve.Fori(0, 2) as e:
                    it = half * 2 + e
                    base = dve.snap(it * ITEMS)
                    with dve.Fori(0, 2) as c2:
                        for cc in range(2):
                            gbase = dve.snap(base + c2 * 32 + 16 * cc)
                            for j in range(AHEAD, 16 + AHEAD):
                                low(gbase, j)
                            dve.wait_ge(b1_landed[cc], it * 32 + c2 * 16 + 16)
                            for t in range(4):
                                if t < 3:
                                    dve.wait_ge(row_done, it * 12 + c2 * 6 + (3 * cc + t + 1))
                                else:
                                    dve.wait_ge(w_used, gbase + (16 + RING))
                                nc.vector.tensor_tensor(hid[:, t, bass.ds(c2 * 1024 + 512 * cc, 512)], banks[cc][t][:],
                                                        b1_row[:, cc, :], ALU.add).then_inc(hid_done, 1)
                                dve.wait_ge(hid_done, it * 16 + c2 * 8 + (4 * cc + t + 1 + HID0))
                                nc.vector.bn_stats(stats[:, t, bass.ds(c2 * 12 + 6 * cc, 6)],
                                                   hid[:, t, bass.ds(c2 * 1024 + 512 * cc, 512)]).then_inc(stat_done, 1)
                    dve.wait_ge(stat_done, it * 20 + 16)
                    dve.nop(nofuse=True)
                    for t in range(4):
                        nc.vector.bn_aggr(mean_var[:, t, :], stats[:, t, :]).then_inc(stat_done, 1)
                    dve.wait_ge(std_done, it + 1)
                    nc.vector.reciprocal(rstd[:], std[:]).then_inc(rstd_done, 1)
                    dve.wait_ge(rstd_done, it + 1)

                    def normalise(first, last):
                        for t in range(4):
                            nc.vector.tensor_scalar(hid[:, t, first:last], hid[:, t, first:last], mean_var[:, t, 0:1],
                                                    rstd[:, t:t + 1], ALU.subtract, ALU.mult).then_inc(z_done, 1)
                    normalise(0, P)
                    normalise(P, 512)
                    for i in range(AHEAD, RING):
                        low(base, 64 + i)
                    normalise(512, 1024)
                    for k in range(KT + 2):
                        if k < KT:
                            dve.wait_ge(act_hi_done, it * KT + (k + 1))
                            nc.vector.tensor_tensor(act_lo[:, k, :], act_f[:, k % 2, :], act_hi[:, k, :].bitcast(F32),
                                                    ALU.subtract).then_inc(act_lo_done, 1)
                        if k in (1, 5):
                            normalise(1024 + k // 4 * 512, 1536 + k // 4 * 512)
                        if k >= 2:
                            low(base, 64 + RING + k - 2)
                    for n in range(1, 4):
                        for j in range(RING, 16 + RING):
                            if 16 * n + j < 64:
                                low(base, 64 + 16 * n + j)
                            if n == 2:
                                low_x(it + 1, j - RING)
                    for i in range(AHEAD):
                        low(base, ITEMS + i)

        @block.tensor
        def _(pe):
            pe.sem_inc(w_used, RING)
            pe.wait_ge(ident_ready, 2)
            with pe.Fori(0, HALVES) as half:
                with pe.Fori(0, 2) as e:
                    it = half * 2 + e
                    base = pe.snap(it * ITEMS)
                    with pe.Fori(0, 2) as c2:
                        for cc in range(2):
                            pe.wait_ge(hid_done, it * 16 + c2 * 8 + (4 * cc + 4))
                            pe.wait_ge(s_done, it * 16 + (12 + 4 * cc))

                            def row(k, t):
                                s = slice(P * t, P * t + P)
                                return product(nc, banks[cc][t][:], (x_hi[:, k, s], x_lo[:, k, s]),
                                               (w_hi[:, k % RING, :], w_lo[:, k % RING, :]), k == 0, k == KT - 1)

                            for k in range(KT):
                                pe.wait_ge(x_lo_done, it * KT + (k + 1))
                                pe.wait_ge(w_lo_done, base + c2 * 32 + (16 * cc + k + 1 + LO0))
                                if k < KT - 2:
                                    for t in range(4):
                                        mm = row(k, t)
                                    mm.then_inc(w_used, 1)
                            for t in range(4):
                                mm = row(KT - 2, t)
                                if t == 3:
                                    mm.then_inc(w_used, 1)
                                row(KT - 1, t).then_inc(row_done if t < 3 else w_used, 1)

                    def turn(k):
                        if k:
                            pe.wait_ge(z_done, it * 20 + (k // 4 * 4 + 8))
                        if k >= 4:
                            pe.wait_ge(gelu_done, it * KT + (k - 3))
                        for t in range(4):
                            if not k:
                                pe.wait_ge(z_done, it * 20 + (t + 1))
                            mm = nc.tensor.transpose(banks[1][k % 4][:, P * t:P * t + P], hid[:, t, P * k:P * k + P], ident[:])
                        mm.then_inc(zt_done, 1)

                    for n in range(4):
                        if n == 0:
                            for k in range(3):
                                turn(k)
                            pe.wait_ge(hid_done, it * 16 + (12 + HID0))
                        elif n == 1:
                            pe.wait_ge(gelu_done, it * KT + KT)
                        else:
                            pe.wait_ge(s_done, it * 16 + (4 * n - 4 + S0))
                        for k in range(KT):
                            pe.wait_ge(w_lo_done, base + (64 + 16 * n + k + 1 + LO0))
                            if n == 0:
                                pe.wait_ge(act_lo_done, it * KT + (k + 1))
                            a = (act_hi[:, k, :], act_lo[:, k, :])
                            for f in range(4):
                                s = slice(P * f, P * f + P)
                                mm = product(nc, banks[n % 2][f][:], (w_hi[:, k % RING, s], w_lo[:, k % RING, s]), a,
                                             k == 0, k == KT - 1)
                            mm.then_inc(w_used, 1)
                            if n == 0 and k + 3 < KT:
                                turn(k + 3)


def projections(nc, s_in, w_qkv, b_qkvT, b_v, qkv_out):
    with ExitStack() as ctx:
        m = Mem(nc, ctx, "proj")
        MATS = 6
        w_hi = m.sb("w_hi", [P, MATS, DT, 512], R32)
        w_lo = m.sb("w_lo", [P, MATS, DT, 512], R32)
        s_raw = m.sb("s_raw", [P, 2, DT, 512])
        s_hi = m.sb("s_hi", [P, 2, 2, DT, 512], R32)
        s_lo = m.sb("s_lo", [P, 2, 2, DT, 512], R32)
        stage_a = m.sb("stage_a", [P, DT, 512])
        stage_d = m.sb("stage_d", [P, DT, 512])
        b_col = m.sb("b_col", [P, 4, DT])
        bv_row = m.sb("bv_row", [P, 2, 512])
        banks = [[m.bank(f"acc{s}{t}") for t in range(4)] for s in range(2)]

        b_landed = m.sem("b_landed")
        w_landed = [m.sem(f"w_landed{i}") for i in range(2)]
        s_landed = [m.sem(f"s_landed{i}") for i in range(2)]
        w_hi_done, w_lo_done = m.sem("w_hi_done"), m.sem("w_lo_done")
        s_hi_done, s_lo_done = m.sem("s_hi_done"), m.sem("s_lo_done")
        mm_done, act_out, dve_out, neg_out = m.sem("mm_done"), m.sem("act_out"), m.sem("dve_out"), m.sem("neg_out")
        act_stored, dve_stored = m.sem("act_stored"), m.sem("dve_stored")
        block = ctx.enter_context(nc.Block())

        def by_group(x):
            return x.rearrange("p (n g t) -> p g n t", n=N, g=4)

        def grouped(x, buf, comp, k):
            return x[:, buf, comp, k, :].rearrange("p (g n t) -> p g n t", n=N, g=4)

        AO, DO, SL, ST, MM = 8, 16, 8, 16, 6

        @block.sync
        def _(sp):

            def load_s(c):
                for comp in range(2):
                    sp.wait_ge(s_lo_done, c * 8 + (4 * comp + 4))
                    sp.dma_start(s_raw[:, comp, :, :].rearrange("p k (n t) -> p k n t", n=N),
                                 s_in[bass.ds(c % CH, 1), comp].rearrange("a p k n t -> p (a k) n t")).then_inc(s_landed[comp], 16)

            for mat in range(MATS):
                if mat >= 2:
                    sp.wait_ge(w_lo_done, DT * (mat - 1))
                sp.dma_start((stage_a, stage_d)[mat % 2][:], w_qkv[mat]).then_inc(w_landed[mat % 2], 16)
                if mat == 0:
                    load_s(0)
                if mat == 2:
                    sp.dma_start(b_col[:], b_qkvT).then_inc(b_landed, 16)
                    sp.dma_start(bv_row[:], b_v.partition_broadcast(P)).then_inc(b_landed, 16)
            with sp.Fori(0, CH) as c:
                load_s(c + 1)
                for g in range(4):
                    sp.wait_ge(dve_out, c * 16 + (4 * g + 4 + DO))
                    sp.dma_start(qkv_out[bass.ds(c, 1), 2 + g].rearrange("a p k j -> p (a k) j"), stage_d[:]).then_inc(dve_stored, 16)
            sp.wait_ge(dve_stored, CH * 4 * 16 + ST)
            for comp in range(2):
                sp.wait_ge(s_landed[comp], (CH + 1) * 16)

        @block.scalar
        def _(act):
            act.sem_inc(act_out, AO)
            act.sem_inc(act_stored, ST)

            def high_s(c, buf):
                for comp in range(2):
                    act.wait_ge(s_landed[comp], c * 16 + 16)
                    for k in range(DT):
                        nc.scalar.activation(grouped(s_hi, buf, comp, k), by_group(s_raw[:, comp, k, :]), ACT.Copy).then_inc(s_hi_done, 1)

            def high_w(mat):
                act.wait_ge(w_landed[mat % 2], 16 * (mat // 2 + 1))
                for k in range(DT):
                    nc.scalar.activation(w_hi[:, mat, k, :], (stage_a, stage_d)[mat % 2][:, k, :], ACT.Copy).then_inc(w_hi_done, 1)

            high_w(0)
            high_s(0, 0)
            for mat in range(1, MATS):
                high_w(mat)
            act.wait_ge(b_landed, 32)
            act.wait_ge(w_lo_done, (MATS - 1) * DT)
            with act.Fori(0, CH // 2) as c2:
                for u in range(2):
                    c = act.snap(c2 * 2 + u)
                    for g in range(2):
                        act.wait_ge(mm_done, c * 6 + (g + 1 + MM))
                        act.wait_ge(act_stored, c * 48 + (16 * g + ST))
                        for f in range(4):
                            nc.scalar.activation(stage_a[:, f, :], banks[g][f][:], ACT.Identity,
                                                 bias=b_col[:, g, f:f + 1]).then_inc(act_out, 1)
                        act.wait_ge(act_out, c * 8 + (4 * g + 4 + AO))
                        act.dma_start(qkv_out[bass.ds(c, 1), g].rearrange("a p k j -> p (a k) j"), stage_a[:]).then_inc(act_stored, 16)
                    act.wait_ge(mm_done, c * 6 + MM)
                    high_s(c + 1, 1 - u)
                    act.wait_ge(dve_out, c * 16 + (8 + DO))
                    act.wait_ge(act_stored, c * 48 + (32 + ST))
                    nc.scalar.activation(stage_a[:], stage_d[:], ACT.Copy, scale=-1.0).then_inc(neg_out, 1)
                    act.wait_ge(neg_out, c + 1)
                    act.dma_start(qkv_out[bass.ds(c, 1), 6].rearrange("a p k j -> p (a k) j"), stage_a[:]).then_inc(act_stored, 16)
            act.wait_ge(act_stored, CH * 48 + ST)

        @block.vector
        def _(dve):
            dve.sem_inc(s_lo_done, SL)
            dve.sem_inc(dve_out, DO)
            dve.sem_inc(dve_stored, ST)

            def low_s(c, buf):
                for comp in range(2):
                    for k in range(DT):
                        dve.wait_ge(s_hi_done, c * 8 + (4 * comp + k + 1))
                        nc.vector.tensor_tensor(grouped(s_lo, buf, comp, k), by_group(s_raw[:, comp, k, :]),
                                                grouped(s_hi, buf, comp, k).bitcast(F32), ALU.subtract).then_inc(s_lo_done, 1)

            def low_w(mat):
                for k in range(DT):
                    dve.wait_ge(w_hi_done, DT * mat + k + 1)
                    nc.vector.tensor_tensor(w_lo[:, mat, k, :], (stage_a, stage_d)[mat % 2][:, k, :],
                                            w_hi[:, mat, k, :].bitcast(F32), ALU.subtract).then_inc(w_lo_done, 1)

            low_w(0)
            low_s(0, 0)
            for mat in range(1, MATS):
                low_w(mat)
            dve.wait_ge(b_landed, 32)
            dve.wait_ge(w_lo_done, MATS * DT)
            with dve.Fori(0, CH // 2) as c2:
                for u in range(2):
                    c = dve.snap(c2 * 2 + u)
                    for g in range(4):
                        dve.wait_ge(mm_done, c * 6 + (g + 3 + MM))
                        dve.wait_ge(dve_stored, c * 64 + (16 * g + ST))
                        if g == 2:
                            dve.wait_ge(neg_out, c + 1)
                        for f in range(4):
                            if g < 2:
                                nc.vector.tensor_scalar(stage_d[:, f, :], banks[g % 2][f][:], b_col[:, 2 + g, f:f + 1], None,
                                                        ALU.add).then_inc(dve_out, 1)
                            else:
                                nc.vector.tensor_tensor(stage_d[:, f, :], banks[g % 2][f][:], bv_row[:, g - 2, :],
                                                        ALU.add).then_inc(dve_out, 1)
                        if g == 1:
                            low_s(c + 1, 1 - u)

        @block.tensor
        def _(pe):
            pe.sem_inc(mm_done, MM)
            with pe.Fori(0, CH // 2) as c2:
                for u in range(2):
                    c = pe.snap(c2 * 2 + u)
                    for g in range(6):
                        if g in (2, 3):
                            pe.wait_ge(act_out, c * 8 + (4 * g - 4 + AO))
                        else:
                            pe.wait_ge(dve_out, c * 16 + {0: 12, 1: 16, 4: 4 + DO, 5: 8 + DO}[g])
                        comp = g % 2
                        for k in range(DT):
                            if u == 0:
                                pe.wait_ge(w_lo_done, DT * g + k + 1)
                            if g < 2:
                                pe.wait_ge(s_lo_done, c * 8 + (4 * comp + k + 1 + SL))
                            for t in range(4):
                                s = slice(P * t, P * t + P)
                                if g < 4:
                                    a = (w_hi[:, g, k, s], w_lo[:, g, k, s])
                                    b = (s_hi[:, u, comp, k, :], s_lo[:, u, comp, k, :])
                                else:
                                    a = (s_hi[:, u, comp, k, s], s_lo[:, u, comp, k, s])
                                    b = (w_hi[:, g, k, :], w_lo[:, g, k, :])
                                mm = product(nc, banks[g % 2][t][:], a, b, k == 0, k == DT - 1)
                        mm.then_inc(mm_done, 1)


def attention(nc, qkv_in, w_o, b_oT, attn_out):
    with ExitStack() as ctx:
        m = Mem(nc, ctx, "attn")
        G = P // 32
        SCALE = float(HD) ** -0.5
        w_hi = m.sb("w_hi", [P, 2, DT, 512], R32)
        w_lo = m.sb("w_lo", [P, 2, DT, 512], R32)
        q = m.sb("q", [P, H, 512])
        kk = m.sb("kk", [P, H, 2, 512])
        v = m.sb("v", [P, G, H, 2, HD])
        o_hi = m.sb("o_hi", [P, 2, DT, 512], R32)
        o_lo = m.sb("o_lo", [P, 2, DT, 512], R32)
        stage = m.sb("stage", [P, 2, DT, 512])
        masked = m.sb("masked", [P, 2, 512])
        mask = m.sb("mask", [P, 32])
        score = m.sb("score", [P, H * G * 8])
        square = m.sb("square", [P, H * G * 8])
        mag = m.sb("mag", [P, H * G, N])
        top = m.sb("top", [P, H * G])
        total = m.sb("total", [P, H * G])
        weight = m.sb("weight", [P, H * G, N])
        turned = m.sb("turned", [P, H * G, N])
        spread = m.sb("spread", [P, 8, 512])
        b_col = m.sb("b_col", [P, 2, DT])
        banks = [m.bank(f"bank{i}") for i in range(8)]

        def av_bank(h):
            return banks[(h + 4) % 8]

        b_landed, w_landed = m.sem("b_landed"), m.sem("w_landed")
        q_landed, v_landed = [m.sem(f"q_landed{i}") for i in range(2)], m.sem("v_landed")
        w_hi_done, w_lo_done, mask_done = m.sem("w_hi_done"), m.sem("w_lo_done"), m.sem("mask_done")
        pair_done, masked_done, score_done = m.sem("pair_done"), m.sem("masked_done"), m.sem("score_done")
        step, mag_done, exp_done, turned_done = m.sem("step"), m.sem("mag_done"), m.sem("exp_done"), m.sem("turned_done")
        sum_done = m.sem("sum_done")
        spread_low, spread_high, av_done, o_hi_done, o_lo_done = m.sem("spread_low"), m.sem("spread_high"), m.sem("av_done"), m.sem("o_hi_done"), m.sem("o_lo_done")
        wo_done, out_done = m.sem("wo_done"), m.sem("out_done")
        stored = [m.sem(f"stored{i}") for i in range(2)]
        block = ctx.enter_context(nc.Block())

        HEADS = [0, 2, 4, 6, 1, 3, 5, 7]
        STEPS = 6
        OD, ST = 8, 16

        @block.sync
        def _(sp):
            sp.dma_start(b_col[:], b_oT).then_inc(b_landed, 16)

            def rows(c, kind, half):
                return qkv_in[bass.ds(c, 1), kind, 64 * half:64 * half + 64].rearrange("a p f j -> p (a f) j")

            def load(c, waits):
                if waits:
                    sp.wait_ge(pair_done, c * 16)
                for half in range(2):
                    for comp in range(2):
                        part = slice(64 * comp, 64 * comp + 64)
                        sp.dma_start(q[part, half::2, :], rows(c, comp, half)).then_inc(q_landed[half], 16)
                        sp.dma_start(kk[part, half::2, 0, :], rows(c, 2 + comp, half)).then_inc(q_landed[half], 16)
                        sp.dma_start(kk[part, half::2, 1, :], rows(c, (6, 2)[comp], half)).then_inc(q_landed[half], 16)
                if waits:
                    sp.wait_ge(av_done, c * 8)
                for comp in range(2):
                    sp.dma_start(v[:, :, :, comp, :].rearrange("p g h d -> p (g h) d"),
                                 qkv_in[bass.ds(c, 1), 4 + comp].rearrange("a p g (h d) -> p (a g h) d", h=H)).then_inc(v_landed, 16)

            load(0, False)
            for mat in range(2):
                sp.dma_start(stage[:, mat, :, :], w_o[mat]).then_inc(w_landed, 16)
            with sp.Fori(1, CH) as c:
                load(c, True)

        def chunks(eng, first, rest, tail=None):
            first(0)
            with eng.Fori(1, CH) as c:
                rest(c)
            if tail:
                tail()

        def spread_heads(eng, hh, g):
            w = turned[:].rearrange("p (h g) n -> p h g n", g=G)[:, 4 * hh:4 * hh + 4, g, :]
            for j in range(4):
                ins = eng.tensor_tensor(spread[:, 4 * hh + g, P * j:P * j + P].rearrange("p (n t) -> p n t", n=N),
                                        w[:, j, :].unsqueeze(2).to_broadcast([P, N, 32]),
                                        mask[:].unsqueeze(1).to_broadcast([P, N, 32]), ALU.mult)
            return ins

        @block.gpsimd
        def _(pool):
            nc.gpsimd.memset(mask[:], 0.0).then_inc(mask_done, 1)
            pool.wait_ge(mask_done, 1)
            for n in range(N):
                if n:
                    pool.wait_ge(mask_done, n + 1)
                nc.gpsimd.affine_select(out=mask[:], in_=mask[:], compare_op=ALU.not_equal, fill=1.0, base=-32 * n,
                                        pattern=[[-1, 32]], channel_multiplier=1).then_inc(mask_done, 1)
            pool.wait_ge(mask_done, 5)

            def spread_out(c):
                pool.wait_ge(turned_done, (c + 1) * 16)
                for g in range(G):
                    spread_heads(nc.gpsimd, 1, g).then_inc(spread_high, 1)

            chunks(pool, spread_out, spread_out)

        @block.scalar
        def _(act):
            act.sem_inc(out_done, OD)
            for comp in range(2):
                act.sem_inc(stored[comp], ST)

            def magnitudes(c):
                act.wait_ge(step, c * STEPS + 2)
                nc.scalar.activation(mag[:], mag[:], ACT.Sqrt).then_inc(mag_done, 1)
                act.wait_ge(step, c * STEPS + 4)
                nc.scalar.activation(weight[:], mag[:], ACT.Exp, scale=SCALE).then_inc(exp_done, 1)

            def values(c):
                for h in range(H):
                    act.wait_ge(av_done, c * 8 + (h + 1))
                    for comp in range(2):
                        part, to = slice(64 * comp, 64 * comp + 64), slice(64 * (h % 2), 64 * (h % 2) + 64)
                        nc.scalar.activation(o_hi[to, comp, h // 2, :], av_bank(h)[part, :], ACT.Copy).then_inc(o_hi_done, 1)

            def outputs(c):
                for comp in range(2):
                    act.wait_ge(wo_done, c * 2 + (comp + 1))
                    act.wait_ge(stored[comp], c * 16 + ST)
                    for f in range(4):
                        nc.scalar.activation(stage[:, comp, f, :].rearrange("p (n g t) -> p n g t", n=N, g=G),
                                             banks[4 - 4 * comp + f][:].rearrange("p (g n t) -> p n g t", n=N, g=G), ACT.Identity,
                                             bias=b_col[:, comp, f:f + 1]).then_inc(out_done, 1)
                    act.wait_ge(out_done, c * 8 + (4 * comp + 4 + OD))
                    act.dma_start(attn_out[bass.ds(c, 1), comp].rearrange("a p f j -> p (a f) j"),
                                  stage[:, comp, :, :]).then_inc(stored[comp], 16)

            def first(c):
                magnitudes(c)
                for mat in range(2):
                    act.wait_ge(w_landed, 32)
                    nc.scalar.activation(w_hi[:, mat, :, :], stage[:, mat, :, :], ACT.Copy).then_inc(w_hi_done, 1)
                act.wait_ge(b_landed, 16)
                values(c)
                act.wait_ge(w_lo_done, 2)

            def rest(c):
                magnitudes(c)
                outputs(c - 1)
                values(c)

            chunks(act, first, rest, lambda: outputs(CH - 1))
            for comp in range(2):
                act.wait_ge(stored[comp], CH * 16 + ST)

        @block.vector
        def _(dve):
            dve.wait_ge(mask_done, 5)

            def scores(c):
                for i in range(16):
                    dve.wait_ge(pair_done, c * 16 + (i + 1))
                    nc.vector.tensor_tensor(masked[:, i % 2, :].rearrange("p (a t) -> p a t", t=32),
                                            banks[i % 4][:].rearrange("p (a t) -> p a t", t=32),
                                            mask[:].unsqueeze(1).to_broadcast([P, 16, 32]), ALU.mult).then_inc(masked_done, 1)
                    dve.wait_ge(masked_done, c * 16 + (i + 1))
                    at = 16 * (2 * HEADS[i // 2] + i % 2)
                    nc.vector.tensor_reduce(score[:, at:at + 16], masked[:, i % 2, :].rearrange("p (a t) -> p a t", t=32),
                                            AX.X, ALU.add).then_inc(score_done, 1)

            def softmax(c):
                b = c * STEPS
                dve.wait_ge(score_done, c * 16 + 16)
                nc.vector.tensor_tensor(square[:], score[:], score[:], ALU.mult).then_inc(step, 1)
                dve.wait_ge(step, b + 1)
                parts = square[:].rearrange("p (a w n) -> p a w n", w=2, n=N)
                nc.vector.scalar_tensor_tensor(out=mag[:], in0=parts[:, :, 0, :], scalar=1e-8, in1=parts[:, :, 1, :],
                                               op0=ALU.add, op1=ALU.add).then_inc(step, 1)
                dve.wait_ge(mag_done, c + 1)
                nc.vector.tensor_reduce(top[:], mag[:], AX.X, ALU.max).then_inc(step, 1)
                dve.wait_ge(step, b + 3)
                nc.vector.tensor_tensor(mag[:], mag[:], top[:].unsqueeze(2).to_broadcast([P, H * G, N]),
                                        ALU.subtract).then_inc(step, 1)
                dve.wait_ge(exp_done, c + 1)
                nc.vector.tensor_reduce(total[:], weight[:], AX.X, ALU.add).then_inc(sum_done, 1)
                dve.wait_ge(sum_done, c + 1)
                nc.vector.reciprocal(total[:], total[:]).then_inc(step, 1)
                dve.wait_ge(step, b + 5)
                nc.vector.tensor_tensor(weight[:], weight[:], total[:].unsqueeze(2).to_broadcast([P, H * G, N]),
                                        ALU.mult).then_inc(step, 1)
                dve.wait_ge(step, b + 6)
                for n in range(N):
                    for k in range(N):
                        nc.vector.tensor_copy(turned[32 * k:32 * k + 32, :, n], weight[32 * n:32 * n + 32, :, k]).then_inc(turned_done, 1)
                dve.wait_ge(turned_done, (c + 1) * 16)
                for g in range(G):
                    spread_heads(nc.vector, 0, g).then_inc(spread_low, 1)

            def values(c):
                for h in range(H):
                    for comp in range(2):
                        dve.wait_ge(o_hi_done, c * 16 + (2 * h + comp + 1))
                        part, to = slice(64 * comp, 64 * comp + 64), slice(64 * (h % 2), 64 * (h % 2) + 64)
                        nc.vector.tensor_tensor(o_lo[to, comp, h // 2, :], av_bank(h)[part, :],
                                                o_hi[to, comp, h // 2, :].bitcast(F32), ALU.subtract).then_inc(o_lo_done, 1)

            def whole(c):
                scores(c)
                softmax(c)
                values(c)

            def first(c):
                scores(c)
                softmax(c)
                for mat in range(2):
                    dve.wait_ge(w_hi_done, mat + 1)
                    nc.vector.tensor_tensor(w_lo[:, mat, :, :], stage[:, mat, :, :], w_hi[:, mat, :, :].bitcast(F32),
                                            ALU.subtract).then_inc(w_lo_done, 1)
                values(c)

            chunks(dve, first, whole)

        @block.tensor
        def _(pe):
            def scores(c, between):
                for i in range(16):
                    h, pair = HEADS[i // 2], i % 2
                    if i % 8 == 0:
                        pe.wait_ge(q_landed[h % 2], (c + 1) * (6 * 16))
                    if i >= 4 or type(c) is not int:
                        pe.wait_ge(masked_done, c * 16 + (i - 3))
                    if i < 4 and type(c) is not int:
                        pe.wait_ge(o_lo_done, c * 16 + (2 * i - 6))
                    for gi in range(2):
                        s = slice(P * (2 * pair + gi), P * (2 * pair + gi) + P)
                        mm = nc.tensor.matmul(banks[i % 4][:, 256 * gi:256 * gi + 256].rearrange("p (w r) -> p w r", w=2),
                                              q[:, h, s], kk[:, h, :, s], start=True, stop=True)
                    mm.then_inc(pair_done, 1)
                    between(i)

            def values(c):
                pe.wait_ge(v_landed, (c + 1) * 32)
                if type(c) is not int:
                    pe.wait_ge(out_done, c * 8 + 4)
                for hh, spread_done in enumerate((spread_low, spread_high)):
                    for g in range(G):
                        pe.wait_ge(spread_done, c * G + (g + 1))
                        if hh and not g and type(c) is not int:
                            pe.wait_ge(out_done, c * 8 + 8)
                        for j in range(4):
                            h = 4 * hh + j
                            mm = nc.tensor.matmul(av_bank(h)[:, P * g:P * g + P], v[:, g, h, :, :].rearrange("p w d -> p (w d)"),
                                                  spread[:, 4 * hh + g, P * j:P * j + P], start=True, stop=True)
                            if g == G - 1:
                                mm.then_inc(av_done, 1)

            def output(c, comp, k, f):
                if not comp and (not k or not f):
                    pe.wait_ge(o_lo_done, c * 16 + max(4 * k + 4, 2 * f + 2))
                s = slice(P * f, P * f + P)
                mm = product(nc, banks[4 - 4 * comp + f][:], (w_hi[:, comp, k, s], w_lo[:, comp, k, s]),
                             (o_hi[:, comp, k, :], o_lo[:, comp, k, :]), k == 0, k == DT - 1)
                if (k, f) == (DT - 1, 3):
                    mm.then_inc(wo_done, 1)

            def outputs(c, comp):
                for k in range(DT):
                    for f in range(4):
                        if comp and not k:
                            pe.wait_ge(masked_done, CH * 16 if type(c) is int else c * 16 + (16 + 13 + f))
                        output(c, comp, k, f)

            def first(c):
                scores(c, lambda i: None)
                values(c)
                pe.wait_ge(w_lo_done, 2)

            def rest(c):
                BETWEEN = (4, 5, 7, 8, 10, 11, 13, 14)
                for at in range(8):
                    output(c - 1, 0, at // 4, at % 4)

                def between(i):
                    if i in BETWEEN:
                        at = 8 + BETWEEN.index(i)
                        output(c - 1, 0, at // 4, at % 4)

                scores(c, between)
                outputs(c - 1, 1)
                values(c)

            def tail():
                outputs(CH - 1, 0)
                outputs(CH - 1, 1)

            chunks(pe, first, rest, tail)


def superposition(nc, attn_in, w_int, ids, tables, sup_out, xT, w_top, top_out):
    with ExitStack() as ctx:
        m = Mem(nc, ctx, "sup")
        W = D // N
        a_raw = m.sb("a_raw", [P, 2, 2, DT, P])
        a_hi = m.sb("a_hi", [P, 2, 2, DT, P], R32)
        a_lo = m.sb("a_lo", [P, 2, 2, DT, P], R32)
        ri = m.sb("ri", [P, 2, N, 2, 512])
        part = m.sb("part", [P, 512])
        mag = m.sb("mag", [P, 2, N, W])
        u = m.sb("u", [P, 2, N, W])
        cos = m.sb("cos", [P, 6, W])
        cos_i = m.sb("cos_i", [P, 6, W])
        g = m.sb("g", [P, N, W])
        sup = m.sb("sup", [P, 2, 512])
        index = m.sb("index", [P, CH, N], I32)
        strengths = m.sb("strengths", [P, CH, N, N])
        strength = m.sb("strength", [P, N, N])
        norm = m.sb("norm", [P, 3])
        eps = m.sb("eps", [P, 1])
        banks = [m.bank(f"bank{i}") for i in range(8)]
        with ExitStack() as until_used:
            weights = Mem(nc, until_used, "sup")
            w_hi = weights.sb("w_hi", [P, 2 * N, DT, 512], R32)
            w_lo = weights.sb("w_lo", [P, 2 * N, DT, 512], R32)
        SLOTS, WIDE = 4, 1 + HALVES
        top_raw = m.sb("top_raw", [P, SLOTS, WIDE, 512])
        top_hi = m.sb("top_hi", [P, SLOTS, WIDE, 512], R32)
        top_lo = m.sb("top_lo", [P, SLOTS, WIDE, 512], R32)
        top_stage = m.sb("top_stage", [P, HALVES, DT, 512])
        TOP_BANKS = [[6, 7, 0, 1], [2, 3, 4, 5]]
        STEPS_AT = [(1, 3), (3, 5), (5, 7), (7, 9), (9, 11), (11, KT)]

        index_landed, strengths_landed = m.sem("index_landed"), m.sem("strengths_landed")
        w_landed = [m.sem(f"w_landed{i}") for i in range(4)]
        a_landed = [m.sem(f"a_landed{i}") for i in range(2)]
        w_hi_done, w_lo_done, a_hi_done, a_lo_done = m.sem("w_hi_done"), m.sem("w_lo_done"), m.sem("a_hi_done"), m.sem("a_lo_done")
        mm_done, part_done, i_out, r_out = m.sem("mm_done"), m.sem("part_done"), m.sem("i_out"), m.sem("r_out")
        sq_done, m2_done, mag_done, inv_done = m.sem("sq_done"), m.sem("m2_done"), m.sem("mag_done"), m.sem("inv_done")
        unit_r, unit_i, cos_r_done, cos_i_done = m.sem("unit_r"), m.sem("unit_i"), m.sem("cos_r_done"), m.sem("cos_i_done")
        cos_sum, cos_done, strength_done = m.sem("cos_sum"), m.sem("cos_done"), m.sem("strength_done")
        g_begun, g_step, r_step, i_step = m.sem("g_begun"), m.sem("g_step"), m.sem("r_step"), m.sem("i_step")
        eps_set, norm_sum, norm_root, norm_done, sup_done = (m.sem(x) for x in (
            "eps_set", "norm_sum", "norm_root", "norm_done", "sup_done"))
        stored = m.sem("stored")
        top_landed = [m.sem(f"top_landed{i}") for i in range(SLOTS)]
        top_hi_done, top_low_w, top_low_x, top_used = m.sem("top_hi_done"), m.sem("top_low_w"), m.sem("top_low_x"), m.sem("top_used")
        top_half, top_staged, top_stored = m.sem("top_half"), m.sem("top_staged"), m.sem("top_stored")
        block = ctx.enter_context(nc.Block())
        MM, OUT, STEP, UNIT, SUM, ST = 3, 2, 3, 2, 2, 16

        PAIRS = [(0, 1), (1, 2), (2, 3), (0, 2), (1, 3), (0, 3)]
        OTHERS = [(1, 2, 3), (0, 2, 3), (1, 0, 3), (2, 0, 1)]

        def pair(i, j):
            return cos[:, PAIRS.index((min(i, j), max(i, j))), :]

        def products(eng, out, x):
            eng.tensor_tensor(out[:, 0:3], x[:, 0:3], x[:, 1:4], ALU.mult)
            eng.tensor_tensor(out[:, 3:5], x[:, 0:2], x[:, 2:4], ALU.mult)
            return eng.tensor_tensor(out[:, 5:6], x[:, 0:1], x[:, 3:4], ALU.mult)

        def units(eng, unit, magnitude, quarter, top_step):
            def work(c, par, n, known):
                def do(meanwhile=lambda: None):
                    if n == 0:
                        if known >= 2:
                            quarter(c - 2, par, N - 1, c - 1, meanwhile)
                        else:
                            if known == 1:
                                magnitude(c - 1, 1 - par, 0)
                            meanwhile()
                    elif known >= 1:
                        quarter(c - 1, 1 - par, n - 1, c - 1, meanwhile)
                    else:
                        meanwhile()
                return do

            for c in (0, 1):
                for n in range(N):
                    unit(c, c, n, work(c, c, n, c))
            with eng.Fori(1, CH // 2) as c2:
                for par in (0, 1):
                    c = eng.snap(c2 * 2 + par)
                    for n in range(N):
                        unit(c, par, n, work(c, par, n, 2))
            top_step(0)
            for n in range(N + 1):
                def steps():
                    for k in range(*STEPS_AT[n]):
                        top_step(k)

                if n < N:
                    work(CH, 0, n, 2)(steps)
                else:
                    quarter(CH - 1, 1, N - 1, None, steps)

        def slot(mat):
            return ri[:, mat // 2 % 2, 2 * (mat % 2):2 * (mat % 2) + 2].rearrange("p n w j -> p (n w j)")

        @block.sync
        def _(sp):
            def load_a(c, n):
                for comp in range(2):
                    sp.dma_start(a_raw[:, n % 2, comp], attn_in[bass.ds(c, 1), comp, :, :, P * n:P * n + P].rearrange("a p f t -> p (a f) t")
                                 ).then_inc(a_landed[n % 2], 16)

            def load_w(mat):
                sp.dma_start(slot(mat), w_int[mat]).then_inc(w_landed[mat % 4], 16)

            load_a(0, 0)
            for mat in range(4):
                load_w(mat)
            load_a(0, 1)
            sp.dma_start(index[:], ids).then_inc(index_landed, 16)
            for mat in range(4, 8):
                sp.wait_ge(w_lo_done, DT * (mat - 3))
                load_w(mat)
            with sp.Fori(0, CH) as c:
                for n in range(N):
                    sp.wait_ge(a_lo_done, c * N + (n + 1))
                    load_a(c if n < 2 else (c + 1) % CH, (n + 2) % N)
            sp.wait_ge(mm_done, (CH * N - 2) * 3 + MM)
            for k in range(KT):
                if k >= SLOTS:
                    sp.wait_ge(top_low_w, k - SLOTS + 1)
                    sp.wait_ge(top_low_x, k - SLOTS + 1)
                sp.dma_start(top_raw[:, k % SLOTS, 0, :], w_top[k]).then_inc(top_landed[k % SLOTS], 16)
                sp.dma_start(top_raw[:, k % SLOTS, 1:WIDE, :],
                             xT.rearrange("(h k) p t -> k p h t", h=HALVES)[k]).then_inc(top_landed[k % SLOTS], 16)
            for s in range(2):
                sp.wait_ge(a_landed[s], (CH * 2 + 1) * 32)

        @block.gpsimd
        def _(pool):
            def low_a(c, n):
                pool.wait_ge(a_hi_done, c * N + (n + 1))
                nc.gpsimd.tensor_tensor(a_lo[:, n % 2], a_raw[:, n % 2], a_hi[:, n % 2].bitcast(F32),
                                        ALU.subtract).then_inc(a_lo_done, 1)

            def magnitude(c, par, q):
                pool.wait_ge(sq_done, c * N + (q + 1))
                nc.gpsimd.tensor_tensor(mag[:, q % 2], mag[:, q % 2], u[:, 1], ALU.add).then_inc(m2_done, 1)

            def quarter(c, par, q, of, meanwhile):
                s = c * N + q
                ci = ri[:, par, :, 1, W * q:W * q + W]
                if of is not None:
                    pool.wait_ge(m2_done, s + 2)
                pool.wait_ge(inv_done, s + 1)
                nc.gpsimd.tensor_tensor(u[:, 1], ci, mag[:, q % 2], ALU.mult).then_inc(unit_i, 1)
                pool.wait_ge(unit_i, s + (1 + UNIT))
                pool.wait_ge(cos_sum, s * 2 + SUM)
                products(nc.gpsimd, cos_i, u[:, 1]).then_inc(cos_i_done, 1)
                meanwhile()
                pool.wait_ge(g_step, s * 8 + 8)
                nc.gpsimd.tensor_tensor(ci, ci, g[:], ALU.mult).then_inc(i_step, 1)
                if not (type(c) is int and c == CH - 1 and q >= N - 2):
                    magnitude(c + (q + 2) // N, None, (q + 2) % N)
                pool.wait_ge(i_step, s * 3 + (STEP + 1))
                nc.gpsimd.tensor_tensor(ci[:, 0:2], ci[:, 0:2], ci[:, 2:4], ALU.add).then_inc(i_step, 1)
                pool.wait_ge(i_step, s * 3 + (STEP + 2))
                if q == 0:
                    pool.wait_ge(stored, c * 16 + ST)
                nc.gpsimd.tensor_tensor(sup[:, 1, W * q:W * q + W], ci[:, 0, :], ci[:, 1, :], ALU.add).then_inc(i_step, 1)

            def unit(c, par, n, work):
                if type(c) is not int or c:
                    work(lambda: low_a(c + (n + 1) // N, (n + 1) % N))
                else:
                    work()
                if type(c) is int and c == 1 and n == 0:
                    magnitude(0, None, 1)

            pool.sem_inc(i_step, STEP)
            pool.sem_inc(unit_i, UNIT)
            pool.sem_inc(cos_i_done, 1)
            nc.gpsimd.memset(eps[:], 1e-8).then_inc(eps_set, 1)
            pool.wait_ge(index_landed, 16)
            for c in range(CH):
                for f in range(N):
                    nc.gpsimd.indirect_dma_start(out=strengths[:, c, f, :], out_offset=None, in_=tables[f],
                                                 in_offset=bass.IndirectOffsetOnAxis(ap=index[:, c, f:f + 1], axis=0)
                                                 ).then_inc(strengths_landed, 16)

            def top_step(k):
                pool.wait_ge(top_hi_done, k + 1)
                nc.gpsimd.tensor_tensor(top_lo[:, k % SLOTS, WIDE - 1, :], top_raw[:, k % SLOTS, WIDE - 1, :],
                                        top_hi[:, k % SLOTS, WIDE - 1, :].bitcast(F32), ALU.subtract).then_inc(top_low_x, 1)

            units(pool, unit, magnitude, quarter, top_step)
            for k in range(*STEPS_AT[N + 1]):
                top_step(k)

        @block.scalar
        def _(act):
            act.sem_inc(i_out, OUT)
            act.sem_inc(stored, ST)

            def high_a(c, n):
                act.wait_ge(a_landed[n % 2], c * 64 + 32 * (n // 2 + 1))
                act.wait_ge(mm_done, c * 12 + (3 * n - 3 + MM))
                nc.scalar.activation(a_hi[:, n % 2], a_raw[:, n % 2], ACT.Copy).then_inc(a_hi_done, 1)

            def high_w(mat):
                act.wait_ge(w_landed[mat % 4], 16 * (mat // 4 + 1))
                for k in range(DT):
                    nc.scalar.activation(w_hi[:, mat, k, :], slot(mat)[:, 512 * k:512 * k + 512], ACT.Copy).then_inc(w_hi_done, 1)

            def magnitude(c, par, q):
                s, cols = c * N + q, slice(W * q, W * q + W)
                if q == 0:
                    act.wait_ge(r_out, c * 4 + (4 + OUT))
                    act.wait_ge(i_out, c * 4 + (4 + OUT))
                act.wait_ge(unit_r, s + (UNIT - 1))
                act.wait_ge(unit_i, s + (UNIT - 1))
                if type(c) is not int or s:
                    act.wait_ge(cos_i_done, s)
                nc.scalar.activation(mag[:, q % 2], ri[:, par, :, 0, cols], ACT.Square)
                nc.scalar.activation(u[:, 1], ri[:, par, :, 1, cols], ACT.Square).then_inc(sq_done, 1)
                act.wait_ge(m2_done, s + 1)
                nc.scalar.activation(mag[:, q % 2], mag[:, q % 2], ACT.Sqrt).then_inc(mag_done, 1)

            def begin_g(c, q):
                s = c * N + q
                act.wait_ge(r_step, s * 3 + 1)
                act.wait_ge(i_step, s * 3 + 1)
                if q == 0:
                    act.wait_ge(strengths_landed, CH * N * 16)
                    nc.scalar.activation(strength[:], strengths[:, bass.ds(c, 1)].rearrange("p a i j -> p (a i) j"),
                                         ACT.Copy).then_inc(strength_done, 1)
                    act.wait_ge(strength_done, c + 1)
                act.wait_ge(cos_done, s * 2 + 1)
                for j in range(N):
                    i = OTHERS[j][0]
                    nc.scalar.activation(g[:, j, :], pair(i, j), ACT.Identity, bias=strength[:, j, j:j + 1],
                                         scale=strength[:, i, j:j + 1]).then_inc(g_begun, 1)

            def norm_of(c, outs):
                act.wait_ge(r_step, c * 12 + (12 + STEP))
                act.wait_ge(i_step, c * 12 + (12 + STEP))
                act.wait_ge(r_out, outs + OUT)
                for w in range(2):
                    if w:
                        act.wait_ge(norm_sum, c * 3 + 1)
                    nc.scalar.activation(part[:], sup[:, w, :], ACT.Square,
                                         accum_out=norm[:, w:w + 1]).then_inc(norm_sum, 1)
                act.wait_ge(norm_sum, c * 3 + 2)
                nc.scalar.activation(norm[:, 1:2], norm[:, 1:2], ACT.Identity, bias=eps[:, 0:1]).then_inc(norm_sum, 1)
                act.wait_ge(norm_sum, c * 3 + 3)
                nc.scalar.activation(norm[:, 0:1], norm[:, 0:1], ACT.Sqrt, bias=norm[:, 1:2]).then_inc(norm_root, 1)
                act.wait_ge(norm_done, c + 1)
                flat = sup[:].rearrange("p w j -> p (w j)")
                nc.scalar.activation(flat, flat, ACT.Copy, scale=norm[:, 2:3]).then_inc(sup_done, 1)
                act.wait_ge(sup_done, c + 1)
                act.dma_start(sup_out[bass.ds(c, 1)].rearrange("a p j -> p (a j)"), flat).then_inc(stored, 16)

            def quarter(c, par, q, of, meanwhile):
                if of is not None:
                    magnitude(of, par if q < N - 1 else 1 - par, (q + 1) % N)
                meanwhile()
                if q == 0 and (type(c) is not int or c):
                    norm_of(c - 1, CH * N if type(c) is int and c == CH - 1 else c * 4 + 5)
                begin_g(c, q)

            act.wait_ge(a_landed[0], 32)
            nc.scalar.activation(a_hi[:, 0], a_raw[:, 0], ACT.Copy).then_inc(a_hi_done, 1)
            for mat in range(8):
                high_w(mat)
                if mat == 1:
                    high_a(0, 1)
            act.wait_ge(eps_set, 1)
            act.wait_ge(w_lo_done, 8 * DT)

            def imaginary_out(c, par, n):
                act.wait_ge(mm_done, c * 12 + (3 * n + 3 + MM))
                if n == 0 and (type(c) is not int or c >= 2):
                    act.wait_ge(i_step, c * 12 + (STEP - 12))
                nc.scalar.activation(ri[:, par, n, 1, :], banks[n % 2 * 3 + 2][:], ACT.Copy).then_inc(i_out, 1)

            def unit(c, par, n, work):
                if type(c) is not int or c or n:
                    high_a(c + (n + 1) // N, (n + 1) % N)
                if n == 1:
                    work(lambda: imaginary_out(c, par, 0))
                else:
                    work()
                act.wait_ge(mm_done, c * 12 + (3 * n + 2 + MM))
                act.wait_ge(r_out, c * 4 + (n + OUT))
                nc.scalar.activation(part[:], banks[n % 2 * 3 + 1][:], ACT.Copy).then_inc(part_done, 1)
                if n:
                    imaginary_out(c, par, n)

            def top_step(k):
                act.wait_ge(top_landed[k % SLOTS], 32 * (k // SLOTS + 1))
                if k >= SLOTS:
                    act.wait_ge(top_used, k - SLOTS + 1)
                nc.scalar.activation(top_hi[:, k % SLOTS], top_raw[:, k % SLOTS], ACT.Copy).then_inc(top_hi_done, 1)

            units(act, unit, magnitude, quarter, top_step)
            for k in range(*STEPS_AT[N + 1]):
                if k == STEPS_AT[N + 1][0] + 1:
                    norm_of(CH - 1, CH * N)
                top_step(k)
            for h in range(HALVES):
                act.wait_ge((top_half, top_used)[h], (1, KT)[h])
                for f in range(DT):
                    nc.scalar.activation(top_stage[:, h, f, :], banks[TOP_BANKS[h][f]][:], ACT.Copy).then_inc(top_staged, 1)
                act.wait_ge(top_staged, DT * (h + 1))
                act.dma_start(top_out[h], top_stage[:, h]).then_inc(top_stored, 16)
            act.wait_ge(stored, CH * 16 + ST)
            act.wait_ge(top_stored, HALVES * 16)

        @block.vector
        def _(dve):
            dve.sem_inc(r_out, OUT)
            dve.sem_inc(r_step, STEP)
            dve.sem_inc(unit_r, UNIT)
            dve.sem_inc(cos_sum, SUM)

            def low_w(mat):
                for k in range(DT):
                    dve.wait_ge(w_hi_done, DT * mat + k + 1)
                    nc.vector.tensor_tensor(w_lo[:, mat, k, :], slot(mat)[:, 512 * k:512 * k + 512],
                                            w_hi[:, mat, k, :].bitcast(F32), ALU.subtract).then_inc(w_lo_done, 1)

            def low_a(c, n):
                dve.wait_ge(a_hi_done, c * N + (n + 1))
                nc.vector.tensor_tensor(a_lo[:, n % 2], a_raw[:, n % 2], a_hi[:, n % 2].bitcast(F32),
                                        ALU.subtract).then_inc(a_lo_done, 1)

            def norm_of(c):
                dve.wait_ge(norm_root, c + 1)
                nc.vector.reciprocal(norm[:, 2:3], norm[:, 0:1]).then_inc(norm_done, 1)

            def magnitude(c, par, q):
                dve.wait_ge(mag_done, c * N + (q + 1))
                nc.vector.reciprocal(mag[:, q % 2], mag[:, q % 2]).then_inc(inv_done, 1)

            def quarter(c, par, q, of, meanwhile):
                s = c * N + q
                cr = ri[:, par, :, 0, W * q:W * q + W]
                dve.wait_ge(inv_done, s + 1)
                nc.vector.tensor_tensor(u[:, 0], cr, mag[:, q % 2], ALU.mult).then_inc(unit_r, 1)
                dve.wait_ge(unit_r, s + (1 + UNIT))
                products(nc.vector, cos, u[:, 0]).then_inc(cos_r_done, 1)
                if of is not None:
                    magnitude(of, None, (q + 1) % N)
                meanwhile()
                if q == 0 and (type(c) is not int or c):
                    norm_of(c - 1)
                dve.wait_ge(cos_r_done, s + 1)
                dve.wait_ge(cos_i_done, s + 2)
                for some in (slice(0, 3), slice(3, 6)):
                    nc.vector.tensor_tensor(cos[:, some], cos[:, some], cos_i[:, some], ALU.add).then_inc(cos_sum, 1)
                for i, some in enumerate((slice(0, 3), slice(3, 6))):
                    dve.wait_ge(cos_sum, s * 2 + (i + 1 + SUM))
                    nc.vector.tensor_scalar(cos[:, some], cos[:, some], 1.0, None, ALU.min).then_inc(cos_done, 1)
                dve.wait_ge(cos_done, s * 2 + 2)
                for k in (1, 2):
                    for j in range(N):
                        i = OTHERS[j][k]
                        if k == 1:
                            dve.wait_ge(g_begun, s * 4 + (j + 1))
                        else:
                            dve.wait_ge(g_step, s * 8 + (j + 1))
                        nc.vector.scalar_tensor_tensor(out=g[:, j, :], in0=pair(i, j), scalar=strength[:, i, j:j + 1],
                                                       in1=g[:, j, :], op0=ALU.mult, op1=ALU.add).then_inc(g_step, 1)
                dve.wait_ge(g_step, s * 8 + 8)
                nc.vector.tensor_tensor(cr, cr, g[:], ALU.mult).then_inc(r_step, 1)
                dve.wait_ge(r_step, s * 3 + (STEP + 1))
                nc.vector.tensor_tensor(cr[:, 0:2], cr[:, 0:2], cr[:, 2:4], ALU.add).then_inc(r_step, 1)
                dve.wait_ge(r_step, s * 3 + (STEP + 2))
                if q == 0:
                    dve.wait_ge(stored, c * 16 + ST)
                nc.vector.tensor_tensor(sup[:, 0, W * q:W * q + W], cr[:, 0, :], cr[:, 1, :], ALU.add).then_inc(r_step, 1)

            low_a(0, 0)
            for mat in range(8):
                low_w(mat)
                if mat == 1:
                    low_a(0, 1)

            def unit(c, par, n, work):
                if type(c) is int and not c and n:
                    low_a(c + (n + 1) // N, (n + 1) % N)
                work()
                dve.wait_ge(mm_done, c * 12 + (3 * n + 1 + MM))
                dve.wait_ge(part_done, c * 4 + (n + 1))
                if n == 0 and (type(c) is not int or c >= 2):
                    dve.wait_ge(r_step, c * 12 + (STEP - 12))
                nc.vector.tensor_tensor(ri[:, par, n, 0, :], banks[n % 2 * 3][:], part[:], ALU.subtract).then_inc(r_out, 1)

            def top_step(k):
                dve.wait_ge(top_hi_done, k + 1)
                if k >= SLOTS:
                    dve.wait_ge(top_used, k - SLOTS + 1)
                nc.vector.tensor_tensor(top_lo[:, k % SLOTS, 0:WIDE - 1, :], top_raw[:, k % SLOTS, 0:WIDE - 1, :],
                                        top_hi[:, k % SLOTS, 0:WIDE - 1, :].bitcast(F32), ALU.subtract).then_inc(top_low_w, 1)

            units(dve, unit, magnitude, quarter, top_step)
            for k in range(*STEPS_AT[N + 1]):
                if k == STEPS_AT[N + 1][0] + 1:
                    norm_of(CH - 1)
                top_step(k)

        @block.tensor
        def _(pe):
            pe.sem_inc(mm_done, MM)

            def chunk(c, first):
                for n in range(N):
                    pe.wait_ge(a_lo_done, c * N + (n + 1))
                    pe.wait_ge(r_out, c * 4 + (n - 1 + OUT))
                    pe.wait_ge(i_out, c * 4 + (n - 1 + OUT))
                    for x, terms in enumerate((((0, 0),), ((1, 1),), ((0, 1), (1, 0)))):
                        for i, (comp, w) in enumerate(terms):
                            for k in range(DT):
                                if first and x < 2:
                                    pe.wait_ge(w_lo_done, DT * (2 * n + x) + k + 1)
                                mm = product(nc, banks[n % 2 * 3 + x][:], (a_hi[:, n % 2, comp, k, :], a_lo[:, n % 2, comp, k, :]),
                                             (w_hi[:, 2 * n + w, k, :], w_lo[:, 2 * n + w, k, :]),
                                             i == 0 and k == 0, i == len(terms) - 1 and k == DT - 1)
                        mm.then_inc(mm_done, 1)

            chunk(0, True)
            with pe.Fori(1, CH) as c:
                chunk(c, False)
            for k in range(KT):
                pe.wait_ge(top_low_w, k + 1)
                pe.wait_ge(top_low_x, k + 1)
                for h in range(HALVES):
                    if k == 0 and h == 1:
                        pe.wait_ge(r_out, CH * N + OUT)
                        pe.wait_ge(i_out, CH * N + OUT)
                    for f in range(DT):
                        s = slice(P * f, P * f + P)
                        mm = product(nc, banks[TOP_BANKS[h][f]][:], (top_hi[:, k % SLOTS, 0, s], top_lo[:, k % SLOTS, 0, s]),
                                     (top_hi[:, k % SLOTS, 1 + h, :], top_lo[:, k % SLOTS, 1 + h, :]), k == 0, k == KT - 1)
                    if h == 0 and k == KT - 1:
                        mm.then_inc(top_half, 1)
                mm.then_inc(top_used, 1)


def tower(nc, sup_in, top_in, w_tail, b_post, g_postT, be_postT, b1T, b2T, w3, y_out):
    with ExitStack() as ctx:
        m = Mem(nc, ctx, "tower")
        RAW, RING = 3, 6
        sup = m.sb("sup", [P, 4, 2 * D])
        sup_hi = m.sb("sup_hi", [P, 2 * DT, HALF], R32)
        sup_lo = m.sb("sup_lo", [P, 2 * DT, HALF], R32)
        w_raw = m.sb("w_raw", [P, RAW, 2, 512])
        w_hi = m.sb("w_hi", [P, RING, 512], R32)
        w_lo = m.sb("w_lo", [P, RING, 512], R32)
        top_x = m.sb("top_x", [P, DT, HALF])
        square_r = m.sb("square_r", [P, DT, HALF])
        square_i = m.sb("square_i", [P, 2, HALF])
        f32 = m.sb("f32", [P, DT, HALF])
        y_hi = [m.sb(f"y_hi{i}", [P, DT, HALF], R32) for i in range(3)]
        y_lo = [m.sb(f"y_lo{i}", [P, DT, HALF], R32) for i in range(3)]
        post = m.sb("post", [P, 4, D])
        h2 = m.sb("h2", [P, 2, HALF])
        y = m.sb("y", [1, HALF])
        ident = m.sb("ident", [P, P])
        post_row = m.sb("post_row", [P, D])
        stats = m.sb("stats", [P, 4, 6])
        mean_var = m.sb("mean_var", [P, 4, 2])
        std = m.sb("std", [P, 4])
        rstd = m.sb("rstd", [P, 4])
        gain = m.sb("gain", [P, DT])
        shift = m.sb("shift", [P, DT])
        b1 = m.sb("b1", [P, DT])
        b2 = m.sb("b2", [P, 2])
        w3_col = m.sb("w3_col", [P, 2])
        banks = [m.bank(f"bank{i}") for i in range(8)]

        TILES = ([("mr", k, 1) for k in range(4)] + [("mr", 4 + k, -1) for k in range(4)]
                 + [("mi", 4 + k, 1) for k in range(4)] + [("mi", k, 1) for k in range(4)]
                 + [("post", k, 1) for k in range(4)] + [("z", k, 1) for k in range(4)]
                 + [("top2", k, 1) for k in range(2)])
        PAIRS = [0, 1, 2, 3, 0, 1, 2, 3, 4, 5, 6, 7, 8]
        NT = len(TILES)
        FIRST = {layer: [t[0] for t in TILES].index(layer) for layer in ("mr", "mi", "post", "z", "top2")}

        c_landed, ident_ready = m.sem("c_landed"), m.sem("ident_ready")
        sup_landed = [m.sem(f"sup_landed{i}") for i in range(2)]
        w_landed = [m.sem(f"w_landed{i}") for i in range(RAW)]
        top_landed, top_added = m.sem("top_landed"), m.sem("top_added")
        w_hi_done, w_lo_done, w_used = m.sem("w_hi_done"), m.sem("w_lo_done"), m.sem("w_used")
        turned, sup_hi_done, sup_lo_done = m.sem("turned"), m.sem("sup_hi_done"), m.sem("sup_lo_done")
        sq_r_done, sq_i_done, power = m.sem("sq_r_done"), m.sem("sq_i_done"), m.sem("power")
        mi_row, post_row_done, z_row = m.sem("mi_row"), m.sem("post_row_done"), m.sem("z_row")
        f32_done, y_hi_done, y_lo_done = m.sem("f32_done"), m.sem("y_hi_done"), m.sem("y_lo_done")
        post_done, stat_done, var_done, std_done, rstd_done, z_done, zt_done = (m.sem(x) for x in (
            "post_done", "stat_done", "var_done", "std_done", "rstd_done", "z_done", "zt_done"))
        h2_done, top_done, y_done, y_stored = m.sem("h2_done"), m.sem("top_done"), m.sem("y_done"), m.sem("y_stored")
        block = ctx.enter_context(nc.Block())

        LO, TL, SL, ST = 2 * RAW, 4, 8, 16

        def landed(hf, pair):
            per_half = len(range(pair % RAW, NT // 2, RAW))
            return hf * (16 * per_half) + 16 * (pair // RAW + 1)

        @block.sync
        def _(sp):
            with sp.Fori(0, HALVES) as hf:
                sp.wait_ge(sup_lo_done, hf * 8 + SL)
                for w in range(2):
                    sp.dma_start(sup[:, :, D * w:D * w + D],
                                 sup_in[bass.ds(hf * 4, 4), :, D * w:D * w + D].rearrange("t p j -> p t j")).then_inc(sup_landed[w], 16)
                sp.wait_ge(top_added, hf * 4 + TL)
                for pair in range(NT // 2):
                    sp.wait_ge(w_lo_done, hf * NT + (max(0, 2 * pair + 2 - 2 * RAW) + LO))
                    sp.dma_start(w_raw[:, pair % RAW], w_tail[PAIRS[pair]]).then_inc(w_landed[pair % RAW], 16)
                    if pair == RAW:
                        sp.dma_start(top_x[:], top_in[bass.ds(hf, 1)].rearrange("a p f t -> p (a f) t")).then_inc(top_landed, 16)

        @block.gpsimd
        def _(pool):
            for to, of in ((post_row[:], b_post.partition_broadcast(P)), (gain[:], g_postT), (shift[:], be_postT),
                           (b1[:], b1T), (b2[:], b2T), (w3_col[:], w3)):
                pool.dma_start(to, of).then_inc(c_landed, 16)
            nc.gpsimd.memset(ident[:], 0.0).then_inc(ident_ready, 1)
            pool.wait_ge(ident_ready, 1)
            nc.gpsimd.affine_select(out=ident[:], in_=ident[:], compare_op=ALU.not_equal, fill=1.0, base=0,
                                    pattern=[[-1, P]], channel_multiplier=1).then_inc(ident_ready, 1)

        @block.scalar
        def _(act):
            def high(hf, i):
                if i % 2 == 0:
                    act.wait_ge(w_landed[i // 2 % RAW], landed(hf, i // 2))
                act.wait_ge(w_used, hf * NT + max(i + 1, RING))
                nc.scalar.activation(w_hi[:, i % RING, :], w_raw[:, i // 2 % RAW, i % 2, :], ACT.Copy,
                                     scale=float(TILES[i][2])).then_inc(w_hi_done, 1)

            def split_high(hf, layer, k):
                act.wait_ge(f32_done, hf * 12 + (4 * layer + k + 1))
                nc.scalar.activation(y_hi[layer][:, k, :], f32[:, k, :], ACT.Copy).then_inc(y_hi_done, 1)

            act.sem_inc(y_stored, ST)
            with act.Fori(0, HALVES) as hf:
                for k in range(8):
                    act.wait_ge(turned, hf * 8 + (k + 1))
                    nc.scalar.activation(sup_hi[:, k, :], banks[4 + k % 4][:], ACT.Copy).then_inc(sup_hi_done, 1)
                    if k < RING:
                        high(hf, k)
                for i in range(RING, FIRST["z"]):
                    high(hf, i)
                    if i == FIRST["mi"] + RING - 1:
                        act.wait_ge(w_used, hf * NT + (FIRST["mi"] + RING))
                        for f in range(4):
                            nc.scalar.activation(square_r[:, f, :], banks[f][:], ACT.Square).then_inc(sq_r_done, 1)
                for f in range(5):
                    if f < 4:
                        if f < 3:
                            act.wait_ge(mi_row, hf * 3 + (f + 1))
                        else:
                            act.wait_ge(w_used, hf * NT + (FIRST["post"] + RING))
                        nc.scalar.activation(square_i[:, f % 2, :], banks[4 + f][:], ACT.Square).then_inc(sq_i_done, 1)
                    if f:
                        act.wait_ge(power, hf * 4 + f)
                        nc.scalar.activation(f32[:, f - 1, :], f32[:, f - 1, :], ACT.Sqrt).then_inc(f32_done, 1)
                        split_high(hf, 0, f - 1)
                for i in range(FIRST["z"], NT):
                    high(hf, i)
                act.wait_ge(var_done, hf + 1)
                nc.scalar.activation(std[:], mean_var[:, :, 1], ACT.Sqrt).then_inc(std_done, 1)
                act.wait_ge(c_landed, 6 * 16)
                for k in range(4):
                    act.wait_ge(zt_done, hf * 4 + (k + 1))
                    nc.scalar.activation(f32[:, k, :], banks[k][:], ACT.Gelu, bias=shift[:, k:k + 1],
                                         scale=gain[:, k:k + 1]).then_inc(f32_done, 1)
                    split_high(hf, 1, k)
                for f in range(4):
                    act.wait_ge(top_added, hf * 4 + (f + 1 + TL))
                    nc.scalar.activation(f32[:, f, :], f32[:, f, :], ACT.Relu, bias=b1[:, f:f + 1]).then_inc(f32_done, 1)
                    split_high(hf, 2, f)
                act.wait_ge(w_used, hf * NT + (NT + RING))
                for f in range(2):
                    nc.scalar.activation(h2[:, f, :], banks[f][:], ACT.Relu, bias=b2[:, f:f + 1]).then_inc(h2_done, 1)
                act.wait_ge(top_done, hf + 1)
                act.wait_ge(y_stored, hf * 16 + ST)
                nc.scalar.activation(y[:], banks[2][0:1, :], ACT.Copy).then_inc(y_done, 1)
                act.wait_ge(y_done, hf + 1)
                act.dma_start(y_out[bass.ds(hf * HALF, HALF), :].rearrange("t a -> a t"), y[:]).then_inc(y_stored, 16)
            act.wait_ge(y_stored, HALVES * 16 + ST)

        @block.vector
        def _(dve):
            def low(hf, i):
                raw, hi, lo = w_raw[:, i // 2 % RAW, i % 2, :], w_hi[:, i % RING, :].bitcast(F32), w_lo[:, i % RING, :]
                dve.wait_ge(w_hi_done, hf * NT + (i + 1))
                if TILES[i][2] < 0:
                    nc.vector.scalar_tensor_tensor(out=lo, in0=raw, scalar=-1.0, in1=hi, op0=ALU.mult,
                                                   op1=ALU.subtract).then_inc(w_lo_done, 1)
                else:
                    nc.vector.tensor_tensor(lo, raw, hi, ALU.subtract).then_inc(w_lo_done, 1)

            def split_low(hf, layer, k):
                dve.wait_ge(y_hi_done, hf * 12 + (4 * layer + k + 1))
                nc.vector.tensor_tensor(y_lo[layer][:, k, :], f32[:, k, :], y_hi[layer][:, k, :].bitcast(F32),
                                        ALU.subtract).then_inc(y_lo_done, 1)

            dve.sem_inc(w_lo_done, LO)
            dve.sem_inc(top_added, TL)
            dve.sem_inc(sup_lo_done, SL)
            with dve.Fori(0, HALVES) as hf:
                for k in range(8):
                    dve.wait_ge(sup_hi_done, hf * 8 + (k + 1))
                    nc.vector.tensor_tensor(sup_lo[:, k, :], banks[4 + k % 4][:], sup_hi[:, k, :].bitcast(F32),
                                            ALU.subtract).then_inc(sup_lo_done, 1)
                    if k < RING:
                        low(hf, k)
                for i in range(RING, FIRST["z"]):
                    low(hf, i)
                dve.wait_ge(sq_r_done, hf * 4 + 4)
                for f in range(4):
                    dve.wait_ge(sq_i_done, hf * 4 + (f + 1))
                    nc.vector.tensor_tensor(f32[:, f, :], square_r[:, f, :], square_i[:, f % 2, :], ALU.add).then_inc(power, 1)
                    if f:
                        split_low(hf, 0, f - 1)
                split_low(hf, 0, 3)
                for i in range(FIRST["z"], NT - 2):
                    low(hf, i)
                dve.wait_ge(c_landed, 6 * 16)
                for t in range(4):
                    if t < 3:
                        dve.wait_ge(post_row_done, hf * 3 + (t + 1))
                    else:
                        dve.wait_ge(w_used, hf * NT + (FIRST["post"] + 4 + RING))
                    nc.vector.tensor_tensor(post[:, t, :], banks[t][:], post_row[:], ALU.add).then_inc(post_done, 1)
                    dve.wait_ge(post_done, hf * 4 + (t + 1))
                    nc.vector.bn_stats(stats[:, t, :], post[:, t, :]).then_inc(stat_done, 1)
                dve.wait_ge(stat_done, hf * 8 + 4)
                dve.nop(nofuse=True)
                for t in range(4):
                    nc.vector.bn_aggr(mean_var[:, t, :], stats[:, t, :]).then_inc(stat_done, 1)
                dve.wait_ge(stat_done, hf * 8 + 8)
                nc.vector.tensor_scalar(mean_var[:, :, 1], mean_var[:, :, 1], EPS, None, ALU.add).then_inc(var_done, 1)
                dve.wait_ge(std_done, hf + 1)
                nc.vector.reciprocal(rstd[:], std[:]).then_inc(rstd_done, 1)
                dve.wait_ge(rstd_done, hf + 1)
                for cols in (slice(0, P), slice(P, D)):
                    for t in range(4):
                        nc.vector.tensor_scalar(post[:, t, cols], post[:, t, cols], mean_var[:, t, 0:1], rstd[:, t:t + 1],
                                                ALU.subtract, ALU.mult).then_inc(z_done, 1)
                for i in range(NT - 2, NT):
                    low(hf, i)
                for k in range(4):
                    split_low(hf, 1, k)
                dve.wait_ge(top_landed, hf * 16 + 16)
                for f in range(4):
                    if f < 3:
                        dve.wait_ge(z_row, hf * 3 + (f + 1))
                    else:
                        dve.wait_ge(w_used, hf * NT + (FIRST["top2"] + RING))
                    nc.vector.tensor_tensor(f32[:, f, :], banks[4 + f][:], top_x[:, f, :], ALU.add).then_inc(top_added, 1)
                    if f:
                        split_low(hf, 2, f - 1)
                split_low(hf, 2, 3)

        @block.tensor
        def _(pe):
            pe.sem_inc(w_used, RING)
            pe.wait_ge(ident_ready, 2)
            with pe.Fori(0, HALVES) as hf:
                def w(i, cols=slice(0, 512)):
                    return (w_hi[:, i % RING, cols], w_lo[:, i % RING, cols])

                for k in range(8):
                    pe.wait_ge(sup_landed[k // 4], hf * 16 + 16)
                    if k < 4:
                        pe.wait_ge(top_added, hf * 4 + TL)
                    else:
                        pe.wait_ge(sup_lo_done, hf * 8 + (k - 3 + SL))
                    for t in range(4):
                        mm = nc.tensor.transpose(banks[4 + k % 4][:, P * t:P * t + P], sup[:, t, P * k:P * k + P], ident[:])
                    mm.then_inc(turned, 1)
                for i, (layer, k, _) in enumerate(TILES):
                    if i == FIRST["z"]:
                        for j in range(4):
                            pe.wait_ge(z_done, hf * 8 + (8 if j else 4))
                            for t in range(4):
                                mm = nc.tensor.transpose(banks[j][:, P * t:P * t + P], post[:, t, P * j:P * j + P], ident[:])
                            mm.then_inc(zt_done, 1)
                    pe.wait_ge(w_lo_done, hf * NT + (i + 1 + LO))
                    if i == FIRST["mi"]:
                        pe.wait_ge(sup_lo_done, hf * 8 + (8 + SL))
                    if layer == "mr":
                        pe.wait_ge(sup_lo_done, hf * 8 + (k + 1 + SL))
                    if layer == "post":
                        if k == 0:
                            pe.wait_ge(sq_r_done, hf * 4 + 4)
                        pe.wait_ge(y_lo_done, hf * 12 + (k + 1))
                    if layer == "z":
                        pe.wait_ge(y_lo_done, hf * 12 + (4 + k + 1))
                    if layer == "top2":
                        pe.wait_ge(y_lo_done, hf * 12 + (8 + 2 * k + 2))
                        for kk in range(2):
                            for f in range(2):
                                c = 256 * kk + P * f
                                kt = 2 * k + kk
                                mm = product(nc, banks[f][:], w(i, slice(c, c + P)), (y_hi[2][:, kt, :], y_lo[2][:, kt, :]),
                                             kt == 0, kt == 3)
                        mm.then_inc(w_used, 1)
                        continue
                    last_two = {"mi": 3, "post": 3, "z": 3}.get(layer) == k
                    if {"mi": 2, "post": 2, "z": 2}.get(layer) == k:
                        continue
                    if layer == "z" and k == 0:
                        pe.wait_ge(sq_i_done, hf * 4 + 4)
                    for f in range(4):
                        for j in ((i - 1, i) if last_two else (i,)):
                            kk, s = TILES[j][1], slice(P * f, P * f + P)
                            if layer == "mr":
                                mm = product(nc, banks[f][:], w(j, s), (sup_hi[:, kk, :], sup_lo[:, kk, :]), kk == 0, kk == 7)
                            elif layer == "mi":
                                mm = product(nc, banks[4 + f][:], w(j, s), (sup_hi[:, kk, :], sup_lo[:, kk, :]), kk == 4, kk == 3)
                            elif layer == "post":
                                mm = product(nc, banks[f][:], (y_hi[0][:, kk, s], y_lo[0][:, kk, s]), w(j), kk == 0, kk == 3)
                            else:
                                mm = product(nc, banks[4 + f][:], w(j, s), (y_hi[1][:, kk, :], y_lo[1][:, kk, :]), kk == 0, kk == 3)
                            if last_two and j < i and f == 3:
                                mm.then_inc(w_used, 1)
                        if last_two and f < 3:
                            mm.then_inc({"mi": mi_row, "post": post_row_done, "z": z_row}[layer], 1)
                    mm.then_inc(w_used, 1)
                pe.wait_ge(c_landed, 6 * 16)
                for f in range(2):
                    pe.wait_ge(h2_done, hf * 2 + (f + 1))
                    mm = nc.tensor.matmul(banks[2][0:1, :], w3_col[:, f:f + 1], h2[:, f, :], start=(f == 0), stop=(f == 1))
                mm.then_inc(top_done, 1)


def kernel(**inputs):
    import concourse.bacc as bacc
    from concourse.bass_utils import run_bass_kernel_spmd

    p = {k.removeprefix("L0_rec_"): np.asarray(v) for k, v in inputs.items()}

    def tiles(w):
        return w.reshape(w.shape[0], -1, P).transpose(2, 1, 0)

    def pairs(w):
        return w.reshape(-1, 2, P, w.shape[1]).transpose(0, 2, 1, 3)

    def columns(*vectors):
        return np.stack(vectors).reshape(len(vectors), -1, P).transpose(2, 0, 1)

    enc = ("er", "ei")
    top1 = p["W_top1"]
    host = {
        "xT": p["r_x"].reshape(HALVES, HALF, KT, P).transpose(0, 2, 3, 1).reshape(HALVES * KT, P, HALF),
        "w_enc": np.stack([p[f"{e}_{w}"].reshape(4, 512, KT // 2, 2, P).transpose(0, 2, 4, 3, 1)
                           for e in enc for w in ("W1", "W2")]).reshape(-1, P, 2, 512),
        "b1": np.stack([p[f"{e}_b1"] for e in enc]).reshape(-1, 512),
        "g1T": columns(*[p[f"{e}_g1"] for e in enc]).transpose(1, 0, 2),
        "be1T": columns(*[p[f"{e}_be1"] for e in enc]).transpose(1, 0, 2),
        "b2T": columns(*[p[f"{e}_b2"] for e in enc]).transpose(1, 0, 2),
        "w_qkv": np.stack([tiles(p[n]) for n in ("Wq_r", "Wq_i", "Wk_r", "Wk_i", "Wv_r", "Wv_i")]),
        "b_qkT": columns(p["bq_r"], p["bq_i"], p["bk_r"], p["bk_i"]),
        "b_v": np.stack([p["bv_r"], p["bv_i"]]),
        "w_o": np.stack([tiles(p["Wo_r"]), tiles(p["Wo_i"])]),
        "b_oT": columns(p["bo_r"], p["bo_i"]),
        "w_int": np.stack([tiles(p[w][n]).reshape(P, DT * 512) for n in range(N) for w in ("int_Wr", "int_Wi")]),
        "ids": p["ids"].reshape(CH, P, N).transpose(1, 0, 2),
        "w_tail": np.concatenate([pairs(p["meas_Mr"].T), pairs(p["meas_Mi"].T), pairs(p["post_W"].T),
                                  pairs(top1[:D]),
                                  p["W_top2"].reshape(1, 2, 2, P, 256).transpose(0, 3, 1, 2, 4).reshape(1, P, 2, 512)]),
        "w_top": top1[D:].reshape(KT, P, 512),
        "b_post": p["post_b"],
        "g_postT": columns(p["post_g"])[:, 0],
        "be_postT": columns(p["post_be"])[:, 0],
        "b_top1T": columns(p["b_top1"])[:, 0],
        "b_top2T": columns(p["b_top2"])[:, 0],
        "w3": p["W_top3"].reshape(2, P).T,
    }
    for f in range(N):
        host[f"tbl_{f}"] = p[f"tbl_{f}"]
    nc = bacc.Bacc("TRN2", target_bir_lowering=False, num_devices=1)
    arrays, d = {}, {}
    for name, a in host.items():
        arrays[f"in_{name}"] = np.ascontiguousarray(a)
        d[name] = nc.dram_tensor(f"in_{name}", a.shape, mybir.dt.from_np(a.dtype), kind="ExternalInput").ap()

    def scratch(name, shape):
        return nc.dram_tensor(name, shape, F32, kind="Internal").ap()

    s = scratch("s", (CH, 2, P, DT, N, P))
    qkv = scratch("qkv", (CH, 7, P, DT, 512))
    attn = scratch("attn", (CH, 2, P, DT, 512))
    sup = scratch("sup", (CH, P, 2 * D))
    top = scratch("top", (HALVES, P, DT, HALF))
    y = nc.dram_tensor("out_y", (TOK, 1), F32, kind="ExternalOutput").ap()
    encoders(nc, d["xT"], d["w_enc"], d["b1"], d["g1T"], d["be1T"], d["b2T"], s)
    projections(nc, s, d["w_qkv"], d["b_qkT"], d["b_v"], qkv)
    attention(nc, qkv, d["w_o"], d["b_oT"], attn)
    superposition(nc, attn, d["w_int"], d["ids"], [d[f"tbl_{f}"] for f in range(N)], sup,
                  d["xT"], d["w_top"], top)
    tower(nc, sup, top, d["w_tail"], d["b_post"], d["g_postT"], d["be_postT"], d["b_top1T"], d["b_top2T"], d["w3"], y)
    return run_bass_kernel_spmd(nc, [arrays], core_ids=[0]).results[0]["out_y"]
```
